# Optimizing a Trainium2 kernel written in Bass

```python
import numpy as np
import jax
import jax.numpy as jnp

def _softmax(x, axis=-1):
    return jax.nn.softmax(x, axis=axis)

def _gelu(x):
    return jax.nn.gelu(x, approximate=True)

def _silu(x):
    return jax.nn.silu(x)

def _sigmoid(x):
    return jax.nn.sigmoid(x)

def _layernorm(x, axis=-1, eps=1e-05):
    m = jnp.mean(x, axis=axis, keepdims=True)
    v = jnp.var(x, axis=axis, keepdims=True)
    return (x - m) / jnp.sqrt(v + eps)

def _scatter_add(tgt, idx, src, axis=0):
    return tgt.at[idx].add(src)

def _segment_sum(src, seg, n):
    return jax.ops.segment_sum(src, seg, n)
kernel_name = 'mk_adaln_attn_ffn_d2_seqx_r4_5018b5'

def setup_inputs(seed: int=0):
    np.random.seed(seed)
    _w = jnp.asarray

    def _rec_inputs():
        import jax
        import jax.numpy as jnp
        _rk = jax.random.key(seed)
        x = -0.0003929 + 0.9999 * jax.random.normal(jax.random.fold_in(_rk, 1), (8, 256, 256), jnp.float32)
        _lenS = 256 - jax.random.randint(jax.random.fold_in(_rk, 7), (8,), 0, max(1, 256 // 4) + 1, jnp.int32)
        _lenS2 = 256 - jax.random.randint(jax.random.fold_in(_rk, 8), (8,), 0, max(1, 256 // 4) + 1, jnp.int32)
        cond_1024 = 0.00513981 + 1.0024 * jax.random.normal(jax.random.fold_in(_rk, 11), (8, 256), jnp.float32)
        return (x, cond_1024)
    x, cond_1024 = _rec_inputs()

    def _L0_cond_setup():
        import jax, jax.numpy as jnp
        import numpy as np
        D = 256
        H = 256
        key = jax.random.key(seed)
        k1, k2, k3, k4 = jax.random.split(key, 4)
        x = jax.random.normal(k1, (32, 128, D), dtype=jnp.float32)
        h0 = jax.random.normal(k2, (32, H), dtype=jnp.float32)
        Wx = jax.random.normal(k3, (D, 4 * H), dtype=jnp.float32) / jnp.sqrt(float(D))
        Wh = jax.random.normal(k4, (H, 4 * H), dtype=jnp.float32) / jnp.sqrt(float(H))
        b = jnp.zeros((4 * H,), dtype=jnp.float32)
        return {'x': x, 'h0': h0, 'Wx': Wx, 'Wh': Wh, 'b': b}
    _L0_cond_all = _L0_cond_setup()
    _L0_cond_in = {k: v for k, v in _L0_cond_all.items() if k in ('Wx', 'Wh', 'b')}
    del _L0_cond_all

    def _L0_attn_setup():
        import jax, jax.numpy as jnp
        import numpy as np
        NUM_HEADS = 16
        EPS = 1e-06
        key = jax.random.key(seed)
        ks = jax.random.split(key, 5)
        L, N, E = (512, 8, 256)
        scale = 1.0 / np.sqrt(E)
        return {'query': jax.random.normal(ks[0], (L, N, E), jnp.float32), 'Wq': jax.random.normal(ks[1], (E, E), jnp.float32) * scale, 'Wk': jax.random.normal(ks[2], (E, E), jnp.float32) * scale, 'Wv': jax.random.normal(ks[3], (E, E), jnp.float32) * scale, 'Wo': jax.random.normal(ks[4], (E, E), jnp.float32) * scale}
    _L0_attn_all = _L0_attn_setup()
    _L0_attn_in = {k: v for k, v in _L0_attn_all.items() if k in ('Wq', 'Wk', 'Wv', 'Wo')}
    del _L0_attn_all

    def _L0_cond2_setup():
        import jax, jax.numpy as jnp
        import numpy as np
        import math
        N, T, D, H = (128, 128, 256, 256)
        key = jax.random.key(seed)
        k1, k2, k3, k4 = jax.random.split(key, 4)
        x = jax.random.normal(k1, (N, T, D), dtype=jnp.float32)
        h0 = jax.random.normal(k2, (N, H), dtype=jnp.float32)
        Wx = jax.random.normal(k3, (D, H), dtype=jnp.float32) / math.sqrt(D)
        Wh = jax.random.normal(k4, (H, H), dtype=jnp.float32) / math.sqrt(H)
        b = jnp.zeros((H,), dtype=jnp.float32)
        return {'x': x, 'h0': h0, 'Wx': Wx, 'Wh': Wh, 'b': b}
    _L0_cond2_all = _L0_cond2_setup()
    _L0_cond2_in = {k: v for k, v in _L0_cond2_all.items() if k in ('Wx', 'Wh', 'b')}
    del _L0_cond2_all

    def _L0_ffn_setup():
        import jax, jax.numpy as jnp
        import numpy as np
        BS, L, D = (4, 512, 256)
        H, E, K = (8, 16, 2)
        HD = D // H
        I = 1024 // H
        key = jax.random.key(seed)
        ks = jax.random.split(key, 10)
        s = lambda k, shp, fan: jax.random.normal(k, shp, jnp.float32) / np.sqrt(fan)
        return {'x': jax.random.normal(ks[0], (BS, L, D), jnp.float32), 'Wm': s(ks[1], (D, D), D), 'bm': jnp.zeros((D,), jnp.float32), 'expert_emb': jax.random.normal(ks[2], (HD, E), jnp.float32), 'W1': s(ks[3], (E, HD, I), HD), 'b1': jnp.zeros((E, I), jnp.float32), 'W2': s(ks[4], (E, I, HD), I), 'b2': jnp.zeros((E, HD), jnp.float32), 'Wo': s(ks[5], (D, D), D), 'bo': jnp.zeros((D,), jnp.float32)}
    _L0_ffn_all = _L0_ffn_setup()
    _L0_ffn_in = {k: v for k, v in _L0_ffn_all.items() if k in ('Wm', 'bm', 'expert_emb', 'W1', 'b1', 'W2', 'b2', 'Wo', 'bo')}
    del _L0_ffn_all

    def _L1_cond_setup():
        import jax, jax.numpy as jnp
        import numpy as np
        import math
        N, T, D, H = (64, 128, 256, 256)
        key = jax.random.key(seed)
        k1, k2, k3, k4 = jax.random.split(key, 4)
        x = jax.random.normal(k1, (N, T, D), dtype=jnp.float32)
        h0 = jax.random.normal(k2, (N, H), dtype=jnp.float32)
        Wx = jax.random.normal(k3, (D, 4 * H), dtype=jnp.float32) / math.sqrt(D)
        Wh = jax.random.normal(k4, (H, 4 * H), dtype=jnp.float32) / math.sqrt(H)
        b = jnp.zeros((4 * H,), dtype=jnp.float32)
        return {'x': x, 'h0': h0, 'Wx': Wx, 'Wh': Wh, 'b': b}
    _L1_cond_all = _L1_cond_setup()
    _L1_cond_in = {k: v for k, v in _L1_cond_all.items() if k in ('Wx', 'Wh', 'b')}
    del _L1_cond_all

    def _L1_attn_setup():
        import jax, jax.numpy as jnp
        import numpy as np
        H = 8
        LN_EPS = 1e-05
        key = jax.random.key(seed)
        ks = jax.random.split(key, 4)
        B, S, D = (4, 512, 256)
        x = jax.random.normal(ks[0], (B, S, D), dtype=jnp.float32)
        sc = 1.0 / np.sqrt(D)
        Wq = jax.random.normal(ks[1], (D, D), dtype=jnp.float32) * sc
        Wk = jax.random.normal(ks[2], (D, D), dtype=jnp.float32) * sc
        Wv = jax.random.normal(ks[3], (D, D * H), dtype=jnp.float32) * sc
        return {'x': x, 'Wq': Wq, 'bq': jnp.zeros((D,), jnp.float32), 'Wk': Wk, 'bk': jnp.zeros((D,), jnp.float32), 'Wv': Wv, 'bv': jnp.zeros((D * H,), jnp.float32), 'gamma': jnp.ones((D,), jnp.float32), 'beta': jnp.zeros((D,), jnp.float32)}
    _L1_attn_all = _L1_attn_setup()
    _L1_attn_in = {k: v for k, v in _L1_attn_all.items() if k in ('Wq', 'bq', 'Wk', 'bk', 'Wv', 'bv', 'gamma', 'beta')}
    del _L1_attn_all

    def _L1_cond2_setup():
        import jax, jax.numpy as jnp
        import numpy as np
        B, T, D_IN, V_IN, E = (64, 128, 256, 256, 256)
        key = jax.random.key(seed)
        ks = jax.random.split(key, 16)
        s = 0.01
        return {'video': jax.random.normal(ks[0], (B, V_IN), jnp.float32), 'seq': jax.random.normal(ks[1], (B, T, D_IN), jnp.float32), 'W_z': jax.random.normal(ks[2], (D_IN, E), jnp.float32) * s, 'U_z': jax.random.normal(ks[3], (E, E), jnp.float32) * s, 'C_z': jax.random.normal(ks[4], (V_IN, E), jnp.float32) * s, 'b_z': jnp.zeros((E,), jnp.float32), 'W_r': jax.random.normal(ks[5], (D_IN, E), jnp.float32) * s, 'U_r': jax.random.normal(ks[6], (E, E), jnp.float32) * s, 'C_r': jax.random.normal(ks[7], (V_IN, E), jnp.float32) * s, 'b_r': jnp.zeros((E,), jnp.float32), 'W': jax.random.normal(ks[8], (D_IN, E), jnp.float32) * s, 'U': jax.random.normal(ks[9], (E, E), jnp.float32) * s, 'C': jax.random.normal(ks[10], (V_IN, E), jnp.float32) * s, 'b': jnp.zeros((E,), jnp.float32)}
    _L1_cond2_all = _L1_cond2_setup()
    _L1_cond2_in = {k: v for k, v in _L1_cond2_all.items() if k in ('W_z', 'U_z', 'C_z', 'b_z', 'W_r', 'U_r', 'C_r', 'b_r', 'W', 'U', 'C', 'b')}
    del _L1_cond2_all

    def _L1_ffn_setup():
        import jax, jax.numpy as jnp
        import numpy as np
        E, K = (8, 4)
        B, S, D = (4, 256, 256)
        H = D * 2 * 4 // 3

        def _swiglu(u, w1, w2, w3):
            h = jnp.einsum('...d,hd->...h', u, w1)
            v = jnp.einsum('...d,hd->...h', u, w2)
            return jnp.einsum('...h,dh->...d', jax.nn.sigmoid(h) * h * v, w3)
        key = jax.random.key(seed)
        ks = jax.random.split(key, 9)
        std = 0.02
        return {'x': jax.random.normal(ks[0], (B, S, D), jnp.float32), 'Wg': jax.random.normal(ks[1], (E, D), jnp.float32) * std, 'routing_bias': jnp.zeros((E,), jnp.float32), 'W1': jax.random.normal(ks[2], (E, H, D), jnp.float32) * std, 'W2': jax.random.normal(ks[3], (E, H, D), jnp.float32) * std, 'W3': jax.random.normal(ks[4], (E, D, H), jnp.float32) * std, 'Ws1': jax.random.normal(ks[5], (H, D), jnp.float32) * std, 'Ws2': jax.random.normal(ks[6], (H, D), jnp.float32) * std, 'Ws3': jax.random.normal(ks[7], (D, H), jnp.float32) * std}
    _L1_ffn_all = _L1_ffn_setup()
    _L1_ffn_in = {k: v for k, v in _L1_ffn_all.items() if k in ('Wg', 'routing_bias', 'W1', 'W2', 'W3', 'Ws1', 'Ws2', 'Ws3')}
    del _L1_ffn_all
    return {'x': x, 'cond_1024': cond_1024, 'L0_cond_Wx': _L0_cond_in['Wx'], 'L0_cond_Wh': _L0_cond_in['Wh'], 'L0_cond_b': _L0_cond_in['b'], 'L0_attn_Wq': _L0_attn_in['Wq'], 'L0_attn_Wk': _L0_attn_in['Wk'], 'L0_attn_Wv': _L0_attn_in['Wv'], 'L0_attn_Wo': _L0_attn_in['Wo'], 'L0_cond2_Wx': _L0_cond2_in['Wx'], 'L0_cond2_Wh': _L0_cond2_in['Wh'], 'L0_cond2_b': _L0_cond2_in['b'], 'L0_ffn_Wm': _L0_ffn_in['Wm'], 'L0_ffn_bm': _L0_ffn_in['bm'], 'L0_ffn_expert_emb': _L0_ffn_in['expert_emb'], 'L0_ffn_W1': _L0_ffn_in['W1'], 'L0_ffn_b1': _L0_ffn_in['b1'], 'L0_ffn_W2': _L0_ffn_in['W2'], 'L0_ffn_b2': _L0_ffn_in['b2'], 'L0_ffn_Wo': _L0_ffn_in['Wo'], 'L0_ffn_bo': _L0_ffn_in['bo'], 'L1_cond_Wx': _L1_cond_in['Wx'], 'L1_cond_Wh': _L1_cond_in['Wh'], 'L1_cond_b': _L1_cond_in['b'], 'L1_attn_Wq': _L1_attn_in['Wq'], 'L1_attn_bq': _L1_attn_in['bq'], 'L1_attn_Wk': _L1_attn_in['Wk'], 'L1_attn_bk': _L1_attn_in['bk'], 'L1_attn_Wv': _L1_attn_in['Wv'], 'L1_attn_bv': _L1_attn_in['bv'], 'L1_attn_gamma': _L1_attn_in['gamma'], 'L1_attn_beta': _L1_attn_in['beta'], 'L1_cond2_W_z': _L1_cond2_in['W_z'], 'L1_cond2_U_z': _L1_cond2_in['U_z'], 'L1_cond2_C_z': _L1_cond2_in['C_z'], 'L1_cond2_b_z': _L1_cond2_in['b_z'], 'L1_cond2_W_r': _L1_cond2_in['W_r'], 'L1_cond2_U_r': _L1_cond2_in['U_r'], 'L1_cond2_C_r': _L1_cond2_in['C_r'], 'L1_cond2_b_r': _L1_cond2_in['b_r'], 'L1_cond2_W': _L1_cond2_in['W'], 'L1_cond2_U': _L1_cond2_in['U'], 'L1_cond2_C': _L1_cond2_in['C'], 'L1_cond2_b': _L1_cond2_in['b'], 'L1_ffn_Wg': _L1_ffn_in['Wg'], 'L1_ffn_routing_bias': _L1_ffn_in['routing_bias'], 'L1_ffn_W1': _L1_ffn_in['W1'], 'L1_ffn_W2': _L1_ffn_in['W2'], 'L1_ffn_W3': _L1_ffn_in['W3'], 'L1_ffn_Ws1': _L1_ffn_in['Ws1'], 'L1_ffn_Ws2': _L1_ffn_in['Ws2'], 'L1_ffn_Ws3': _L1_ffn_in['Ws3']}

def reference(x, cond_1024, L0_cond_Wx, L0_cond_Wh, L0_cond_b, L0_attn_Wq, L0_attn_Wk, L0_attn_Wv, L0_attn_Wo, L0_cond2_Wx, L0_cond2_Wh, L0_cond2_b, L0_ffn_Wm, L0_ffn_bm, L0_ffn_expert_emb, L0_ffn_W1, L0_ffn_b1, L0_ffn_W2, L0_ffn_b2, L0_ffn_Wo, L0_ffn_bo, L1_cond_Wx, L1_cond_Wh, L1_cond_b, L1_attn_Wq, L1_attn_bq, L1_attn_Wk, L1_attn_bk, L1_attn_Wv, L1_attn_bv, L1_attn_gamma, L1_attn_beta, L1_cond2_W_z, L1_cond2_U_z, L1_cond2_C_z, L1_cond2_b_z, L1_cond2_W_r, L1_cond2_U_r, L1_cond2_C_r, L1_cond2_b_r, L1_cond2_W, L1_cond2_U, L1_cond2_C, L1_cond2_b, L1_ffn_Wg, L1_ffn_routing_bias, L1_ffn_W1, L1_ffn_W2, L1_ffn_W3, L1_ffn_Ws1, L1_ffn_Ws2, L1_ffn_Ws3):
    import jax
    import jax.numpy as jnp

    def _L0_cond_ref(x, h0, Wx, Wh, b):
        import jax, jax.numpy as jnp
        import numpy as np
        D = 256
        H = 256
        Hdim = h0.shape[1]
        x_proj = jnp.einsum('ntd,df->ntf', x, Wx) + b

        def step(carry, xp_t):
            prev_h, prev_c = carry
            h_bar = xp_t + prev_h @ Wh
            i = jax.nn.sigmoid(h_bar[:, 0:Hdim])
            f = jax.nn.sigmoid(h_bar[:, Hdim:2 * Hdim])
            o = jax.nn.sigmoid(h_bar[:, 2 * Hdim:3 * Hdim])
            g = jnp.tanh(h_bar[:, 3 * Hdim:4 * Hdim])
            next_c = f * prev_c + i * g
            next_h = o * jnp.tanh(next_c)
            return ((next_h, next_c), next_h)
        c0 = jnp.zeros_like(h0)
        xs = jnp.swapaxes(x_proj, 0, 1)
        _, hs = jax.lax.scan(step, (h0, c0), xs)
        return jnp.swapaxes(hs, 0, 1)

    def _L0_attn_ref(query, Wq, Wk, Wv, Wo):
        import jax, jax.numpy as jnp
        import numpy as np
        NUM_HEADS = 16
        EPS = 1e-06
        L, N, E = query.shape
        h = NUM_HEADS
        d = E // h
        q = jax.nn.relu(query @ Wq.T)
        k = jax.nn.relu(query @ Wk.T)
        v = query @ Wv.T

        def split_heads(x):
            return x.reshape(L, N * h, d).transpose(1, 0, 2)
        q, k, v = (split_heads(q), split_heads(k), split_heads(v))
        idx = jnp.pi / 2 * jnp.arange(1, L + 1, dtype=jnp.float32) / L
        sin = jnp.sin(idx)[None, :, None]
        cos = jnp.cos(idx)[None, :, None]
        q_ = jnp.concatenate([q * sin, q * cos], axis=-1)
        k_ = jnp.concatenate([k * sin, k * cos], axis=-1)
        kv = jnp.einsum('nld,nlm->ndm', k_, v)
        z = 1.0 / jnp.maximum(jnp.einsum('nld,nd->nl', q_, k_.sum(axis=1)), EPS)
        attn = jnp.einsum('nld,ndm->nlm', q_, kv) * z[..., None]
        attn = attn.transpose(1, 0, 2).reshape(L, N, E)
        return attn @ Wo.T

    def _L0_cond2_ref(x, h0, Wx, Wh, b):
        import jax, jax.numpy as jnp
        import numpy as np
        import math
        N, T, D, H = (128, 128, 256, 256)
        xW = jnp.einsum('ntd,dh->nth', x, Wx) + b

        def step(h_prev, xw_t):
            h_next = jnp.tanh(h_prev @ Wh + xw_t)
            return (h_next, h_next)
        _, hs = jax.lax.scan(step, h0, jnp.swapaxes(xW, 0, 1))
        return jnp.swapaxes(hs, 0, 1)

    def _L0_ffn_ref(x, Wm, bm, expert_emb, W1, b1, W2, b2, Wo, bo):
        import jax, jax.numpy as jnp
        import numpy as np
        BS, L, D = (4, 512, 256)
        H, E, K = (8, 16, 2)
        HD = D // H
        I = 1024 // H
        bs, L_, d = x.shape
        h = x @ Wm + bm
        t = h.reshape(bs * L_ * H, HD)
        logits = t @ expert_emb
        w = jax.nn.softmax(logits, axis=-1)
        topw, topi = jax.lax.top_k(w, K)
        hmid = jax.nn.gelu(jnp.einsum('td,edi->tei', t, W1) + b1, approximate=False)
        eo = jnp.einsum('tei,eio->teo', hmid, W2) + b2
        sel = jnp.take_along_axis(eo, topi[:, :, None], axis=1)
        comb = (sel * topw[:, :, None]).sum(axis=1)
        out = comb.reshape(bs, L_, d)
        return out @ Wo + bo

    def _L1_cond_ref(x, h0, Wx, Wh, b):
        import jax, jax.numpy as jnp
        import numpy as np
        import math
        N, T, D, H = (64, 128, 256, 256)
        Hdim = h0.shape[1]
        xW = jnp.einsum('ntd,dg->ntg', x, Wx) + b

        def step(carry, xw_t):
            prev_h, prev_c = carry
            a = xw_t + prev_h @ Wh
            i = jax.nn.sigmoid(a[:, :Hdim])
            f = jax.nn.sigmoid(a[:, Hdim:2 * Hdim])
            o = jax.nn.sigmoid(a[:, 2 * Hdim:3 * Hdim])
            g = jnp.tanh(a[:, 3 * Hdim:])
            next_c = f * prev_c + i * g
            next_h = o * jnp.tanh(next_c)
            return ((next_h, next_c), next_h)
        c0 = jnp.zeros_like(h0)
        _, hs = jax.lax.scan(step, (h0, c0), jnp.swapaxes(xW, 0, 1))
        return jnp.swapaxes(hs, 0, 1)

    def _L1_attn_ref(x, Wq, bq, Wk, bk, Wv, bv, gamma, beta):
        import jax, jax.numpy as jnp
        import numpy as np
        H = 8
        LN_EPS = 1e-05
        B, S, D = x.shape
        dk = D // H
        mu = jnp.mean(x, axis=-1, keepdims=True)
        var = jnp.mean(jnp.square(x - mu), axis=-1, keepdims=True)
        xn = (x - mu) * jax.lax.rsqrt(var + LN_EPS) * gamma + beta
        q = (xn @ Wq + bq).reshape(B, S, H, dk).transpose(0, 2, 1, 3)
        k = (xn @ Wk + bk).reshape(B, S, H, dk).transpose(0, 2, 1, 3)
        v = (xn @ Wv + bv).reshape(B, S, H, D).transpose(0, 2, 1, 3)
        scores = jnp.einsum('bhsd,bhtd->bhst', q, k) / jnp.sqrt(jnp.asarray(dk, x.dtype))
        p = jax.nn.softmax(scores, axis=-1)
        att = jnp.einsum('bhst,bhtd->bhsd', p, v)
        out = att.reshape(S, B, D, H).sum(axis=-1).reshape(B, S, D)
        return out

    def _L1_cond2_ref(video, seq, W_z, U_z, C_z, b_z, W_r, U_r, C_r, b_r, W, U, C, b):
        import jax, jax.numpy as jnp
        import numpy as np
        B, T, D_IN, V_IN, E = (64, 128, 256, 256, 256)
        vz = video @ C_z + b_z
        vr = video @ C_r + b_r
        vh = video @ C + b
        xz = jnp.einsum('btd,de->bte', seq, W_z)
        xr = jnp.einsum('btd,de->bte', seq, W_r)
        xh = jnp.einsum('btd,de->bte', seq, W)

        def step(h, xs):
            xzt, xrt, xht = xs
            z = jax.nn.sigmoid(xzt + h @ U_z + vz)
            r = jax.nn.sigmoid(xrt + h @ U_r + vr)
            hh = jnp.tanh(xht + r * h @ U + vh)
            h_new = (1.0 - z) * h + z * hh
            return (h_new, h_new)
        h0 = jnp.zeros((seq.shape[0], U.shape[0]), seq.dtype)
        xs = (jnp.swapaxes(xz, 0, 1), jnp.swapaxes(xr, 0, 1), jnp.swapaxes(xh, 0, 1))
        _, out_t = jax.lax.scan(step, h0, xs)
        return jnp.swapaxes(out_t, 0, 1)

    def _L1_ffn_ref(x, Wg, routing_bias, W1, W2, W3, Ws1, Ws2, Ws3):
        import jax, jax.numpy as jnp
        import numpy as np
        E, K = (8, 4)
        B, S, D = (4, 256, 256)
        H = D * 2 * 4 // 3

        def _swiglu(u, w1, w2, w3):
            h = jnp.einsum('...d,hd->...h', u, w1)
            v = jnp.einsum('...d,hd->...h', u, w2)
            return jnp.einsum('...h,dh->...d', jax.nn.sigmoid(h) * h * v, w3)
        gate = jnp.einsum('bsd,ed->bse', x, Wg) + routing_bias
        _, top_idx = jax.lax.top_k(gate, K)
        mask = jax.nn.one_hot(top_idx, E, dtype=gate.dtype).sum(-2)
        masked_gate = jnp.where(mask > 0, gate, -jnp.inf)
        probs = jax.nn.softmax(masked_gate, axis=-1)
        weights = probs * mask
        out = _swiglu(x, Ws1, Ws2, Ws3)
        h1 = jnp.einsum('bsd,ehd->ebsh', x, W1)
        h2 = jnp.einsum('bsd,ehd->ebsh', x, W2)
        eo = jnp.einsum('ebsh,edh->ebsd', jax.nn.sigmoid(h1) * h1 * h2, W3)
        out = out + jnp.einsum('ebsd,bse->bsd', eo, weights)
        return out
    x = x + _L0_attn_ref(_L0_cond_ref(x, cond_1024, L0_cond_Wx, L0_cond_Wh, L0_cond_b), L0_attn_Wq, L0_attn_Wk, L0_attn_Wv, L0_attn_Wo)
    x = x + _L0_ffn_ref(_L0_cond2_ref(x, cond_1024, L0_cond2_Wx, L0_cond2_Wh, L0_cond2_b), L0_ffn_Wm, L0_ffn_bm, L0_ffn_expert_emb, L0_ffn_W1, L0_ffn_b1, L0_ffn_W2, L0_ffn_b2, L0_ffn_Wo, L0_ffn_bo)
    x = x + _L1_attn_ref(_L1_cond_ref(x, cond_1024, L1_cond_Wx, L1_cond_Wh, L1_cond_b), L1_attn_Wq, L1_attn_bq, L1_attn_Wk, L1_attn_bk, L1_attn_Wv, L1_attn_bv, L1_attn_gamma, L1_attn_beta)
    x = x + _L1_ffn_ref(_L1_cond2_ref(cond_1024, x, L1_cond2_W_z, L1_cond2_U_z, L1_cond2_C_z, L1_cond2_b_z, L1_cond2_W_r, L1_cond2_U_r, L1_cond2_C_r, L1_cond2_b_r, L1_cond2_W, L1_cond2_U, L1_cond2_C, L1_cond2_b), L1_ffn_Wg, L1_ffn_routing_bias, L1_ffn_W1, L1_ffn_W2, L1_ffn_W3, L1_ffn_Ws1, L1_ffn_Ws2, L1_ffn_Ws3)
    return x

_drawn_inputs = setup_inputs


def setup_inputs(seed=0):
    import zlib

    import numpy as np

    out = dict(_drawn_inputs(seed))
    spreads = {'L0_cond_b': (0.0, 0.1),
     'L0_cond2_b': (0.0, 0.1),
     'L0_ffn_bm': (0.0, 0.1),
     'L0_ffn_b1': (0.0, 0.1),
     'L0_ffn_b2': (0.0, 0.1),
     'L0_ffn_bo': (0.0, 0.1),
     'L1_cond_b': (0.0, 0.1),
     'L1_attn_bq': (0.0, 0.1),
     'L1_attn_bk': (0.0, 0.8),
     'L1_attn_bv': (0.0, 0.1),
     'L1_attn_gamma': (1.0, 0.2),
     'L1_attn_beta': (0.0, 0.1),
     'L1_cond2_b_z': (0.0, 0.8),
     'L1_cond2_b_r': (0.0, 0.8),
     'L1_cond2_b': (0.0, 0.8),
     'L1_ffn_routing_bias': (0.0, 0.8)}
    factors = {'L1_cond2_W_z': 8.0,
     'L1_cond2_U_z': 8.0,
     'L1_cond2_C_z': 8.0,
     'L1_cond2_W_r': 8.0,
     'L1_cond2_U_r': 8.0,
     'L1_cond2_C_r': 8.0,
     'L1_cond2_W': 8.0,
     'L1_cond2_U': 8.0,
     'L1_cond2_C': 8.0,
     'L1_ffn_Wg': 8.0,
     'L1_ffn_W1': 8.0,
     'L1_ffn_W2': 8.0,
     'L1_ffn_W3': 8.0,
     'L1_ffn_Ws1': 8.0,
     'L1_ffn_Ws2': 8.0,
     'L1_ffn_Ws3': 8.0}
    for name, (base, spread) in spreads.items():
        noise = np.random.default_rng([zlib.crc32(name.encode()), seed]).standard_normal(out[name].shape)
        drawn = base * np.exp(spread * noise) if base else spread * noise
        out[name] = jnp.asarray(drawn.astype(out[name].dtype))
    for name, factor in factors.items():
        out[name] = (out[name] * factor).astype(out[name].dtype)
    return out
```

```python
from contextlib import ExitStack

import numpy as np

import concourse.bass as bass
from concourse import mybir

F32 = mybir.dt.float32
F16 = mybir.dt.float16
U32 = mybir.dt.uint32
ALU = mybir.AluOpType
ACT = mybir.ActivationFunctionType
AX_X = mybir.AxisListType.X

P = 128
B = 8
T = 256
D = 256
KT = D // P
C = 16
CW = C * B
HALF = CW // 2
NCH = T // C
LAG = 4
NI = NCH + LAG
S = 64.0
G4 = 4 * D
HD = 32
NH = D // HD
E1 = 16
EPS_Z = 1e-6

C0 = 9
W1_0 = 11
MISC = (0, 1, 2, 3, 4, 5, 7, 9, 10, 11, 13, 14)


def z_use(slot, second):
    return slot + sum(1 for m in MISC if m < slot) + (1 if second and slot in MISC else 0)


Z_USES = z_use(C, False)


def at(i, per, k):
    return (i + 1) * per + k


def split_matmul(pe, out, w, x, start, last=False):
    ins = None
    for k in range(KT):
        for wp, xp in ((0, 0), (1, 0), (0, 1)):
            ins = pe.matmul(out, w[wp](k), x[xp](k), start=start, stop=last and k == KT - 1 and xp == 1,
                            skip_group_check=True)
            start = False
    return ins


def pipeline_one(nc, t, xs, hs1):
    with ExitStack() as ctx:
        def sb(name, shape, dt=F32):
            return ctx.enter_context(nc.sbuf_tensor(name, shape, dt))

        def sem(name):
            return ctx.enter_context(nc.semaphore(name))

        names = (("a_wx", G4), ("a_wh", G4), ("e_wx", G4), ("e_wh", G4), ("wq", D), ("wk", D), ("wv", D), ("wo", D),
                 ("c_wx", D), ("c_wh", D), ("f_wo", D))
        w_hi = {n: sb(n + "_hi", [P, KT, w], F16) for n, w in names}
        w_lo = {n: sb(n + "_lo", [P, KT, w], F16) for n, w in names}
        wm_hi = sb("wm_hi", [P, KT, NH, 4, HD], F16)
        wm_lo = sb("wm_lo", [P, KT, NH, 4, HD], F16)
        w1s = sb("w1s", [P, E1, P], F16)
        es = sb("es", [P, E1], F16)
        w2_hi = sb("w2_hi", [P, E1, HD], F16)
        w2_lo = sb("w2_lo", [P, E1, HD], F16)
        b1 = sb("b1", [P, E1])
        NB = {"a_b": (0, G4), "e_b": (G4, G4), "c_b": (2 * G4, D), "f_bo": (2 * G4 + D, D),
              "f_bm": (2 * G4 + 2 * D, 4 * D), "f_b2": (2 * G4 + 6 * D, E1 * HD)}
        BR = 2 * G4 + 6 * D + E1 * HD
        brow = sb("brow", [2, BR], F16)
        ones2 = sb("ones2", [2, CW], F16)
        ident = sb("ident", [P, P])
        gsum = sb("gsum", [P, P])
        wcos = sb("wcos", [P, B * B])
        iota = sb("iota", [P, E1])
        keep = sb("keep", [P, 4, NI])
        h0c = sb("h0c", [P, 2, KT, B], F16)
        h0e = sb("h0e", [P, 2, KT, B], F16)
        a_hh = sb("a_hh", [P, KT, CW], F16)
        a_hl = sb("a_hl", [P, KT, CW], F16)
        e_hh = sb("e_hh", [P, KT, CW], F16)
        e_hl = sb("e_hl", [P, KT, CW], F16)
        c_hh = sb("c_hh", [P, KT, CW], F16)
        c_hl = sb("c_hl", [P, KT, CW], F16)
        ga, ge = sb("ga", [P, 64]), sb("ge", [P, 64])
        pa, pe_ = sb("pa", [P, 2, 16]), sb("pe_", [P, 2, 16])
        ca, ce = sb("ca", [P, 16]), sb("ce", [P, 16])
        ta, te_ = sb("ta", [P, 16]), sb("te_", [P, 16])
        fa, fe = sb("fa", [P, 16]), sb("fe", [P, 16])
        c32 = sb("c32", [P, 16])
        rst = sb("rst", [P, 4, 16], F16)
        rstc = sb("rstc", [P, 16])
        def tile(name, dt=F16):
            return sb(name, [P, KT, CW], dt)
        x_h, x_l = tile("x_h"), tile("x_l")
        ac_h, ac_l = tile("ac_h"), tile("ac_l")
        cc_h, cc_l = tile("cc_h"), tile("cc_l")
        x1, x1_h, x1_l = tile("x1", F32), tile("x1_h"), tile("x1_l")
        x2, x2_h, x2_l = tile("x2", F32), tile("x2_h"), tile("x2_l")
        qk = sb("qk", [P, 2, KT, CW])
        vv = tile("vv", F32)
        prod = sb("prod", [P, 4, 512])
        sw = sb("sw", [P, 2, 512])
        sv = sb("sv", [P, 2, 512])
        den, num = tile("den", F32), tile("num", F32)
        dmx, rcd, att = tile("dmx", F32), tile("rcd", F32), tile("att", F32)
        at_h, at_l = tile("at_h"), tile("at_l")
        t32 = sb("t32", [P, 512])
        tnew = sb("tnew", [P, NH * CW], F16)
        tst = sb("tst", [P, NH * CW], F16)
        lg = sb("lg", [P, NH, E1])
        m8 = sb("m8", [P, NH, 8])
        i8 = sb("i8", [P, NH, 8], U32)
        idf = sb("idf", [P, NH, 2])
        rt = sb("rt", [P, 8, NH, E1])
        sm = sb("sm", [P, 2, NH])
        wts = sb("wts", [P, NH, E1])
        hm32 = sb("hm32", [P, 2, NH * CW])
        hm_h = sb("hm_h", [P, 2, NH * CW], F16)
        hm_l = sb("hm_l", [P, 2, NH * CW], F16)
        tmp = sb("tmp", [P, 2, NH, HD])
        acc = sb("acc", [P, D])
        om_h, om_l = tile("om_h"), tile("om_l")

        g_a = [ctx.enter_context(nc.psum_tensor(f"g_a{h}", [P, 8, 8, B], F32)) for h in range(2)]
        g_e = [ctx.enter_context(nc.psum_tensor(f"g_e{h}", [P, 8, 8, B], F32)) for h in range(2)]
        g_c = ctx.enter_context(nc.psum_tensor("g_c", [P, C, KT, B], F32))
        xy = [ctx.enter_context(nc.psum_tensor(f"xy{h}", [P, 512], F32)) for h in range(2)]
        z = ctx.enter_context(nc.psum_tensor("z", [P, 512], F32))

        def wh(n, m):
            return (lambda k: w_hi[n][:, k, m * P:(m + 1) * P], lambda k: w_lo[n][:, k, m * P:(m + 1) * P])

        def cols(hi, lo, a, b):
            return (lambda k: hi[:, k, a:b], lambda k: lo[:, k, a:b])

        def bias(n, m):
            o = NB[n][0] + m * P
            return brow[0:2, o:o + P]

        with ExitStack() as st:
            def stage(name, shape):
                return st.enter_context(nc.sbuf_tensor("st_" + name, shape, F32))
            s_w = {"a_wx": hs1[:, :, 0:G4], "a_wh": hs1[:, :, G4:2 * G4], "wq": hs1[:, :, 2 * G4:2 * G4 + D],
                   "wk": hs1[:, :, 2 * G4 + D:2 * G4 + 2 * D], "e_wx": xs[:, :, 0:G4], "e_wh": xs[:, :, G4:2 * G4]}
            free = {"wv": prod[:, 0], "wo": prod[:, 1], "c_wx": sw[:, 0], "c_wh": sv[:, 0], "f_wo": t32[:, :]}
            s_w |= {n: ap.rearrange("p (k n) -> p k n", k=KT) for n, ap in free.items()}
            s_wm = prod[:, 2].rearrange("p (k h d) -> p k h d", k=KT, d=HD)
            s_w1 = hm32[:, :, :].rearrange("p a (e i) -> p (a e) i", i=P)
            s_es = stage("es", [P, E1])
            s_w2 = prod[:, 3].rearrange("p (e d) -> p e d", d=HD)
            s_b = stage("b", [1, BR])
            s_bl = st.enter_context(nc.sbuf_tensor("st_bl", [1, BR], F16))
            s_cond = stage("cond", [P, KT, B])
            s_c2 = stage("c2", [P, KT, B])
            loaded = st.enter_context(nc.semaphore("loaded"))
            loaded_const = st.enter_context(nc.semaphore("loaded_const"))
            loaded_x = st.enter_context(nc.semaphore("loaded_x"))
            xs_cleared = st.enter_context(nc.semaphore("xs_cleared"))
            hi_done = st.enter_context(nc.semaphore("hi_done"))
            lo_done = st.enter_context(nc.semaphore("lo_done"))
            row_done = st.enter_context(nc.semaphore("row_done"))
            row_sent = st.enter_context(nc.semaphore("row_sent"))
            cleared = st.enter_context(nc.semaphore("cleared"))
            keep_set = st.enter_context(nc.semaphore("keep_set"))
            cond_2 = st.enter_context(nc.semaphore("cond_2"))
            gates = ("a_wx", "a_wh", "e_wx", "e_wh")

            def jobs():
                for n, w in names:
                    if n in gates:
                        f = S if n.endswith("wx") else S / 2
                        yield s_w[n][:, :, 0:3 * D], w_hi[n][:, :, 0:3 * D], w_lo[n][:, :, 0:3 * D], f
                        yield s_w[n][:, :, 3 * D:G4], w_hi[n][:, :, 3 * D:G4], w_lo[n][:, :, 3 * D:G4], 2 * f
                    else:
                        f = S / 2 if n in ("wq", "wk", "wv") else S
                        yield s_w[n][:, :, :], w_hi[n][:, :, :], w_lo[n][:, :, :], f
                for k in range(KT):
                    for r in range(4):
                        yield s_wm[:, k, :, :], wm_hi[:, k, :, r, :], wm_lo[:, k, :, r, :], S
                yield s_w2, w2_hi[:, :, :], w2_lo[:, :, :], S
                yield s_w1, w1s[:, :, :], None, S
                yield s_es[:, :], es[:, :], None, S
                yield s_cond[:, :, :], h0c[:, 0], h0c[:, 1], 1.0
                yield s_cond[:, :, :], h0e[:, 0], h0e[:, 1], 2.0

            def bias_jobs():
                for n in ("a_b", "e_b"):
                    o = NB[n][0]
                    yield o, o + 3 * D, S
                    yield o + 3 * D, o + G4, 2 * S
                yield 2 * G4, BR, S

            NJ = len(list(jobs()))
            loads = [(s_w[n], t[n].rearrange("(k p) n -> p k n", p=P)) for n, _ in names]
            loads += [(s_wm, t["f_wm"].rearrange("(k p) (h d) -> p k h d", p=P, d=HD))]
            loads += [(s_w1[r * HD:(r + 1) * HD, :, :], t["f_w1"].rearrange("e d i -> d e i")) for r in range(4)]
            loads += [(s_es[r * HD:(r + 1) * HD, :], t["f_emb"]) for r in range(4)]
            loads += [(s_w2, t["f_w2"].rearrange("e i o -> i e o")), (b1[:, :], t["f_b1"]),
                      (s_cond[:, :, :], t["cond"].rearrange("(k p) b -> p k b", p=P))]
            for n, (o, w) in NB.items():
                if n == "f_bm":
                    for r in range(4):
                        loads.append((s_b[0:1, o:o + w].rearrange("a (h r d) -> a h r d", r=4, d=HD)[:, :, r, :],
                                      t[n].rearrange("(a h d) -> a h d", a=1, d=HD)))
                else:
                    loads.append((s_b[0:1, o:o + w], t[n].rearrange("(a n) -> a n", a=1)))
            consts = [(ident[:, :], t["k_ident"]), (gsum[:, :], t["k_gsum"]), (wcos[:, :], t["k_wcos"]),
                      (iota[:, :], t["k_iota"])]

            block = st.enter_context(nc.Block())

            @block.sync
            def _(sp):
                for dst, src in loads[0::2]:
                    sp.dma_start(dst, src).then_inc(loaded, 16)
                for dst, src in consts:
                    sp.dma_start(dst, src).then_inc(loaded_const, 16)
                sp.wait_ge(row_done, 5)
                sp.dma_start(brow[1:2, :], s_bl[0:1, :]).then_inc(row_sent, 16)
                sp.wait_ge(row_sent, 16)
                sp.wait_ge(loaded_const, 16 * len(consts))

            @block.scalar
            def _(act):
                for dst, src in loads[1::2]:
                    act.dma_start(dst, src).then_inc(loaded, 16)
                act.wait_ge(loaded, 16 * len(loads))
                for src, hi, _lo, f in jobs():
                    act.activation(hi, src, ACT.Copy, scale=f).then_inc(hi_done, 1)
                for a, b, f in bias_jobs():
                    act.activation(brow[0:1, a:b], s_b[0:1, a:b], ACT.Copy, scale=f).then_inc(hi_done, 1)

            @block.vector
            def _(dve):
                for tl in (a_hl, c_hl, e_hl, a_hh, c_hh, e_hh, x2_h, x2_l, x1_h, x1_l, cc_h, cc_l):
                    dve.memset(tl[:, :, :], 0.0).then_inc(cleared, 1)
                for tl in (ca, ce, acc):
                    dve.memset(tl[:, :], 0.0).then_inc(cleared, 1)
                dve.memset(ones2[:, :], 1.0).then_inc(cleared, 1)
                dve.memset(keep[:, 0:3:2, :], 1.0).then_inc(keep_set, 1)
                dve.memset(keep[:, 1:4:2, :], 0.0).then_inc(keep_set, 1)
                dve.wait_ge(keep_set, 2)
                for row, it in ((0, 1), (2, LAG - 1)):
                    dve.memset(keep[:, row, it:it + 1], 0.0).then_inc(keep_set, 1)
                    dve.memset(keep[:, row + 1, it:it + 1], 1.0).then_inc(keep_set, 1)
                for n, (src, hi, lo, f) in enumerate(jobs()):
                    dve.wait_ge(hi_done, n + 1)
                    if lo is not None:
                        dve.scalar_tensor_tensor(out=lo, in0=src, scalar=f, in1=hi, op0=ALU.mult,
                                                 op1=ALU.subtract).then_inc(lo_done, 1)
                    else:
                        for a in (HD, 3 * HD):
                            dve.scalar_tensor_tensor(out=hi[a:a + HD], in0=src[a:a + HD], scalar=f,
                                                     in1=hi[a:a + HD], op0=ALU.mult,
                                                     op1=ALU.subtract).then_inc(lo_done, 1)
                for n, (a, b, f) in enumerate(bias_jobs()):
                    dve.wait_ge(hi_done, NJ + n + 1)
                    dve.scalar_tensor_tensor(out=s_bl[0:1, a:b], in0=s_b[0:1, a:b], scalar=f, in1=brow[0:1, a:b],
                                             op0=ALU.mult, op1=ALU.subtract).then_inc(row_done, 1)
                dve.wait_ge(lo_done, NJ + 2)
                dve.wait_ge(cleared, 22)
                dve.tensor_copy(a_hh[:, :, CW - B:CW], h0e[:, 0]).then_inc(lo_done, 1)
                dve.tensor_copy(a_hl[:, :, CW - B:CW], h0e[:, 1]).then_inc(lo_done, 1)

            @block.gpsimd
            def _(pool):
                for tl in (hm_h, hm_l):
                    pool.memset(tl[:, :, :], 0.0).then_inc(cleared, 1)
                pool.memset(tst[:, :], 0.0).then_inc(cleared, 1)
                pool.memset(wts[:, :, :], 0.0).then_inc(cleared, 1)
                pool.memset(ac_h[:, :, :], 0.0).then_inc(cleared, 1)
                pool.memset(ac_l[:, :, :], 0.0).then_inc(cleared, 1)
                pool.wait_ge(lo_done, 8)
                pool.wait_ge(lo_done, NJ + 2)
                pool.memset(hm32[:, :, :], 0.0).then_inc(cleared, 1)
                pool.memset(xs[:, :, :], 0.0).then_inc(xs_cleared, 1)
                pool.wait_ge(xs_cleared, 1)
                pool.dma_start(xs[:, :, LAG * CW:(LAG + NCH) * CW],
                               t["x"].rearrange("(k p) n -> p k n", p=P)).then_inc(loaded_x, 16)
                pool.wait_ge(loaded_x, 16)

        a_pe, a_act, a_part, a_cell, a_tanh = (sem("a_" + n) for n in ("pe", "act", "part", "cell", "tanh"))
        e_pe, e_act, e_part, e_cell, e_tanh = (sem("e_" + n) for n in ("pe", "act", "part", "cell", "tanh"))
        a_hi, a_h32, a_lo = (sem("a_" + n) for n in ("hi", "h32", "lo"))
        e_hi, e_h32, e_lo = (sem("e_" + n) for n in ("hi", "h32", "lo"))
        c_pe, c_hi, c_32, c_lo = (sem("c_" + n) for n in ("pe", "hi", "32", "lo"))
        x_split, ac_copied, cc_copied, c_reset, e_reset = (
            sem(n) for n in ("x_split", "ac_copied", "cc_copied", "c_reset", "e_reset"))
        z_full, z_free, xy_full = sem("z_full"), sem("z_free"), sem("xy_full")
        g_hi, g_32, g_lo = sem("g_hi"), sem("g_32"), sem("g_lo")
        acc_part, acc_done = sem("acc_part"), sem("acc_done")
        proj_read, prod_done, s_read, b_fin, x1_done, x1_split, x1_kept = (
            sem(n) for n in ("proj_read", "prod_done", "s_read", "b_fin", "x1_done", "x1_split", "x1_kept"))
        t_read, t_split, t_copied, route, route_t = (
            sem(n) for n in ("t_read", "t_split", "t_copied", "route", "route_t"))
        om_split, x2_done, x2_split, x2_kept = (sem(n) for n in ("om_split", "x2_done", "x2_split", "x2_kept"))
        ROUTE = 2 * NH + 12
        per = [(a_pe, 16), (a_act, 16), (a_part, 32), (a_cell, 16), (a_tanh, 16), (a_hi, 16), (a_h32, 16), (a_lo, 16),
               (e_pe, 16), (e_act, 16), (e_part, 32), (e_cell, 16), (e_tanh, 16), (e_hi, 16), (e_h32, 16), (e_lo, 16),
               (c_pe, 16), (c_hi, 16), (c_32, 16), (c_lo, 16), (x_split, 2), (ac_copied, 2), (cc_copied, 2),
               (c_reset, 4), (e_reset, 6), (z_full, Z_USES), (z_free, Z_USES - 1), (xy_full, 32), (g_hi, 32),
               (g_32, 32), (g_lo, 32), (acc_part, 16), (acc_done, 16), (proj_read, 2), (prod_done, 4), (s_read, 16),
               (b_fin, 4), (x1_done, 1), (x1_split, 1), (x1_kept, 1), (t_read, 2), (t_split, 4), (t_copied, 1),
               (route, ROUTE), (route_t, 1), (om_split, 1), (x2_done, 1), (x2_split, 1), (x2_kept, 1)]

        def project_half(pe, name, bank, half, xh, xl):
            first = True
            for m in range(8):
                out = bank[half][:, :, m, :]
                pe.matmul(out, bias(name + "_b", m), ones2[0:2, 0:HALF], start=first, stop=False,
                          skip_group_check=True)
                first = False
                last = split_matmul(pe, out, wh(name + "_wx", m), cols(xh, xl, half * HALF, (half + 1) * HALF), False)
            return last

        def project_c(pe):
            for m in range(KT):
                pe.matmul(g_c[:, :, m, :], bias("c_b", m), ones2[0:2, 0:CW], start=(m == 0), stop=False,
                          skip_group_check=True)
                last = split_matmul(pe, g_c[:, :, m, :], wh("c_wx", m), cols(x1_h, x1_l, 0, CW), False)
            return last

        with ExitStack() as st:
            x_first = st.enter_context(nc.semaphore("x_first"))
            primed = st.enter_context(nc.semaphore("primed"))
            block = st.enter_context(nc.Block())

            @block.vector
            def _(dve):
                first = xs[:, :, LAG * CW:(LAG + 1) * CW]
                dve.tensor_copy(x_h[:, :, :], first).then_inc(x_first, 1)
                dve.wait_ge(x_first, 1)
                dve.tensor_tensor(x_l[:, :, :], first, x_h[:, :, :], ALU.subtract).then_inc(x_first, 1)

            @block.tensor
            def _(pe):
                pe.wait_ge(x_first, 2)
                project_half(pe, "a", g_a, 0, x_h, x_l)
                project_half(pe, "e", g_e, 0, x2_h, x2_l)
                project_c(pe)
                for h in range(2):
                    pe.matmul(xy[h][:, :], w1s[:, 0, :], tst[:, 0:512], start=True, stop=True)
                pe.matmul(z[:, :], w1s[:, 0, :], tst[:, 0:512], start=True, stop=True).then_inc(primed, 1)

            @block.sync
            def _(sp):
                for s, n in per:
                    sp.sem_inc(s, n)

        block = ctx.enter_context(nc.Block())

        @block.tensor
        def _(pe):
            def lstm_step(i, slot, name, bank, hh, hl, hi_sem, lo_sem, done):
                prev = (slot - 1) % C * B
                out = bank[slot // 8]
                pe.wait_ge(hi_sem, at(i, C, slot))
                for m in range(8):
                    for k in range(KT):
                        for wt in (w_hi, w_lo):
                            pe.matmul(out[:, slot % 8, m, :], wt[name][:, k, m * P:(m + 1) * P],
                                      hh[:, k, prev:prev + B], start=False, stop=False, skip_group_check=True)
                pe.wait_ge(lo_sem, at(i, C, slot))
                for m in range(8):
                    for k in range(KT):
                        last = pe.matmul(out[:, slot % 8, m, :], w_hi[name][:, k, m * P:(m + 1) * P],
                                         hl[:, k, prev:prev + B], start=False, stop=(k == KT - 1),
                                         skip_group_check=True)
                last.then_inc(done, 1)

            def rnn_step(i, slot):
                s = (slot - C0) % C
                prev = (s - 1) % C * B
                pe.wait_ge(c_hi, at(i, C, slot))
                pe.wait_ge(c_32, at(i, C, slot))
                for m in range(KT):
                    for k in range(KT):
                        for wt in (w_hi, w_lo):
                            pe.matmul(g_c[:, s, m, :], wt["c_wh"][:, k, m * P:(m + 1) * P],
                                      c_hh[:, k, prev:prev + B], start=False, stop=False, skip_group_check=True)
                pe.wait_ge(c_lo, at(i, C, slot))
                for m in range(KT):
                    for k in range(KT):
                        last = pe.matmul(g_c[:, s, m, :], w_hi["c_wh"][:, k, m * P:(m + 1) * P],
                                         c_hl[:, k, prev:prev + B], start=False, stop=(k == KT - 1),
                                         skip_group_check=True)
                last.then_inc(c_pe, 1)

            def misc(i, slot):
                if slot == 0:
                    pe.wait_ge(ac_copied, at(i, 2, 0))
                pe_z = at(i, Z_USES, z_use(slot, False))
                if slot in (0, 1):
                    pe.wait_ge(z_free, pe_z)
                    for j, n in enumerate(("wq", "wk") if slot == 0 else ("wv",)):
                        for m in range(KT):
                            o = (2 * j + m) * P
                            last = split_matmul(pe, z[:, o:o + P], wh(n, m), cols(ac_h, ac_l, 0, CW),
                                                start=(o == 0), last=True)
                elif 2 <= slot <= 5:
                    pe.wait_ge(prod_done, at(i, 4, slot - 1))
                    pe.wait_ge(z_free, pe_z)
                    last = pe.matmul(z[:, :], gsum[:, :], prod[:, slot - 2, :], start=True, stop=True)
                elif slot == 7:
                    pe.wait_ge(b_fin, at(i, 4, 4))
                    pe.wait_ge(z_free, pe_z)
                    for m in range(KT):
                        last = split_matmul(pe, z[:, m * P:(m + 1) * P], wh("wo", m), cols(at_h, at_l, 0, CW),
                                            start=(m == 0), last=True)
                elif slot in (9, 10):
                    pe.wait_ge(cc_copied, at(i, 2, 2))
                    pe.wait_ge(z_free, pe_z)
                    for j in range(4):
                        h = 4 * (slot - 9) + j
                        o = z[:, j * CW:(j + 1) * CW]
                        pe.matmul(o, bias("f_bm", h), ones2[0:2, :], start=(j == 0), stop=False,
                                  skip_group_check=True)
                        w = (lambda k, h=h: wm_hi[:, k, h].rearrange("p r d -> p (r d)"),
                             lambda k, h=h: wm_lo[:, k, h].rearrange("p r d -> p (r d)"))
                        last = split_matmul(pe, o, w, cols(cc_h, cc_l, 0, CW), False, last=True)
                elif slot == 11:
                    pe.wait_ge(t_split, at(i, 4, 4))
                    pe.wait_ge(z_free, pe_z)
                    for h in range(NH):
                        last = pe.matmul(z[:, h * E1:(h + 1) * E1], tnew[:, h * CW:(h + 1) * CW], es[:, :],
                                         start=(h == 0), stop=True, skip_group_check=True)
                elif slot == 13:
                    pe.wait_ge(acc_done, at(i, E1, 14))
                    pe.wait_ge(z_free, pe_z)
                    for m in range(KT):
                        last = pe.transpose(z[:, m * P:(m + 1) * P], acc[:, m * P:(m + 1) * P], ident[:, :])
                elif slot == 14:
                    pe.wait_ge(om_split, at(i, 1, 1))
                    pe.wait_ge(z_free, pe_z)
                    for m in range(KT):
                        o = z[:, m * P:(m + 1) * P]
                        pe.matmul(o, bias("f_bo", m), ones2[0:2, :], start=(m == 0), stop=False,
                                  skip_group_check=True)
                        last = split_matmul(pe, o, wh("f_wo", m), cols(om_h, om_l, 0, CW), False, last=True)
                last.then_inc(z_full, 1)

            def w1(i, slot):
                e = (slot - W1_0) % E1
                if slot == W1_0:
                    pe.wait_ge(t_copied, at(i, 1, 1))
                for h in range(2):
                    pe.wait_ge(g_hi, at(i, 32, 2 * slot + 1 + h))
                    pe.wait_ge(g_32, at(i, 32, 2 * slot + 1 + h))
                    pe.matmul(xy[h][:, :], w1s[:, e, :], tst[:, h * 512:(h + 1) * 512], start=True,
                              stop=True).then_inc(xy_full, 1)

            def w2(i, slot):
                e = (slot - W1_0 - 2) % E1
                b = (slot - 1) % 2
                pe.wait_ge(g_lo, at(i, 32, 2 * slot))
                pe.wait_ge(z_free, at(i, Z_USES, z_use(slot, True)))
                o2 = NB["f_b2"][0] + e * HD
                pe.matmul(z[:, 0:D].rearrange("p (h d) -> p h d", d=HD), ones2[0:2, :],
                          brow[0:2, o2:o2 + HD].unsqueeze(1).to_broadcast([2, NH, HD]), start=True, stop=False,
                          skip_group_check=True)
                for h in range(NH):
                    o = z[:, h * HD:(h + 1) * HD]
                    hh = hm_h[:, b, h * CW:(h + 1) * CW]
                    pe.matmul(o, hh, w2_hi[:, e, :], start=False, stop=False, skip_group_check=True)
                    pe.matmul(o, hh, w2_lo[:, e, :], start=False, stop=False, skip_group_check=True)
                    last = pe.matmul(o, hm_l[:, b, h * CW:(h + 1) * CW], w2_hi[:, e, :], start=False, stop=True,
                                     skip_group_check=True)
                last.then_inc(z_full, 1)

            with pe.Fori(0, NI) as i:
                for slot in range(C):
                    lstm_step(i, slot, "a_wh", g_a, a_hh, a_hl, a_hi, a_lo, a_pe)
                    if slot == 2:
                        pe.wait_ge(a_act, at(i, C, 0))
                        project_half(pe, "a", g_a, 1, x_h, x_l)
                    if slot == 10:
                        pe.wait_ge(x_split, at(i, 2, 2))
                        pe.wait_ge(a_act, at(i, C, 8))
                        project_half(pe, "a", g_a, 0, x_h, x_l)
                    if slot in MISC:
                        misc(i, slot)
                    if slot == 0:
                        pe.wait_ge(e_reset, at(i, 6, 0))
                    lstm_step(i, slot, "e_wh", g_e, e_hh, e_hl, e_hi, e_lo, e_pe)
                    if slot == 4:
                        pe.wait_ge(e_act, at(i, C, 0))
                        project_half(pe, "e", g_e, 1, x2_h, x2_l)
                    if slot == 15:
                        pe.wait_ge(x2_split, at(i, 1, 1))
                        pe.wait_ge(e_act, at(i, C, 8))
                        project_half(pe, "e", g_e, 0, x2_h, x2_l)
                    if slot == C0:
                        pe.wait_ge(c_reset, at(i, 4, 4))
                    rnn_step(i, slot)
                    if slot == C0 - 1:
                        pe.wait_ge(x1_split, at(i, 1, 1))
                        pe.wait_ge(c_hi, at(i, C, C0))
                        pe.wait_ge(c_32, at(i, C, C0))
                        project_c(pe)
                    w1(i, slot)
                    w2(i, slot)

        @block.scalar
        def _(act):
            def gates(i, slot, bank, g, mm, done):
                act.wait_ge(mm, at(i, C, slot + 1))
                act.activation(g[:, :], bank[slot // 8][:, slot % 8].rearrange("p m b -> p (m b)"), ACT.Tanh,
                               scale=1.0 / (2 * S)).then_inc(done, 1)

            def cell_tanh(i, slot, c, tc, cell, done):
                act.wait_ge(cell, at(i, C, slot + 1))
                act.activation(tc[:, :], c[:, :], ACT.Tanh, scale=0.5).then_inc(done, 1)

            def gelu(i, slot, h, hi):
                e = (slot - W1_0 - 1) % E1
                b = slot % 2
                dst = hm_h if hi else hm32
                if hi:
                    act.wait_ge(xy_full, at(i, 32, 2 * slot - 1 + h))
                    if h == 0:
                        act.wait_ge(z_full, at(i, Z_USES, z_use(slot, False)))
                act.activation(dst[:, b, h * 512:(h + 1) * 512], xy[h][:, :], ACT.Gelu, bias=b1[:, e:e + 1],
                               scale=1.0 / S).then_inc(g_hi if hi else g_32, 1)

            def misc(i, slot):
                act.wait_ge(z_full, at(i, Z_USES, z_use(slot, False) + 1))
                if slot == 0:
                    act.activation(qk[:, :, :, :].rearrange("p a k n -> p (a k n)"), z[:, :], ACT.Relu,
                                   scale=1.0 / S).then_inc(z_free, 1)
                elif slot == 1:
                    act.activation(vv[:, :, :].rearrange("p k n -> p (k n)"), z[:, 0:KT * CW], ACT.Copy,
                                   scale=1.0 / S).then_inc(z_free, 1)
                else:
                    act.wait_ge(t_split, at(i, 4, 2 * (slot - 9)))
                    act.activation(t32[:, :], z[:, :], ACT.Copy, scale=1.0 / S).then_inc(z_free, 1)

            act.activation(rstc[:, :], ca[:, :], ACT.Gelu)
            with act.Fori(0, NI) as i:
                for slot in range(C):
                    gates(i, slot, g_a, ga, a_pe, a_act)
                    gelu(i, slot, 0, True)
                    cell_tanh(i, slot, ca, ta, a_cell, a_tanh)
                    if slot in (0, 1, 9, 10):
                        misc(i, slot)
                    gelu(i, slot, 0, False)
                    gelu(i, slot, 1, True)
                    gates(i, slot, g_e, ge, e_pe, e_act)
                    gelu(i, slot, 1, False)
                    cell_tanh(i, slot, ce, te_, e_cell, e_tanh)
                    s = (slot - C0) % C
                    act.wait_ge(c_pe, at(i, C, slot + 1))
                    act.activation(c_hh[:, :, s * B:(s + 1) * B], g_c[:, s, :, :], ACT.Tanh,
                                   scale=1.0 / S).then_inc(c_hi, 1)
                    act.activation(c32[:, :].rearrange("p (k b) -> p k b", b=B), g_c[:, s, :, :], ACT.Tanh,
                                   scale=1.0 / S).then_inc(c_32, 1)
                    if slot == 12:
                        act.wait_ge(route, at(i, ROUTE, NH + 1))
                        act.activation(rt[:, 1, :, :], rt[:, 0, :, :], ACT.Tanh, scale=0.5).then_inc(route_t, 1)

        @block.gpsimd
        def _(pool):
            with pool.Fori(0, NI) as i:
                for slot in range(C):
                    b = slot % 2
                    if 1 <= slot <= 4:
                        p = slot - 1
                        m, s0 = p // 2, (p % 2) * HALF
                        if p == 0:
                            pool.wait_ge(z_free, at(i, Z_USES, 1))
                        q3 = qk[:, 0, m, s0:s0 + HALF].rearrange("p (t l) -> p t l", l=B)
                        k3 = qk[:, 1, m, s0:s0 + HALF].rearrange("p (t l) -> p t l", l=B)
                        pool.tensor_tensor(prod[:, p, :].rearrange("p (t l m) -> p t l m", l=B, m=B),
                                           q3.unsqueeze(3).to_broadcast([P, 8, B, B]),
                                           k3.unsqueeze(2).to_broadcast([P, 8, B, B]),
                                           ALU.mult).then_inc(prod_done, 1)
                    for h in range(2):
                        pool.wait_ge(g_hi, at(i, 32, 2 * slot + 1 + h))
                        pool.wait_ge(g_32, at(i, 32, 2 * slot + 1 + h))
                        r = slice(h * 512, (h + 1) * 512)
                        pool.tensor_tensor(hm_l[:, b, r], hm32[:, b, r], hm_h[:, b, r],
                                           ALU.subtract).then_inc(g_lo, 1)
                    if slot == 7:
                        pool.wait_ge(x1_done, at(i, 1, 1))
                        pool.tensor_copy(xs[:, :, bass.ds((i + (LAG - 1)) * CW, CW)], x1[:, :, :]).then_inc(x1_kept, 1)
                    if slot == 14:
                        pool.wait_ge(x2_done, at(i, 1, 1))
                        pool.tensor_copy(xs[:, :, bass.ds((i + (LAG - 3)) * CW, CW)], x2[:, :, :]).then_inc(x2_kept, 1)

        @block.vector
        def _(dve):
            def cell(i, slot, g, pt, c, act_sem, part, cell_sem):
                dve.wait_ge(act_sem, at(i, C, slot + 1))
                dve.scalar_tensor_tensor(out=pt[:, 0, :], in0=g[:, 16:32], scalar=1.0, in1=c[:, :], op0=ALU.add,
                                         op1=ALU.mult).then_inc(part, 1)
                dve.scalar_tensor_tensor(out=pt[:, 1, :], in0=g[:, 0:16], scalar=1.0, in1=g[:, 48:64], op0=ALU.add,
                                         op1=ALU.mult).then_inc(part, 1)
                dve.wait_ge(part, at(i, 32, 2 * slot + 2))
                dve.scalar_tensor_tensor(out=c[:, :], in0=pt[:, 0, :], scalar=0.5, in1=pt[:, 1, :], op0=ALU.mult,
                                         op1=ALU.add).then_inc(cell_sem, 1)

            def state(i, slot, g, tc, f, hh, hl, tanh_sem, hi_sem, h32_sem, lo_sem):
                k2 = "p (k b) -> p k b"
                o3, t3, f3 = (v.rearrange(k2, b=B) for v in (g[:, 32:48], tc[:, :], f[:, :]))
                r = slice(slot * B, (slot + 1) * B)
                dve.wait_ge(tanh_sem, at(i, C, slot + 1))
                dve.scalar_tensor_tensor(out=hh[:, :, r], in0=o3, scalar=1.0, in1=t3, op0=ALU.add,
                                         op1=ALU.mult).then_inc(hi_sem, 1)
                dve.scalar_tensor_tensor(out=f3, in0=o3, scalar=1.0, in1=t3, op0=ALU.add,
                                         op1=ALU.mult).then_inc(h32_sem, 1)
                dve.wait_ge(hi_sem, at(i, C, slot + 1))
                dve.wait_ge(h32_sem, at(i, C, slot + 1))
                dve.tensor_tensor(hl[:, :, r], f3, hh[:, :, r], ALU.subtract).then_inc(lo_sem, 1)

            def combine(i, slot):
                e = (slot - W1_0 - 3) % E1
                dve.wait_ge(z_full, at(i, Z_USES, z_use(slot, False)))
                zz = z[:, 0:D].rearrange("p (h d) -> p h d", d=HD)
                w = wts[:, :, e].unsqueeze(2).to_broadcast([P, NH, HD])
                a3 = acc[:, :].rearrange("p (h d) -> p h d", d=HD)
                dve.wait_ge(acc_done, at(i, E1, slot))
                if e == 0:
                    dve.wait_ge(route, at(i, ROUTE, ROUTE))
                dve.tensor_tensor(tmp[:, slot % 2, :, :], zz, w, ALU.mult).then_inc(z_free, 1)
                dve.wait_ge(z_free, at(i, Z_USES, z_use(slot, False)))
                if e == 0:
                    dve.tensor_copy(a3, tmp[:, slot % 2, :, :]).then_inc(acc_done, 1)
                else:
                    dve.tensor_tensor(a3, a3, tmp[:, slot % 2, :, :], ALU.add).then_inc(acc_done, 1)

            def misc(i, slot):
                def z_wait():
                    dve.wait_ge(z_full, at(i, Z_USES, z_use(slot, False) + 1))
                z_read = at(i, Z_USES, z_use(slot, False) + 1)
                if 2 <= slot <= 5:
                    p = slot - 2
                    m, s0 = p // 2, (p % 2) * HALF
                    b = p % 2
                    z_wait()
                    dve.tensor_tensor(sw[:, b, :].rearrange("p (t c) -> p t c", c=B * B),
                                      z[:, :].rearrange("p (t c) -> p t c", c=B * B),
                                      wcos[:, :].unsqueeze(1).to_broadcast([P, 8, B * B]), ALU.mult).then_inc(z_free, 1)
                    dve.wait_ge(z_free, z_read)
                    dve.tensor_reduce(den[:, m, s0:s0 + HALF], sw[:, b, :].rearrange("p (c m) -> p c m", m=B), AX_X,
                                      ALU.add).then_inc(s_read, 1)
                    v3 = vv[:, m, s0:s0 + HALF].rearrange("p (t l) -> p t l", l=B)
                    dve.tensor_tensor(sv[:, b, :].rearrange("p (t l m) -> p t l m", l=B, m=B),
                                      sw[:, b, :].rearrange("p (t l m) -> p t l m", l=B, m=B),
                                      v3.unsqueeze(2).to_broadcast([P, 8, B, B]), ALU.mult).then_inc(s_read, 1)
                    dve.wait_ge(s_read, at(i, 16, 4 * p + 2))
                    dve.tensor_reduce(num[:, m, s0:s0 + HALF], sv[:, b, :].rearrange("p (c m) -> p c m", m=B), AX_X,
                                      ALU.add).then_inc(s_read, 1)
                    dve.tensor_scalar(dmx[:, m, s0:s0 + HALF], den[:, m, s0:s0 + HALF], EPS_Z, None,
                                      ALU.max).then_inc(s_read, 1)
                elif slot == 6:
                    dve.wait_ge(s_read, at(i, 16, 16))
                    dve.reciprocal(rcd[:, :, :], dmx[:, :, :]).then_inc(b_fin, 1)
                    dve.wait_ge(b_fin, at(i, 4, 1))
                    dve.tensor_tensor(att[:, :, :], num[:, :, :], rcd[:, :, :], ALU.mult).then_inc(b_fin, 1)
                    dve.wait_ge(b_fin, at(i, 4, 2))
                    dve.tensor_copy(at_h[:, :, :], att[:, :, :]).then_inc(b_fin, 1)
                    dve.wait_ge(b_fin, at(i, 4, 3))
                    dve.tensor_tensor(at_l[:, :, :], att[:, :, :], at_h[:, :, :], ALU.subtract).then_inc(b_fin, 1)
                elif slot == 7:
                    z_wait()
                    dve.wait_ge(x1_kept, at(i, 1, 0))
                    dve.scalar_tensor_tensor(out=x1[:, :, :], in0=z[:, 0:KT * CW].rearrange("p (k n) -> p k n", n=CW),
                                             scalar=1.0 / S, in1=xs[:, :, bass.ds((i + (LAG - 1)) * CW, CW)],
                                             op0=ALU.mult, op1=ALU.add).then_inc(x1_done, 1)
                    dve.wait_ge(x1_done, at(i, 1, 1))
                    dve.tensor_copy(x1_h[:, :, :], x1[:, :, :]).then_inc(z_free, 1)
                    dve.wait_ge(z_free, z_read)
                    dve.tensor_tensor(x1_l[:, :, :], x1[:, :, :], x1_h[:, :, :], ALU.subtract).then_inc(x1_split, 1)
                elif slot == 8:
                    nxt = xs[:, :, bass.ds((i + (LAG + 1)) * CW, CW)]
                    dve.tensor_scalar(x_h[:, :, :], nxt, 1.0, None, ALU.mult).then_inc(x_split, 1)
                    dve.wait_ge(x_split, at(i, 2, 1))
                    dve.tensor_tensor(x_l[:, :, :], nxt, x_h[:, :, :], ALU.subtract).then_inc(x_split, 1)
                elif slot in (9, 10):
                    j = slot - 9
                    r = slice(j * 512, (j + 1) * 512)
                    dve.wait_ge(z_free, z_read)
                    dve.tensor_copy(tnew[:, r], t32[:, :]).then_inc(t_split, 1)
                    dve.wait_ge(t_split, at(i, 4, 2 * j + 1))
                    dve.tensor_tensor(tnew[P // 2:P, r], t32[P // 2:P, :], tnew[P // 2:P, r],
                                      ALU.subtract).then_inc(t_split, 1)
                elif slot == 11:
                    dve.wait_ge(t_split, at(i, 4, 4))
                    dve.wait_ge(xy_full, at(i, 32, 2 * slot))
                    z_wait()
                    dve.tensor_scalar(lg[:, :, :].rearrange("p h e -> p (h e)"), z[:, 0:NH * E1], 1.0 / S, None,
                                      ALU.mult).then_inc(z_free, 1)
                    dve.wait_ge(z_free, z_read)
                    dve.tensor_copy(tst[:, :], tnew[:, :]).then_inc(t_copied, 1)
                    for h in range(NH):
                        dve.max(m8[:, h, :], lg[:, h, :]).then_inc(route, 1)
                elif slot == 12:
                    dve.wait_ge(route, at(i, ROUTE, NH))
                    dve.tensor_tensor(rt[:, 0, :, :], lg[:, :, :], m8[:, :, 0].unsqueeze(2).to_broadcast([P, NH, E1]),
                                      ALU.subtract).then_inc(route, 1)
                    for h in range(NH):
                        dve.max_index(i8[:, h, :], m8[:, h, :], lg[:, h, :]).then_inc(route, 1)
                    dve.wait_ge(route, at(i, ROUTE, 2 * NH + 1))
                    dve.tensor_copy(idf[:, :, :], i8[:, :, 0:2]).then_inc(route, 1)
                elif slot == 13:
                    z_wait()
                    z3 = z[:, 0:KT * CW].rearrange("p (k n) -> p k n", n=CW)
                    dve.tensor_copy(om_h[:, :, :], z3).then_inc(om_split, 1)
                    dve.wait_ge(om_split, at(i, 1, 1))
                    dve.tensor_tensor(om_l[:, :, :], z3, om_h[:, :, :], ALU.subtract).then_inc(z_free, 1)
                    dve.wait_ge(z_free, z_read)
                    n = 2 * NH + 2
                    io = iota[:, :].unsqueeze(1).to_broadcast([P, NH, E1])
                    dve.wait_ge(route, at(i, ROUTE, n))
                    for j in range(2):
                        dve.tensor_tensor(rt[:, 2 + j, :, :], io, idf[:, :, j].unsqueeze(2).to_broadcast([P, NH, E1]),
                                          ALU.is_equal).then_inc(route, 1)
                    dve.wait_ge(route_t, at(i, 1, 1))
                    dve.tensor_scalar(rt[:, 4, :, :], rt[:, 1, :, :], -1.0, 1.0, ALU.mult, ALU.add).then_inc(route, 1)
                    dve.wait_ge(route, at(i, ROUTE, n + 3))
                    dve.reciprocal(rt[:, 5, :, :], rt[:, 4, :, :]).then_inc(route, 1)
                    dve.tensor_tensor(rt[:, 2, :, :], rt[:, 2, :, :], rt[:, 3, :, :], ALU.add).then_inc(route, 1)
                    dve.wait_ge(route, at(i, ROUTE, n + 5))
                    dve.scalar_tensor_tensor(out=rt[:, 6, :, :], in0=rt[:, 1, :, :], scalar=1.0, in1=rt[:, 5, :, :],
                                             op0=ALU.add, op1=ALU.mult).then_inc(route, 1)
                    dve.wait_ge(route, at(i, ROUTE, n + 6))
                    dve.tensor_reduce(sm[:, 0, :], rt[:, 6, :, :], AX_X, ALU.add).then_inc(route, 1)
                    dve.tensor_tensor(rt[:, 7, :, :], rt[:, 6, :, :], rt[:, 2, :, :], ALU.mult).then_inc(route, 1)
                    dve.wait_ge(route, at(i, ROUTE, n + 8))
                    dve.reciprocal(sm[:, 1, :], sm[:, 0, :]).then_inc(route, 1)
                    dve.wait_ge(route, at(i, ROUTE, n + 9))
                    dve.scalar_tensor_tensor(out=wts[:, :, :], in0=rt[:, 7, :, :], scalar=1.0 / S,
                                             in1=sm[:, 1, :].unsqueeze(2).to_broadcast([P, NH, E1]), op0=ALU.mult,
                                             op1=ALU.mult).then_inc(route, 1)
                elif slot == 14:
                    z_wait()
                    dve.wait_ge(x2_kept, at(i, 1, 0))
                    dve.scalar_tensor_tensor(out=x2[:, :, :], in0=z[:, 0:KT * CW].rearrange("p (k n) -> p k n", n=CW),
                                             scalar=1.0 / S, in1=xs[:, :, bass.ds((i + (LAG - 3)) * CW, CW)],
                                             op0=ALU.mult, op1=ALU.add).then_inc(x2_done, 1)
                    dve.wait_ge(x2_done, at(i, 1, 1))
                    dve.tensor_copy(x2_h[:, :, :], x2[:, :, :]).then_inc(z_free, 1)
                    dve.wait_ge(z_free, z_read)
                    dve.tensor_tensor(x2_l[:, :, :], x2[:, :, :], x2_h[:, :, :], ALU.subtract).then_inc(x2_split, 1)

            with dve.Fori(0, NI) as i:
                for slot in range(C):
                    combine(i, slot)
                    cell(i, slot, ga, pa, ca, a_act, a_part, a_cell)
                    state(i, slot, ga, ta, fa, a_hh, a_hl, a_tanh, a_hi, a_h32, a_lo)
                    if slot in MISC[2:] or slot in (6, 8, 12):
                        misc(i, slot)
                    if slot == 0:
                        dve.wait_ge(e_reset, at(i, 6, 0))
                    cell(i, slot, ge, pe_, ce, e_act, e_part, e_cell)
                    state(i, slot, ge, te_, fe, e_hh, e_hl, e_tanh, e_hi, e_h32, e_lo)
                    s = (slot - C0) % C
                    dve.wait_ge(c_hi, at(i, C, slot + 1))
                    dve.wait_ge(c_32, at(i, C, slot + 1))
                    dve.tensor_tensor(c_hl[:, :, s * B:(s + 1) * B], c32[:, :].rearrange("p (k b) -> p k b", b=B),
                                      c_hh[:, :, s * B:(s + 1) * B], ALU.subtract).then_inc(c_lo, 1)
                    if slot == C0 - 1:
                        dve.wait_ge(c_lo, at(i, C, C0))
                        dve.tensor_copy(cc_h[:, :, :], c_hh[:, :, :]).then_inc(cc_copied, 1)
                        dve.tensor_copy(cc_l[:, :, :], c_hl[:, :, :]).then_inc(cc_copied, 1)
                        dve.wait_ge(cc_copied, at(i, 2, 2))
                        for j, hist in enumerate((c_hh, c_hl)):
                            dve.tensor_scalar(rst[:, j, :].rearrange("p (k b) -> p k b", b=B), hist[:, :, CW - B:CW],
                                              keep[:, 0, bass.ds(i, 1)], None, ALU.mult).then_inc(c_reset, 1)
                        dve.wait_ge(c_reset, at(i, 4, 2))
                        for j, hist in enumerate((c_hh, c_hl)):
                            dve.scalar_tensor_tensor(out=hist[:, :, CW - B:CW], in0=h0c[:, j], scalar=keep[:, 1, bass.ds(i, 1)],
                                                     in1=rst[:, j, :].rearrange("p (k b) -> p k b", b=B), op0=ALU.mult,
                                                     op1=ALU.add).then_inc(c_reset, 1)
                    if slot == 15:
                        dve.wait_ge(a_lo, at(i, C, C))
                        dve.wait_ge(e_lo, at(i, C, C))
                        dve.tensor_copy(ac_h[:, :, :], a_hh[:, :, :]).then_inc(ac_copied, 1)
                        dve.tensor_copy(ac_l[:, :, :], a_hl[:, :, :]).then_inc(ac_copied, 1)
                        dve.tensor_tensor(hs1[:, :, bass.ds(i * CW, CW)], e_hh[:, :, :], e_hl[:, :, :],
                                          ALU.add).then_inc(e_reset, 1)
                        for j, hist in enumerate((e_hh, e_hl)):
                            dve.tensor_scalar(rst[:, 2 + j, :].rearrange("p (k b) -> p k b", b=B),
                                              hist[:, :, CW - B:CW], keep[:, 2, bass.ds(i, 1)], None,
                                              ALU.mult).then_inc(e_reset, 1)
                        dve.wait_ge(e_reset, at(i, 6, 3))
                        for j, hist in enumerate((e_hh, e_hl)):
                            dve.scalar_tensor_tensor(out=hist[:, :, CW - B:CW], in0=h0e[:, j],
                                                     scalar=keep[:, 3, bass.ds(i, 1)],
                                                     in1=rst[:, 2 + j, :].rearrange("p (k b) -> p k b", b=B),
                                                     op0=ALU.mult, op1=ALU.add).then_inc(e_reset, 1)
                        dve.tensor_scalar(ce[:, :], ce[:, :], keep[:, 2, bass.ds(i, 1)], None,
                                          ALU.mult).then_inc(e_reset, 1)


BT = T
TT = T // P
HV = D // B
LN_EPS = 1e-5
DK = D // NH


def layernorm(nc, hs1, mean_w, gamma, beta):
    W = 512
    with ExitStack() as ctx:
        def sb(name, shape, dt=F32):
            return ctx.enter_context(nc.sbuf_tensor(name, shape, dt))

        def sem(name):
            return ctx.enter_context(nc.semaphore(name))

        dd, sq, xg = (sb("ln_" + n, [P, KT, W]) for n in ("dd", "sq", "xg"))
        va, root, y, yy, vy, rstd = (sb("ln_" + n, [P, W]) for n in ("va", "root", "y", "yy", "vy", "rstd"))
        first_root = sb("ln_first_root", [P, 1])
        mean = ctx.enter_context(nc.psum_tensor("ln_mean", [P, W], F32))
        var = ctx.enter_context(nc.psum_tensor("ln_var", [P, W], F32))
        mean_pe, var_pe, d_ready, sq_ready, root_ready, steps, kept = (
            sem("ln_" + n) for n in ("mean_pe", "var_pe", "d_ready", "sq_ready", "root_ready", "steps", "kept"))
        NST = 5
        per = [(mean_pe, 1), (var_pe, 1), (d_ready, 1), (sq_ready, 1), (root_ready, 1), (steps, NST), (kept, 4)]
        with nc.Block() as block:
            @block.sync
            def _(sp):
                for s, n in per:
                    sp.sem_inc(s, n)

        with nc.Block() as block:
            @block.tensor
            def _(pe):
                with pe.Fori(0, T * B // W) as j:
                    x = hs1[:, :, bass.ds(j * W + LAG * CW, W)]
                    pe.wait_ge(kept, at(j, 4, 0))
                    for k in range(KT):
                        last = pe.matmul(mean[:, :], mean_w[:, :], x[:, k, :], start=(k == 0), stop=(k == KT - 1))
                    last.then_inc(mean_pe, 1)
                    pe.wait_ge(sq_ready, at(j, 1, 1))
                    for k in range(KT):
                        last = pe.matmul(var[:, :], mean_w[:, :], sq[:, k, :], start=(k == 0), stop=(k == KT - 1))
                    last.then_inc(var_pe, 1)

            @block.scalar
            def _(act):
                act.activation(first_root[:, :], mean_w[:, 0:1], ACT.Sqrt)
                with act.Fori(0, T * B // W) as j:
                    act.wait_ge(d_ready, at(j, 1, 1))
                    act.activation(sq[:, :, :], dd[:, :, :], ACT.Square).then_inc(sq_ready, 1)
                    act.wait_ge(steps, at(j, NST, 1))
                    act.activation(root[:, :], va[:, :], ACT.Sqrt).then_inc(root_ready, 1)

            @block.vector
            def _(dve):
                with dve.Fori(0, T * B // W) as j:
                    x = hs1[:, :, bass.ds(j * W + LAG * CW, W)]
                    dve.wait_ge(mean_pe, at(j, 1, 1))
                    dve.tensor_tensor(dd[:, :, :], x, mean[:, :].unsqueeze(1).to_broadcast([P, KT, W]),
                                      ALU.subtract).then_inc(d_ready, 1)
                    dve.wait_ge(var_pe, at(j, 1, 1))
                    dve.tensor_scalar(va[:, :], var[:, :], 4 * LN_EPS, None, ALU.add).then_inc(steps, 1)
                    dve.wait_ge(root_ready, at(j, 1, 1))
                    dve.reciprocal(y[:, :], root[:, :]).then_inc(steps, 1)
                    dve.wait_ge(steps, at(j, NST, 2))
                    dve.tensor_tensor(yy[:, :], y[:, :], y[:, :], ALU.mult).then_inc(steps, 1)
                    dve.wait_ge(steps, at(j, NST, 3))
                    dve.scalar_tensor_tensor(out=vy[:, :], in0=yy[:, :], scalar=-0.5, in1=va[:, :], op0=ALU.mult,
                                             op1=ALU.mult).then_inc(steps, 1)
                    dve.wait_ge(steps, at(j, NST, 4))
                    dve.scalar_tensor_tensor(out=rstd[:, :], in0=vy[:, :], scalar=1.5, in1=y[:, :], op0=ALU.add,
                                             op1=ALU.mult).then_inc(steps, 1)
                    dve.wait_ge(steps, at(j, NST, 5))
                    for k in range(KT):
                        dve.scalar_tensor_tensor(out=xg[:, k, :], in0=dd[:, k, :], scalar=gamma[:, k:k + 1],
                                                 in1=rstd[:, :], op0=ALU.mult, op1=ALU.mult).then_inc(kept, 1)
                    dve.wait_ge(kept, at(j, 4, 2))
                    for k in range(KT):
                        dve.tensor_scalar(x[:, k, :], xg[:, k, :], beta[:, k:k + 1], None, ALU.add).then_inc(kept, 1)


def attention_two(nc, t, hs1, attd):
    with ExitStack() as ctx:
        def sb(name, shape, dt=F32):
            return ctx.enter_context(nc.sbuf_tensor(name, shape, dt))

        def sem(name):
            return ctx.enter_context(nc.semaphore(name))

        w_hi = {n: sb(n + "2_hi", [P, KT, D], F16) for n in ("q", "k", "v")}
        w_lo = {n: sb(n + "2_lo", [P, KT, D], F16) for n in ("q", "k", "v")}
        brow = sb("brow2", [2, 3 * D], F16)
        ones2 = sb("ones2b", [2, BT], F16)
        mean_w = sb("mean_w", [P, P])
        ident = sb("ident2", [P, P])
        gamma, beta = sb("gamma", [P, KT]), sb("beta", [P, KT])
        xn_h, xn_l = sb("xn_h", [P, KT, BT], F16), sb("xn_l", [P, KT, BT], F16)
        q_h, q_l, k_h, k_l = (sb(n, [P, KT, BT], F16) for n in ("q_h", "q_l", "k_h", "k_l"))
        v_h, v_l = sb("v_h", [P, TT, D], F16), sb("v_l", [P, TT, D], F16)
        first_exp = sb("first_exp", [P, 1])
        nmax = sb("nmax", [P, 2, TT])
        prob = sb("prob", [P, 2, TT, BT])
        sums, rinv = sb("sums", [P, NH, TT]), sb("rinv", [P, NH, TT])
        pt_h, pt_l = sb("pt_h", [P, 2, TT, BT], F16), sb("pt_l", [P, 2, TT, BT], F16)
        att = sb("att2", [P, NH, TT, HV])

        sc = [ctx.enter_context(nc.psum_tensor(f"sc{j}", [P, TT, BT], F32)) for j in range(2)]
        pt = [ctx.enter_context(nc.psum_tensor(f"pt{j}", [P, TT, BT], F32)) for j in range(2)]
        po = ctx.enter_context(nc.psum_tensor("po", [P, NH, TT, HV], F32))

        with ExitStack() as st:
            s_q = st.enter_context(nc.sbuf_tensor("s_q", [P, KT, D], F32))
            s_k = st.enter_context(nc.sbuf_tensor("s_k", [P, KT, D], F32))
            s_v8 = st.enter_context(nc.sbuf_tensor("s_v8", [P, KT, D, 8], F32))
            s_v = st.enter_context(nc.sbuf_tensor("s_v", [P, KT, D], F32))
            s_b8 = st.enter_context(nc.sbuf_tensor("s_b8", [1, D, 8], F32))
            s_b = st.enter_context(nc.sbuf_tensor("s_b2", [1, 3 * D], F32))
            s_bl = st.enter_context(nc.sbuf_tensor("s_b2l", [1, 3 * D], F16))
            loaded, v_sum, hi_done, lo_done, row_sent = (
                st.enter_context(nc.semaphore("at_" + n)) for n in ("loaded", "v_sum", "hi", "lo", "row"))
            jobs = [(s_q[:, :, :], w_hi["q"][:, :, :], w_lo["q"][:, :, :]),
                    (s_k[:, :, :], w_hi["k"][:, :, :], w_lo["k"][:, :, :]),
                    (s_v[:, :, :], w_hi["v"][:, :, :], w_lo["v"][:, :, :]),
                    (s_b[0:1, :], brow[0:1, :], s_bl[0:1, :])]
            kp = "(k p) n -> p k n"
            loads = [(s_q[:, :, :], t["l_wq"].rearrange(kp, p=P)), (s_k[:, :, :], t["l_wk"].rearrange(kp, p=P)),
                     (s_v8[:, :, :, :].rearrange("p k n u -> p k (n u)"), t["l_wv"].rearrange(kp, p=P)),
                     (s_b8[:, :, :].rearrange("a n u -> a (n u)"), t["l_bv"].rearrange("(a n) -> a n", a=1)),
                     (s_b[0:1, 0:D], t["l_bq"].rearrange("(a n) -> a n", a=1)),
                     (s_b[0:1, D:2 * D], t["l_bk"].rearrange("(a n) -> a n", a=1)),
                     (gamma[:, :], t["l_gamma"]), (beta[:, :], t["l_beta"]), (ident[:, :], t["k_ident"])]
            block = st.enter_context(nc.Block())

            @block.sync
            def _(sp):
                for dst, src in loads:
                    sp.dma_start(dst, src).then_inc(loaded, 16)
                sp.wait_ge(lo_done, len(jobs))
                sp.dma_start(brow[1:2, :], s_bl[0:1, :]).then_inc(row_sent, 16)
                sp.wait_ge(row_sent, 16)

            @block.scalar
            def _(act):
                act.wait_ge(loaded, 16 * len(loads))
                act.wait_ge(v_sum, KT + 1)
                for src, hi, _lo in jobs:
                    act.activation(hi, src, ACT.Copy, scale=S).then_inc(hi_done, 1)

            @block.vector
            def _(dve):
                dve.memset(mean_w[:, :], 1.0 / D)
                dve.memset(ones2[:, :], 1.0)
                dve.wait_ge(loaded, 16 * len(loads))
                for k in range(KT):
                    dve.tensor_reduce(s_v[:, k, :], s_v8[:, k, :, :], AX_X, ALU.add).then_inc(v_sum, 1)
                dve.tensor_reduce(s_b[0:1, 2 * D:3 * D], s_b8[0:1, :, :], AX_X, ALU.add).then_inc(v_sum, 1)
                for n, (src, hi, lo) in enumerate(jobs):
                    dve.wait_ge(hi_done, n + 1)
                    dve.scalar_tensor_tensor(out=lo, in0=src, scalar=S, in1=hi, op0=ALU.mult,
                                             op1=ALU.subtract).then_inc(lo_done, 1)

        layernorm(nc, hs1, mean_w, gamma, beta)

        xn_steps, proj_pe = sem("xn_steps"), sem("proj_pe")
        proj_read, qk_split, v_split = sem("proj_read2"), sem("qk_split"), sem("v_split")
        sc_pe, neg_max, exp_done, t_pe, pt_hi, pt_lo, pv_pe = (
            sem(n) for n in ("sc_pe", "neg_max", "exp_done", "t_pe", "pt_hi", "pt_lo", "pv_pe"))
        r_done, att_done, att_sent = sem("r_done"), sem("att_done"), sem("att_sent")
        XN = 2
        per = [(xn_steps, XN), (proj_pe, 3), (proj_read, 3), (qk_split, 2),
               (v_split, 1), (sc_pe, NH), (neg_max, NH), (exp_done, 2 * NH), (t_pe, NH), (pt_hi, NH), (pt_lo, NH),
               (pv_pe, NH), (r_done, 1), (att_done, 1), (att_sent, 16)]
        with nc.Block() as block:
            @block.sync
            def _(sp):
                for s, n in per:
                    sp.sem_inc(s, n)

        block = ctx.enter_context(nc.Block())

        @block.sync
        def _(sp):
            rows = attd[0:B * T * D].rearrange("(b h s p j) -> b p h s j", h=NH, s=TT, p=P, j=HV)
            with sp.Fori(0, B) as b:
                sp.wait_ge(att_done, at(b, 1, 1))
                for s_ in range(TT):
                    sp.dma_start(rows[bass.ds(b, 1), :, :, s_, :].rearrange("o p h j -> (o p) h j"),
                                 att[:, :, s_, :]).then_inc(att_sent, 16)
            sp.wait_ge(att_sent, 16 + 16 * TT * B)

        @block.tensor
        def _(pe):
            def scores(b, h):
                r0, m = DK * (h % 4), h // 4
                if h == 0:
                    pe.wait_ge(qk_split, at(b, 2, 2))
                else:
                    pe.wait_ge(exp_done, at(b, 2 * NH, max(0, 2 * (h - 1))))
                for s_ in range(TT):
                    for q, k in ((q_h, k_h), (q_l, k_h), (q_h, k_l)):
                        last = pe.matmul(sc[h % 2][:, s_, :], q[r0:r0 + DK, m, s_ * P:(s_ + 1) * P],
                                         k[r0:r0 + DK, m, :], start=(s_ == 0 and k is k_h and q is q_h),
                                         stop=(k is k_l), skip_group_check=True, tile_position=(r0, 0))
                last.then_inc(sc_pe, 1)

            def turn(b, h):
                pe.wait_ge(exp_done, at(b, 2 * NH, 2 * (h + 1)))
                if h == 0:
                    pe.wait_ge(v_split, at(b, 1, 1))
                pe.wait_ge(pt_lo, at(b, NH, max(0, h - 1)))
                first = True
                for s_ in range(TT):
                    for u in range(TT):
                        last = pe.matmul(pt[h % 2][:, u, s_ * P:(s_ + 1) * P], prob[:, h % 2, s_, u * P:(u + 1) * P],
                                         ident[:, :], is_transpose=True, start=first, stop=True,
                                         skip_group_check=True)
                        first = False
                last.then_inc(t_pe, 1)

            def values(b, h):
                pe.wait_ge(pt_lo, at(b, NH, h + 1))
                if h == 0:
                    pe.wait_ge(att_done, at(b, 1, 0))
                for s_ in range(TT):
                    o = po[:, h, s_, :]
                    for u in range(TT):
                        for pp, vp in ((pt_h, v_h), (pt_h, v_l), (pt_l, v_h)):
                            last = pe.matmul(o, pp[:, h % 2, u, s_ * P:(s_ + 1) * P], vp[:, u, h * HV:(h + 1) * HV],
                                             start=(h == 0 and s_ == 0 and u == 0 and pp is pt_h and vp is v_h),
                                             stop=(u == TT - 1 and pp is pt_l), skip_group_check=True)
                last.then_inc(pv_pe, 1)

            with pe.Fori(0, B) as b:
                pe.wait_ge(xn_steps, at(b, XN, XN))
                pe.wait_ge(exp_done, at(b, 2 * NH, 0))
                for j, n in enumerate("qk"):
                    for m in range(KT):
                        o = sc[j][:, m, :]
                        pe.matmul(o, brow[0:2, j * D + m * P:j * D + (m + 1) * P], ones2[0:2, :], start=(m == 0),
                                  stop=False, skip_group_check=True)
                        w = (lambda k, n=n, m=m: w_hi[n][:, k, m * P:(m + 1) * P],
                             lambda k, n=n, m=m: w_lo[n][:, k, m * P:(m + 1) * P])
                        last = split_matmul(pe, o, w, (lambda k: xn_h[:, k, :], lambda k: xn_l[:, k, :]), False,
                                            last=True)
                    last.then_inc(proj_pe, 1)
                for u in range(TT):
                    o = pt[0][:, u, :]
                    pe.matmul(o, ones2[0:2, 0:P], brow[0:2, 2 * D:3 * D], start=(u == 0), stop=False,
                              skip_group_check=True)
                    w = (lambda k, u=u: xn_h[:, k, u * P:(u + 1) * P], lambda k, u=u: xn_l[:, k, u * P:(u + 1) * P])
                    last = split_matmul(pe, o, w, (lambda k: w_hi["v"][:, k, :], lambda k: w_lo["v"][:, k, :]), False,
                                        last=True)
                last.then_inc(proj_pe, 1)
                for h in range(NH + 2):
                    if h < NH:
                        scores(b, h)
                    if 1 <= h <= NH:
                        turn(b, h - 1)
                    if h >= 2:
                        values(b, h - 2)

        @block.scalar
        def _(act):
            def flat(a):
                return a.rearrange("p k n -> p (k n)")

            def exps(b, h):
                act.wait_ge(neg_max, at(b, NH, h + 1))
                act.wait_ge(t_pe, at(b, NH, max(0, h - 1)))
                for s_ in range(TT):
                    act.activation(prob[:, h % 2, s_, :], sc[h % 2][:, s_, :], ACT.Exp, bias=nmax[:, h % 2, s_:s_ + 1],
                                   accum_out=sums[:, h, s_:s_ + 1]).then_inc(exp_done, 1)

            def high(b, h):
                act.wait_ge(t_pe, at(b, NH, h + 1))
                act.wait_ge(pv_pe, at(b, NH, max(0, h - 1)))
                act.activation(flat(pt_h[:, h % 2]), flat(pt[h % 2][:, :, :]), ACT.Copy).then_inc(pt_hi, 1)

            act.activation(first_exp[:, :], mean_w[:, 0:1], ACT.Exp)
            with act.Fori(0, B) as b:
                act.wait_ge(proj_pe, at(b, 3, 1))
                act.activation(flat(q_h[:, :, :]), flat(sc[0][:, :, :]), ACT.Copy,
                               scale=float(DK) ** -0.5 / S).then_inc(proj_read, 1)
                act.wait_ge(proj_pe, at(b, 3, 2))
                act.activation(flat(k_h[:, :, :]), flat(sc[1][:, :, :]), ACT.Copy, scale=1.0 / S).then_inc(proj_read, 1)
                act.wait_ge(proj_pe, at(b, 3, 3))
                act.activation(flat(v_h[:, :, :]), flat(pt[0][:, :, :]), ACT.Copy, scale=1.0 / S).then_inc(proj_read, 1)
                for h in range(NH + 1):
                    if h < NH:
                        exps(b, h)
                    if h >= 1:
                        high(b, h - 1)

        @block.vector
        def _(dve):
            hist = hs1[:, :, LAG * CW:(LAG + NCH) * CW].rearrange("p k (t b) -> p k t b", b=B)

            def low(b, h):
                dve.wait_ge(pt_hi, at(b, NH, h + 1))
                dve.tensor_tensor(pt_l[:, h % 2], pt[h % 2][:, :, :], pt_h[:, h % 2], ALU.subtract).then_inc(pt_lo, 1)

            with dve.Fori(0, B) as b:
                row = hist[:, :, :, bass.ds(b, 1)].rearrange("p k t o -> p k (t o)")
                dve.tensor_scalar(xn_h[:, :, :], row, 1.0, None, ALU.mult).then_inc(xn_steps, 1)
                dve.wait_ge(xn_steps, at(b, XN, 1))
                dve.tensor_tensor(xn_l[:, :, :], row, xn_h[:, :, :], ALU.subtract).then_inc(xn_steps, 1)
                for j, (lo, hi, f) in enumerate(((q_l, q_h, float(DK) ** -0.5 / S), (k_l, k_h, 1.0 / S))):
                    dve.wait_ge(proj_read, at(b, 3, j + 1))
                    dve.scalar_tensor_tensor(out=lo[:, :, :], in0=sc[j][:, :, :], scalar=f, in1=hi[:, :, :],
                                             op0=ALU.mult, op1=ALU.subtract).then_inc(qk_split, 1)
                dve.wait_ge(proj_read, at(b, 3, 3))
                dve.scalar_tensor_tensor(out=v_l[:, :, :], in0=pt[0][:, :, :], scalar=1.0 / S, in1=v_h[:, :, :],
                                         op0=ALU.mult, op1=ALU.subtract).then_inc(v_split, 1)
                for h in range(NH + 1):
                    if h < NH:
                        dve.wait_ge(sc_pe, at(b, NH, h + 1))
                        dve.wait_ge(exp_done, at(b, 2 * NH, max(0, 2 * (h - 1))))
                        dve.tensor_reduce(nmax[:, h % 2, :], sc[h % 2][:, :, :], AX_X, ALU.max,
                                          negate=True).then_inc(neg_max, 1)
                    if h >= 1:
                        low(b, h - 1)
                dve.wait_ge(exp_done, at(b, 2 * NH, 2 * NH))
                dve.reciprocal(rinv[:, :, :], sums[:, :, :]).then_inc(r_done, 1)
                dve.wait_ge(r_done, at(b, 1, 1))
                dve.wait_ge(pv_pe, at(b, NH, NH))
                dve.wait_ge(att_sent, (b * TT + 1) * 16)
                dve.tensor_tensor(att[:, :, :, :].rearrange("p h s j -> p (h s) j"),
                                  po[:, :, :, :].rearrange("p h s j -> p (h s) j"),
                                  rinv[:, :, :].rearrange("p h s -> p (h s)").unsqueeze(2)
                                  .to_broadcast([P, NH * TT, HV]), ALU.mult).then_inc(att_done, 1)


E2 = 8
EA = E2 + 1
TOP2 = 4
HF = D * 2 * 4 // 3
HM = 6
M_OFF = [min(m * P, HF - P) for m in range(HM)]
G3 = 3 * D
GRP = 2 * EA
GM = HM // 2
NI3 = NCH + 1
OLAG = 2
SLOT_GROUPS = [[0], [1], [2], [3], [4], [5], [6], [7, 8], [9], [10], [11], [12], [13], [14], [15], [16, 17]]
MISC3 = (0, 3, 6)


def pipeline_two(nc, t, arena, attd, x2d, out):
    with ExitStack() as ctx:
        def sb(name, shape, dt=F32):
            return ctx.enter_context(nc.sbuf_tensor(name, shape, dt))

        def sem(name):
            return ctx.enter_context(nc.semaphore(name))

        m12_h, m12_l = sb("m12_h", [P, 2, KT, EA, HF], F16), sb("m12_l", [P, 2, KT, EA, HF], F16)
        m3_h, m3_l = sb("m3_h", [P, EA, HM, D], F16), sb("m3_l", [P, EA, HM, D], F16)
        gx_w = [sb(f"gx_w{p}", [P, KT, G3], F16) for p in range(2)]
        gu_w = [sb(f"gu_w{p}", [P, KT, G3], F16) for p in range(2)]
        wg = [sb(f"wg{p}", [P, KT, E2], F16) for p in range(2)]
        vt_h, vt_l = sb("vt_h", [P, 6, B], F16), sb("vt_l", [P, 6, B], F16)
        rrow = sb("rrow", [2, E2], F16)
        ones2 = sb("ones2c", [2, P], F16)
        ident = sb("ident3", [P, P])
        ident_h = sb("ident_h", [P, P], F16)
        iota = sb("iota3", [P, E2, TOP2])
        k2 = "(k p) n -> p k n"

        with ExitStack() as st:
            s_x = st.enter_context(nc.sbuf_tensor("s_x", [P, KT, G3], F32))
            s_u = st.enter_context(nc.sbuf_tensor("s_u", [P, KT, G3], F32))
            s_c = arena[:, 0, 0:KT * G3].rearrange("p (k n) -> p k n", k=KT)
            s_row = st.enter_context(nc.sbuf_tensor("s_row", [1, G3 + E2], F32))
            s_rl = st.enter_context(nc.sbuf_tensor("s_rl", [1, E2], F16))
            s_wg = st.enter_context(nc.sbuf_tensor("s_wg", [P, KT, E2], F32))
            s_cond = st.enter_context(nc.sbuf_tensor("s_cond3", [P, KT, B], F32))
            s_one = st.enter_context(nc.sbuf_tensor("s_one", [1, B], F32))
            vps = st.enter_context(nc.psum_tensor("vps", [P, 6, B], F32))
            loaded, ready, vt_pe, vt_read, cast, low, low_m, row_sent = (
                st.enter_context(nc.semaphore("g_" + n)) for n in
                ("loaded", "ready", "vt_pe", "vt_read", "cast", "low", "low_m", "row_sent"))
            staged = [st.enter_context(nc.semaphore(f"staged{j}")) for j in range(2)]
            stage = [arena[:, j, 0:E2 * D] for j in range(2)]
            work = []
            for m in range(2):
                for k in range(KT):
                    for e in range(0, EA, 3):
                        src = t[("m_w1", "m_w2")[m]][k * P:(k + 1) * P, e:e + 3, :]
                        work.append((src, (3, HF), m12_h[:, m, k, e:e + 3, 0:HF], m12_l[:, m, k, e:e + 3, 0:HF],
                                     S / 2))
            for m in range(HM):
                for e in range(0, EA, 8):
                    n = min(8, EA - e)
                    src = t["m_w3"][m * P:(m + 1) * P, e:e + n, :]
                    work.append((src, (n, D), m3_h[:, e:e + n, m, :], m3_l[:, e:e + n, m, :], S))

            def staged_at(n):
                _src, (a, b), _hi, _lo, _f = work[n]
                return stage[n % 2][:, 0:a * b].rearrange("p (a b) -> p a b", b=b)

            smalls = [(s_x[:, :, :], gx_w[0][:, :, :], gx_w[1][:, :, :], S),
                      (s_u[:, :, 0:2 * D], gu_w[0][:, :, 0:2 * D], gu_w[1][:, :, 0:2 * D], S / 2),
                      (s_u[:, :, 2 * D:G3], gu_w[0][:, :, 2 * D:G3], gu_w[1][:, :, 2 * D:G3], S / 4),
                      (s_wg[:, :, :], wg[0][:, :, :], wg[1][:, :, :], S / 2),
                      (s_row[0:1, G3:G3 + E2], rrow[0:1, :], s_rl[0:1, :], S),
                      (ident[:, :], ident_h[:, :], None, 1.0)]
            row = "(a n) -> a n"
            loads = [(s_c[:, :, g * D:(g + 1) * D], t["g_c" + n].rearrange(k2, p=P)) for g, n in enumerate("zrh")]
            loads += [(s_x[:, :, g * D:(g + 1) * D], t["g_w" + n].rearrange(k2, p=P)) for g, n in enumerate("zrh")]
            loads += [(s_u[:, :, g * D:(g + 1) * D], t["g_u" + n].rearrange(k2, p=P)) for g, n in enumerate("zrh")]
            loads += [(s_row[0:1, g * D:(g + 1) * D], t["g_b" + n].rearrange(row, a=1)) for g, n in enumerate("zrh")]
            loads += [(s_row[0:1, G3:G3 + E2], t["m_rb"].rearrange(row, a=1)), (s_wg[:, :, :], t["m_wg"].rearrange(k2, p=P)),
                      (s_cond[:, :, :], t["cond"].rearrange("(k p) b -> p k b", p=P)), (ident[:, :], t["k_ident"]),
                      (iota[:, :, :].rearrange("p e j -> p (e j)"), t["k_iota4"])]
            block = st.enter_context(nc.Block())

            @block.sync
            def _(sp):
                for dst, src in loads:
                    sp.dma_start(dst, src).then_inc(loaded, 16)
                sp.wait_ge(vt_pe, 1)
                for n, (src, *_rest) in enumerate(work):
                    if n >= 2:
                        sp.wait_ge(cast, len(smalls) + n - 1)
                        sp.wait_ge(low_m, n - 1)
                    sp.dma_start(staged_at(n), src).then_inc(staged[n % 2], 16)
                sp.wait_ge(low, 5)
                sp.dma_start(rrow[1:2, :], s_rl[0:1, :]).then_inc(row_sent, 16)
                sp.wait_ge(row_sent, 16)

            @block.gpsimd
            def _(pool):
                pool.memset(s_one[0:1, :], 1.0).then_inc(ready, 1)
                pool.memset(ones2[:, :], 1.0).then_inc(ready, 1)

            @block.tensor
            def _(pe):
                pe.wait_ge(loaded, 16 * len(loads))
                pe.wait_ge(ready, 2)
                for m in range(6):
                    pe.matmul(vps[:, m, :], s_row[0:1, m * P:(m + 1) * P], s_one[0:1, :], start=(m == 0), stop=False,
                              skip_group_check=True)
                    for k in range(KT):
                        last = pe.matmul(vps[:, m, :], s_c[:, k, m * P:(m + 1) * P], s_cond[:, k, :], start=False,
                                         stop=(k == KT - 1), skip_group_check=True)
                last.then_inc(vt_pe, 1)

            @block.scalar
            def _(act):
                act.wait_ge(loaded, 16 * len(loads))
                for src, hi, _lo, f in smalls:
                    act.activation(hi, src, ACT.Copy, scale=f).then_inc(cast, 1)
                for n, (_src, _shape, hi, _lo, f) in enumerate(work):
                    act.wait_ge(staged[n % 2], 16 * (n // 2 + 1))
                    act.activation(hi, staged_at(n), ACT.Copy, scale=f).then_inc(cast, 1)

            @block.vector
            def _(dve):
                for n, (src, hi, lo, f) in enumerate(smalls[:5]):
                    dve.wait_ge(cast, n + 1)
                    dve.scalar_tensor_tensor(out=lo, in0=src, scalar=f, in1=hi, op0=ALU.mult,
                                             op1=ALU.subtract).then_inc(low, 1)
                dve.wait_ge(vt_pe, 1)
                dve.tensor_scalar(vt_h[:, :, :], vps[:, :, :], S, None, ALU.mult).then_inc(vt_read, 1)
                dve.wait_ge(vt_read, 1)
                dve.scalar_tensor_tensor(out=vt_l[:, :, :], in0=vps[:, :, :], scalar=S, in1=vt_h[:, :, :],
                                         op0=ALU.mult, op1=ALU.subtract).then_inc(vt_read, 1)
                for n, (_src, _shape, hi, lo, f) in enumerate(work):
                    dve.wait_ge(cast, len(smalls) + n + 1)
                    dve.scalar_tensor_tensor(out=lo, in0=staged_at(n), scalar=f, in1=hi, op0=ALU.mult,
                                             op1=ALU.subtract).then_inc(low_m, 1)

        x3 = arena[:, :, 0:(NCH + OLAG + 2) * CW]
        def tile(name, dt=F16):
            return sb(name, [P, KT, CW], dt)
        g_hh, g_hl = tile("g_hh"), tile("g_hl")
        hc_h, hc_l = tile("hc_h"), tile("hc_l")
        gx_h, gx_l = tile("gx_h"), tile("gx_l")
        attr = sb("attr", [P, D])
        x2r = tile("x2r", F32)
        outc = tile("outc", F32)
        zr = sb("zr", [P, 32])
        cand = sb("cand", [P, 16])
        h32 = sb("h32", [P, 16])
        rh32 = sb("rh32", [P, 16])
        rh_h, rh_l = sb("rh_h", [P, KT, B], F16), sb("rh_l", [P, KT, B], F16)
        zc, zm = sb("zc", [P, 16]), sb("zm", [P, 16])
        th = sb("th", [P, 2, GM * CW])
        uu = sb("uu", [P, GM * CW])
        a32 = sb("a32", [P, 2, GM * CW])
        a_h, a_l = sb("a_h", [P, 2, GM * CW], F16), sb("a_l", [P, 2, GM * CW], F16)
        acc = sb("acc3", [P, D])
        lg = sb("lg3", [P, E2])
        m8 = sb("m83", [P, 8])
        i8 = sb("i83", [P, 8], U32)
        idf = sb("idf3", [P, TOP2])
        eq = sb("eq", [P, E2, TOP2])
        rt = sb("rt3", [P, 4, E2])
        sm = sb("sm3", [P, 3])
        wts = sb("wts3", [P, EA])

        g_b = [ctx.enter_context(nc.psum_tensor(f"g_b{h}", [P, 8, 6, B], F32)) for h in range(2)]
        p1 = [ctx.enter_context(nc.psum_tensor(f"p1{h}", [P, 512], F32)) for h in range(2)]
        p2 = [ctx.enter_context(nc.psum_tensor(f"p2{h}", [P, 512], F32)) for h in range(2)]
        po = ctx.enter_context(nc.psum_tensor("po3", [P, D], F32))
        z = ctx.enter_context(nc.psum_tensor("z3", [P, 512], F32))

        zr_pe, zr_act, u_pe, u_act = (sem(n) for n in ("zr_pe", "zr_act", "u_pe", "u_act"))
        rh_hi, rh_32, rh_lo, z_parts, z_mix, h_new, h_hi, h_lo = (
            sem(n) for n in ("rh_hi", "rh_32", "rh_lo", "z_parts", "z_mix", "h_new", "h_hi3", "h_lo3"))
        hid_pe, th_act, u_done, a_done, a_hi, a_lo, w3_pe, po_free = (
            sem(n) for n in ("hid_pe", "th_act", "u_done", "a_done", "a_hi3", "a_lo3", "w3_pe", "po_free"))
        z_full, gate_read = sem("z_full3"), sem("gate_read")
        hc_copied, route, x3_done, x3_split, out_done = (
            sem(n) for n in ("hc_copied", "route3", "x3_done", "x3_split", "out_done"))
        exp_done = sem("exp3")
        rows_in, out_sent = sem("rows_in"), sem("out_sent")
        RIN = 16 * (B + 1)
        NR = 10
        per = [(zr_pe, 16), (zr_act, 16), (u_pe, 16), (u_act, 16), (rh_hi, 16), (rh_32, 16), (rh_lo, 16),
               (z_parts, 16), (z_mix, 16), (h_new, 16), (h_hi, 16), (h_lo, 16), (hid_pe, GRP), (th_act, GRP), (u_done, GRP),
               (a_done, GRP), (a_hi, GRP), (a_lo, GRP), (w3_pe, GRP), (po_free, EA), (z_full, 3), (gate_read, 1),
               (hc_copied, 2), (route, NR), (x3_done, 1), (x3_split, 2), (out_done, 1), (exp_done, 1),
               (rows_in, RIN), (out_sent, 16)]

        def project_half(pe, half):
            first = True
            for m in range(6):
                o = g_b[half][:, :, m, :]
                for v in (vt_h, vt_l):
                    pe.matmul(o, ident_h[:, :], v[:, m, :].unsqueeze(1).to_broadcast([P, 8, B]), start=first,
                              stop=False, skip_group_check=True)
                    first = False
                w = (lambda k, m=m: gx_w[0][:, k, m * P:(m + 1) * P], lambda k, m=m: gx_w[1][:, k, m * P:(m + 1) * P])
                r = slice(half * HALF, (half + 1) * HALF)
                last = split_matmul(pe, o, w, (lambda k: gx_h[:, k, r], lambda k: gx_l[:, k, r]), False)
            return last

        def load_rows(sp, c, done):
            for b in range(B):
                sp.dma_start(attr[b * C:(b + 1) * C, :],
                             attd[bass.ds(c * (C * D) + b * T * D, C * D)].rearrange("(t d) -> t d", d=D))\
                    .then_inc(done, 16)
            sp.dma_start(x2r[:, :, :], x2d[:, :, bass.ds(c * CW, CW)]).then_inc(done, 16)

        def turn_rows(pe):
            for k in range(KT):
                last = pe.matmul(z[:, k * P:(k + 1) * P], attr[:, k * P:(k + 1) * P], ident[:, :], is_transpose=True,
                                 start=(k == 0), stop=True, skip_group_check=True)
            return last

        def add_rows(dve, dst):
            return dve.tensor_tensor(dst.rearrange("p k (t b) -> p k t b", b=B),
                                     z[:, 0:D].rearrange("p (k b t) -> p k t b", k=KT, b=B),
                                     x2r[:, :, :].rearrange("p k (t b) -> p k t b", b=B), ALU.add)

        with ExitStack() as st:
            cleared, hid_zero, pad_sent, x_in, x_tr, x_out, x_first = (
                st.enter_context(nc.semaphore("f_" + n)) for n in
                ("cleared", "hid_zero", "pad_sent", "x_in", "x_tr", "x_out", "x_first"))
            block = st.enter_context(nc.Block())

            @block.gpsimd
            def _(pool):
                for tl in (g_hh, g_hl, hc_l):
                    pool.memset(tl[:, :, :], 0.0)
                pool.memset(hc_h[:, :, :], 0.0).then_inc(hid_zero, 1)
                pool.memset(x3[:, :, 0:OLAG * CW], 0.0)
                for tl in (a_h, a_l, th):
                    pool.memset(tl[:, :, :], 0.0)
                pool.memset(h32[:, :], 0.0)
                pool.memset(acc[:, :], 0.0).then_inc(cleared, 1)
                pool.memset(wts[:, 0:E2], 0.0)
                pool.memset(wts[:, E2:EA], 1.0 / S)

            @block.sync
            def _(sp):
                load_rows(sp, 0, x_in)
                sp.wait_ge(cleared, 1)
                sp.dma_start(attd[B * T * D:(B * T + 2 * C) * D].rearrange("(r d) -> r d", d=D),
                             acc[0:2 * C, :]).then_inc(pad_sent, 16)
                sp.wait_ge(pad_sent, 16)
                for s, n in per:
                    sp.sem_inc(s, n)

            @block.tensor
            def _(pe):
                pe.wait_ge(x_in, 16 * (B + 1))
                turn_rows(pe).then_inc(x_tr, 1)
                pe.wait_ge(x_first, 2)
                project_half(pe, 0)
                pe.wait_ge(hid_zero, 1)
                for bank in (*p1, *p2):
                    for j in range(GM):
                        pe.matmul(bank[:, j * CW:(j + 1) * CW], gx_w[0][:, 0, 0:P], hc_h[:, 0, :], start=(j == 0),
                                  stop=True, skip_group_check=True)
                for k in range(KT):
                    pe.matmul(po[:, k * CW:(k + 1) * CW], gx_w[0][:, 0, 0:P], hc_h[:, 0, :], start=(k == 0),
                              stop=True, skip_group_check=True)

            @block.vector
            def _(dve):
                dve.wait_ge(x_in, 16 * (B + 1))
                dve.wait_ge(x_tr, 1)
                c0 = x3[:, :, OLAG * CW:(OLAG + 1) * CW]
                add_rows(dve, c0).then_inc(x_out, 1)
                dve.wait_ge(x_out, 1)
                dve.tensor_copy(gx_h[:, :, :], c0).then_inc(x_first, 1)
                dve.wait_ge(x_first, 1)
                dve.tensor_tensor(gx_l[:, :, :], c0, gx_h[:, :, :], ALU.subtract).then_inc(x_first, 1)

        block = ctx.enter_context(nc.Block())

        @block.sync
        def _(sp):
            with sp.Fori(0, NI3) as i:
                sp.wait_ge(x3_done, at(i, 1, 0))
                load_rows(sp, i + 1, rows_in)
                sp.wait_ge(out_done, at(i, 1, 1))
                sp.dma_start(out[:, :, bass.ds(i * CW, CW)], outc[:, :, :]).then_inc(out_sent, 16)
            sp.wait_ge(out_done, at(NI3, 1, 1))
            sp.dma_start(out[:, :, NI3 * CW:(NI3 + 1) * CW], outc[:, :, :]).then_inc(out_sent, 16)
            sp.wait_ge(out_sent, 16 + 16 * (NI3 + 1))

        def before(slot):
            return [(g, (g + 2) % GRP) for g in SLOT_GROUPS[(slot - 1) % C]]

        @block.tensor
        def _(pe):
            def zr_gates(i, slot):
                prev = (slot - 1) % C * B
                o = g_b[slot // 8]
                pe.wait_ge(h_hi, at(i, C, slot))
                for m in range(4):
                    for k in range(KT):
                        for w in gu_w:
                            pe.matmul(o[:, slot % 8, m, :], w[:, k, m * P:(m + 1) * P], g_hh[:, k, prev:prev + B],
                                      start=False, stop=False, skip_group_check=True)
                pe.wait_ge(h_lo, at(i, C, slot))
                for m in range(4):
                    for k in range(KT):
                        last = pe.matmul(o[:, slot % 8, m, :], gu_w[0][:, k, m * P:(m + 1) * P],
                                         g_hl[:, k, prev:prev + B], start=False, stop=(k == KT - 1),
                                         skip_group_check=True)
                last.then_inc(zr_pe, 1)

            def candidate(i, slot):
                o = g_b[slot // 8]
                pe.wait_ge(rh_hi, at(i, C, slot + 1))
                for m in (4, 5):
                    for k in range(KT):
                        for w in gu_w:
                            pe.matmul(o[:, slot % 8, m, :], w[:, k, m * P:(m + 1) * P], rh_h[:, k, :],
                                      start=False, stop=False, skip_group_check=True)
                pe.wait_ge(rh_lo, at(i, C, slot + 1))
                for m in (4, 5):
                    for k in range(KT):
                        last = pe.matmul(o[:, slot % 8, m, :], gu_w[0][:, k, m * P:(m + 1) * P], rh_l[:, k, :],
                                         start=False, stop=(k == KT - 1), skip_group_check=True)
                last.then_inc(u_pe, 1)

            def hidden(i, g):
                e = g // 2
                pe.wait_ge(a_done, at(i, GRP, g + 1))
                for mat, bank in enumerate((p1[g % 2], p2[g % 2])):
                    for j in range(GM):
                        c = M_OFF[g % 2 * GM + j]
                        w = (lambda k: m12_h[:, mat, k, e, c:c + P], lambda k: m12_l[:, mat, k, e, c:c + P])
                        last = split_matmul(pe, bank[:, j * CW:(j + 1) * CW], w,
                                            (lambda k: hc_h[:, k, :], lambda k: hc_l[:, k, :]), j == 0, last=True)
                last.then_inc(hid_pe, 1)

            def down(i, k):
                g = (k - 2) % GRP
                e = g // 2
                pe.wait_ge(a_hi, at(i, GRP, k + 1))
                pe.wait_ge(a_lo, at(i, GRP, k + 1))
                if g % 2 == 0:
                    pe.wait_ge(po_free, at(i, EA, k // 2 + 1))
                for j in range(GM):
                    m = g % 2 * GM + j
                    r = slice(j * CW, (j + 1) * CW)
                    for x, w in ((a_h, m3_h), (a_h, m3_l), (a_l, m3_h)):
                        last = pe.matmul(po[:, :], x[:, g % 2, r], w[:, e, m, :],
                                         start=(m == 0 and x is a_h and w is m3_h), stop=(m == HM - 1 and x is a_l),
                                         skip_group_check=True)
                last.then_inc(w3_pe, 1)

            def misc(i, slot):
                if slot == 0:
                    pe.wait_ge(hc_copied, at(i, 2, 0))
                    pe.wait_ge(x3_done, at(i, 1, 0))
                    pe.matmul(z[:, 0:E2], ones2[0:2, :], rrow[0:2, :], start=True, stop=False, skip_group_check=True)
                    last = split_matmul(pe, z[:, 0:E2], (lambda k: hc_h[:, k, :], lambda k: hc_l[:, k, :]),
                                        (lambda k: wg[0][:, k, :], lambda k: wg[1][:, k, :]), False, last=True)
                elif slot == 3:
                    pe.wait_ge(po_free, at(i, EA, 2))
                    if isinstance(i, int):
                        pe.wait_ge(x3_done, at(i, 1, 0))
                    else:
                        pe.wait_ge(gate_read, at(i, 1, 1))
                    for k in range(KT):
                        last = pe.matmul(z[:, k * P:(k + 1) * P], acc[:, k * P:(k + 1) * P], ident[:, :],
                                         is_transpose=True, start=(k == 0), stop=True, skip_group_check=True)
                else:
                    pe.wait_ge(rows_in, at(i, RIN, RIN))
                    pe.wait_ge(out_done, at(i, 1, 1))
                    last = turn_rows(pe)
                last.then_inc(z_full, 1)

            with pe.Fori(0, NI3) as i:
                for slot in range(C):
                    zr_gates(i, slot)
                    if slot == 2:
                        pe.wait_ge(u_act, at(i, C, 0))
                        project_half(pe, 1)
                    if slot == 12:
                        pe.wait_ge(x3_split, at(i, 2, 2))
                        pe.wait_ge(u_act, at(i, C, 8))
                        project_half(pe, 0)
                    if slot in MISC3:
                        misc(i, slot)
                    for n, k in enumerate(SLOT_GROUPS[slot]):
                        hidden(i, k)
                        if n == 0:
                            candidate(i, slot)
                        down(i, k)
            down(NI3, 0)
            down(NI3, 1)
            misc(NI3, 3)

        @block.scalar
        def _(act):
            def high(i, slot):
                for g, n in before(slot):
                    act.wait_ge(a_done, at(i, GRP, n + 1))
                    act.wait_ge(w3_pe, at(i, GRP, n - 1))
                    act.activation(a_h[:, g % 2, :], a32[:, g % 2, :], ACT.Copy).then_inc(a_hi, 1)

            act.activation(cand[:, 0:1], wts[:, 0:1], ACT.Exp)
            with act.Fori(0, NI3) as i:
                for slot in range(C):
                    bank = g_b[slot // 8]
                    act.wait_ge(zr_pe, at(i, C, slot + 1))
                    act.activation(zr[:, :], bank[:, slot % 8, 0:4].rearrange("p m b -> p (m b)"), ACT.Tanh,
                                   scale=0.5 / S).then_inc(zr_act, 1)
                    high(i, slot)
                    act.wait_ge(u_pe, at(i, C, slot + 1))
                    act.activation(cand[:, :], bank[:, slot % 8, 4:6].rearrange("p m b -> p (m b)"), ACT.Tanh,
                                   scale=1.0 / S).then_inc(u_act, 1)
                    for k in SLOT_GROUPS[slot]:
                        act.wait_ge(hid_pe, at(i, GRP, k + 1))
                        act.wait_ge(u_done, at(i, GRP, k + 1))
                        act.activation(th[:, k % 2, :], p1[k % 2][:, 0:GM * CW], ACT.Tanh,
                                       scale=0.5 / S).then_inc(th_act, 1)
                    if slot == 1:
                        act.wait_ge(route, at(i, NR, 2))
                        act.activation(rt[:, 1, :], rt[:, 0, :], ACT.Exp).then_inc(exp_done, 1)
            high(NI3, 0)

        @block.gpsimd
        def _(pool):
            def low(i, slot):
                for g, n in before(slot):
                    pool.wait_ge(a_hi, at(i, GRP, n + 1))
                    pool.tensor_tensor(a_l[:, g % 2, :], a32[:, g % 2, :], a_h[:, g % 2, :],
                                       ALU.subtract).then_inc(a_lo, 1)

            with pool.Fori(0, NI3) as i:
                for slot in range(C):
                    low(i, slot)
            low(NI3, 0)

        @block.vector
        def _(dve):
            def swiglu(i, slot):
                for g, n in before(slot):
                    dve.wait_ge(th_act, at(i, GRP, n - 1))
                    dve.wait_ge(a_done, at(i, GRP, n))
                    dve.scalar_tensor_tensor(out=uu[:, :], in0=th[:, g % 2, :], scalar=1.0,
                                             in1=p1[g % 2][:, 0:GM * CW], op0=ALU.add, op1=ALU.mult).then_inc(u_done, 1)
                    dve.wait_ge(u_done, at(i, GRP, n + 1))
                    dve.wait_ge(a_lo, at(i, GRP, n - 1))
                    dve.scalar_tensor_tensor(out=a32[:, g % 2, :], in0=uu[:, :], scalar=0.5 / S / S,
                                             in1=p2[g % 2][:, 0:GM * CW], op0=ALU.mult, op1=ALU.mult).then_inc(a_done, 1)

            def add_expert(i, slot):
                for k, _n in before(slot):
                    if k % 2 == 0:
                        continue
                    e = (k - 2) % GRP // 2
                    dve.wait_ge(w3_pe, at(i, GRP, k + 1 - (GRP if slot == 0 else 0)))
                    dve.wait_ge(po_free, at(i, EA, (k // 2 + 1) % EA))
                    if e == 0:
                        dve.wait_ge(route, at(i, NR, NR))
                        dve.tensor_scalar(acc[:, :], po[:, :], wts[:, 0:1], None, ALU.mult).then_inc(po_free, 1)
                    else:
                        dve.scalar_tensor_tensor(out=acc[:, :], in0=po[:, :], scalar=wts[:, e:e + 1], in1=acc[:, :],
                                                 op0=ALU.mult, op1=ALU.add).then_inc(po_free, 1)

            def misc(i, slot):
                if slot == 0:
                    dve.wait_ge(z_full, at(i, 3, 1))
                    dve.tensor_scalar(lg[:, :], z[:, 0:E2], 1.0 / S, None, ALU.mult).then_inc(gate_read, 1)
                elif slot == 1:
                    dve.max(m8[:, :], lg[:, :]).then_inc(route, 1)
                    dve.wait_ge(route, at(i, NR, 1))
                    dve.tensor_tensor(rt[:, 0, :], lg[:, :], m8[:, 0:1].to_broadcast([P, E2]),
                                      ALU.subtract).then_inc(route, 1)
                    dve.max_index(i8[:, :], m8[:, :], lg[:, :]).then_inc(route, 1)
                    dve.wait_ge(route, at(i, NR, 3))
                    dve.tensor_copy(idf[:, :], i8[:, 0:TOP2]).then_inc(route, 1)
                elif slot == 2:
                    dve.wait_ge(route, at(i, NR, 4))
                    dve.tensor_tensor(eq[:, :, :], iota[:, :, :], idf[:, :].unsqueeze(1).to_broadcast([P, E2, TOP2]),
                                      ALU.is_equal).then_inc(route, 1)
                    dve.wait_ge(route, at(i, NR, 5))
                    dve.tensor_reduce(rt[:, 2, :], eq[:, :, :], AX_X, ALU.add).then_inc(route, 1)
                    dve.wait_ge(route, at(i, NR, 6))
                    dve.wait_ge(exp_done, at(i, 1, 1))
                    dve.tensor_tensor(rt[:, 3, :], rt[:, 1, :], rt[:, 2, :], ALU.mult).then_inc(route, 1)
                    dve.wait_ge(route, at(i, NR, 7))
                    dve.tensor_reduce(sm[:, 0:1], rt[:, 3, :], AX_X, ALU.add).then_inc(route, 1)
                    dve.wait_ge(route, at(i, NR, 8))
                    dve.reciprocal(sm[:, 1:2], sm[:, 0:1]).then_inc(route, 1)
                    dve.wait_ge(route, at(i, NR, 9))
                    dve.tensor_scalar(wts[:, 0:E2], rt[:, 3, :], sm[:, 1:2], 1.0 / S, ALU.mult,
                                      ALU.mult).then_inc(route, 1)
                elif slot == 3:
                    dve.wait_ge(z_full, at(i, 3, 1 if isinstance(i, int) else 2))
                    dve.wait_ge(out_sent, at(i, 16, 0))
                    x = x3[:, :, i * CW:(i + 1) * CW] if isinstance(i, int) else x3[:, :, bass.ds(i * CW, CW)]
                    dve.tensor_tensor(outc[:, :, :], z[:, 0:D].rearrange("p (k n) -> p k n", n=CW), x,
                                      ALU.add).then_inc(out_done, 1)
                elif slot == 6:
                    dve.wait_ge(z_full, at(i, 3, 3))
                    x = x3[:, :, bass.ds((i + (OLAG + 1)) * CW, CW)]
                    add_rows(dve, x).then_inc(x3_done, 1)
                    dve.wait_ge(x3_done, at(i, 1, 1))
                    dve.tensor_scalar(gx_h[:, :, :], x, 1.0, None, ALU.mult).then_inc(x3_split, 1)
                    dve.wait_ge(x3_split, at(i, 2, 1))
                    dve.tensor_tensor(gx_l[:, :, :], x, gx_h[:, :, :], ALU.subtract).then_inc(x3_split, 1)

            kb = "p (k b) -> p k b"
            with dve.Fori(0, NI3) as i:
                for slot in range(C):
                    swiglu(i, slot)
                    add_expert(i, slot)
                    dve.wait_ge(zr_act, at(i, C, slot + 1))
                    dve.wait_ge(h_new, at(i, C, slot))
                    r3, h3 = zr[:, 16:32].rearrange(kb, b=B), h32[:, :].rearrange(kb, b=B)
                    dve.scalar_tensor_tensor(out=rh_h[:, :, :], in0=r3, scalar=1.0, in1=h3, op0=ALU.add,
                                             op1=ALU.mult).then_inc(rh_hi, 1)
                    dve.scalar_tensor_tensor(out=rh32[:, :].rearrange(kb, b=B), in0=r3, scalar=1.0, in1=h3,
                                             op0=ALU.add, op1=ALU.mult).then_inc(rh_32, 1)
                    dve.wait_ge(rh_hi, at(i, C, slot + 1))
                    dve.wait_ge(rh_32, at(i, C, slot + 1))
                    dve.tensor_tensor(rh_l[:, :, :], rh32[:, :].rearrange(kb, b=B), rh_h[:, :, :],
                                      ALU.subtract).then_inc(rh_lo, 1)
                    if slot == 0:
                        misc(i, slot)
                        dve.wait_ge(gate_read, at(i, 1, 1))
                    dve.scalar_tensor_tensor(out=zc[:, :], in0=zr[:, 0:16], scalar=1.0, in1=h32[:, :],
                                             op0=ALU.subtract, op1=ALU.mult).then_inc(z_parts, 1)
                    if slot in (1, 2, 3, 6):
                        misc(i, slot)
                    dve.wait_ge(u_act, at(i, C, slot + 1))
                    dve.scalar_tensor_tensor(out=zm[:, :], in0=zr[:, 0:16], scalar=1.0, in1=cand[:, :], op0=ALU.add,
                                             op1=ALU.mult).then_inc(z_mix, 1)
                    dve.wait_ge(z_mix, at(i, C, slot + 1))
                    dve.wait_ge(z_parts, at(i, C, slot + 1))
                    rr = slice(slot * B, (slot + 1) * B)
                    dve.scalar_tensor_tensor(out=g_hh[:, :, rr], in0=zc[:, :].rearrange(kb, b=B), scalar=-0.5,
                                             in1=zm[:, :].rearrange(kb, b=B), op0=ALU.mult, op1=ALU.add).then_inc(h_hi, 1)
                    dve.scalar_tensor_tensor(out=h32[:, :], in0=zc[:, :], scalar=-0.5, in1=zm[:, :], op0=ALU.mult,
                                             op1=ALU.add).then_inc(h_new, 1)
                    dve.wait_ge(h_hi, at(i, C, slot + 1))
                    dve.wait_ge(h_new, at(i, C, slot + 1))
                    dve.tensor_tensor(g_hl[:, :, rr], h32[:, :].rearrange(kb, b=B), g_hh[:, :, rr],
                                      ALU.subtract).then_inc(h_lo, 1)
                    if slot == C - 1:
                        dve.wait_ge(h_lo, at(i, C, C))
                        dve.wait_ge(hid_pe, at(i, GRP, GRP))
                        dve.tensor_copy(hc_h[:, :, :], g_hh[:, :, :]).then_inc(hc_copied, 1)
                        dve.tensor_copy(hc_l[:, :, :], g_hl[:, :, :]).then_inc(hc_copied, 1)
            swiglu(NI3, 0)
            add_expert(NI3, 0)
            add_expert(NI3, 2)
            misc(NI3, 3)


def build_kernel(nc, t, out):
    x2d = nc.dram_tensor("x2_dram", (P, KT, (NCH + 2) * CW), F32).ap()
    attd = nc.dram_tensor("attention_dram", ((B * T + 2 * C) * D,), F32).ap()
    with nc.sbuf_tensor("hs1", [P, KT, NI * CW], F32) as hs1:
        with nc.sbuf_tensor("xs", [P, KT, (NCH + 2 * LAG + 1) * CW], F32) as xs:
            pipeline_one(nc, t, xs, hs1)
            with nc.semaphore("x2_sent") as x2_sent, nc.Block() as block:
                @block.sync
                def _(sp):
                    sp.dma_start(x2d, xs[:, :, LAG * CW:(LAG + NCH + 2) * CW]).then_inc(x2_sent, 16)
                    sp.wait_ge(x2_sent, 16)
        attention_two(nc, t, hs1, attd)
        pipeline_two(nc, t, hs1, attd, x2d, out)


def _layout(d):
    f = np.float32
    head = np.arange(P) // 16
    th = np.pi / 2 * np.arange(1, B + 1) / B
    tr = lambda a: np.ascontiguousarray(np.transpose(a))
    hidden = lambda r, s: np.ascontiguousarray(np.concatenate([d[r], d[s][None]]).transpose(2, 0, 1))
    down = np.concatenate([d["L1_ffn_W3"], d["L1_ffn_Ws3"][None]]).transpose(2, 0, 1)
    cut = (HM - 1) * P
    return {
        "x": np.ascontiguousarray(np.transpose(d["x"], (2, 1, 0)).reshape(D, T * B)),
        "cond": tr(d["cond_1024"]),
        "a_wx": d["L0_cond_Wx"], "a_wh": d["L0_cond_Wh"], "a_b": d["L0_cond_b"],
        "e_wx": d["L1_cond_Wx"], "e_wh": d["L1_cond_Wh"], "e_b": d["L1_cond_b"],
        "wq": tr(d["L0_attn_Wq"]), "wk": tr(d["L0_attn_Wk"]), "wv": tr(d["L0_attn_Wv"]), "wo": tr(d["L0_attn_Wo"]),
        "c_wx": d["L0_cond2_Wx"], "c_wh": d["L0_cond2_Wh"], "c_b": d["L0_cond2_b"],
        "f_wm": d["L0_ffn_Wm"], "f_bm": d["L0_ffn_bm"], "f_emb": d["L0_ffn_expert_emb"],
        "f_w1": d["L0_ffn_W1"], "f_b1": tr(d["L0_ffn_b1"]), "f_w2": d["L0_ffn_W2"],
        "f_b2": d["L0_ffn_b2"].reshape(-1), "f_wo": d["L0_ffn_Wo"], "f_bo": d["L0_ffn_bo"],
        "g_cz": d["L1_cond2_C_z"], "g_cr": d["L1_cond2_C_r"], "g_ch": d["L1_cond2_C"],
        "g_wz": d["L1_cond2_W_z"], "g_wr": d["L1_cond2_W_r"], "g_wh": d["L1_cond2_W"],
        "g_uz": d["L1_cond2_U_z"], "g_ur": d["L1_cond2_U_r"], "g_uh": d["L1_cond2_U"],
        "g_bz": d["L1_cond2_b_z"], "g_br": d["L1_cond2_b_r"], "g_bh": d["L1_cond2_b"],
        "m_wg": tr(d["L1_ffn_Wg"]), "m_rb": d["L1_ffn_routing_bias"],
        "m_w1": hidden("L1_ffn_W1", "L1_ffn_Ws1"), "m_w2": hidden("L1_ffn_W2", "L1_ffn_Ws2"),
        "m_w3": np.concatenate([down[:cut], np.zeros((HM * P - HF, EA, D), f), down[cut:]]),
        "k_iota4": np.tile(np.repeat(np.arange(E2), TOP2)[None], (P, 1)).astype(f),
        "l_wq": d["L1_attn_Wq"], "l_wk": d["L1_attn_Wk"], "l_wv": d["L1_attn_Wv"], "l_bq": d["L1_attn_bq"],
        "l_bk": d["L1_attn_bk"], "l_bv": d["L1_attn_bv"],
        "l_gamma": tr(d["L1_attn_gamma"].reshape(KT, P)), "l_beta": tr(d["L1_attn_beta"].reshape(KT, P)),
        "k_ident": np.eye(P, dtype=f), "k_gsum": (head[:, None] == head[None]).astype(f),
        "k_wcos": np.tile(np.cos(th[:, None] - th[None]).reshape(1, -1), (P, 1)).astype(f),
        "k_iota": np.tile(np.arange(E1)[None], (P, 1)).astype(f),
    }


def kernel(**inputs):
    import concourse.bacc as _bacc
    from concourse.bass_utils import run_bass_kernel_spmd as _run

    nc = _bacc.Bacc("TRN2", target_bir_lowering=False, num_devices=1)
    arrays = {"in_" + k: np.ascontiguousarray(v)
              for k, v in _layout({k: np.asarray(v) for k, v in inputs.items()}).items()}
    t = {k[3:]: nc.dram_tensor(k, v.shape, mybir.dt.from_np(v.dtype), kind="ExternalInput").ap()
         for k, v in arrays.items()}
    out = nc.dram_tensor("out_dram", (P, KT, (NCH + OLAG) * CW), F32, kind="ExternalOutput").ap()
    build_kernel(nc, t, out)
    r = _run(nc, [arrays], core_ids=[0]).results[0]["out_dram"]
    r = r[:, :, OLAG * CW:].transpose(1, 0, 2).reshape(D, T, B)
    return np.ascontiguousarray(r.transpose(2, 1, 0))
```

```python
from contextlib import ExitStack

import numpy as np

import concourse.bass as bass
from concourse import mybir

F32 = mybir.dt.float32
F16 = mybir.dt.float16
U32 = mybir.dt.uint32
ALU = mybir.AluOpType
ACT = mybir.ActivationFunctionType
AX_X = mybir.AxisListType.X

P = 128
B = 8
T = 256
D = 256
KT = D // P
C = 16
CW = C * B
HALF = CW // 2
NCH = T // C
LAG = 4
NI = NCH + LAG
S = 64.0
G4 = 4 * D
HD = 32
NH = D // HD
E1 = 16
EPS_Z = 1e-6
E2 = 8
EA = E2 + 1
TOP2 = 4
HF = D * 2 * 4 // 3
HM = 6

C0 = 9
W1_0 = 11
MISC = (0, 1, 2, 3, 4, 5, 7, 9, 11, 12, 13, 14)


def z_use(slot, second):
    return slot + sum(1 for m in MISC if m < slot) + (1 if second and slot in MISC else 0)


Z_USES = z_use(C, False)


def at(i, per, k):
    return (i + 1) * per + k


def split_matmul(pe, out, w, x, start, last=False):
    ins = None
    for k in range(KT):
        for wp, xp in ((0, 0), (1, 0), (0, 1)):
            ins = pe.matmul(out, w[wp](k), x[xp](k), start=start, stop=last and k == KT - 1 and xp == 1,
                            skip_group_check=True)
            start = False
    return ins


def pipeline_one(nc, t, xs, hs1, x2d):
    with ExitStack() as ctx:
        def sb(name, shape, dt=F32):
            return ctx.enter_context(nc.sbuf_tensor(name, shape, dt))

        def sem(name):
            return ctx.enter_context(nc.semaphore(name))

        names = (("a_wx", G4), ("a_wh", G4), ("e_wx", G4), ("e_wh", G4), ("wq", D), ("wk", D), ("wv", D), ("wo", D),
                 ("c_wx", D), ("c_wh", D), ("f_wm", D), ("f_wo", D))
        w_hi = {n: sb(n + "_hi", [P, KT, w], F16) for n, w in names}
        w_lo = {n: sb(n + "_lo", [P, KT, w], F16) for n, w in names}
        b2_hi, b2_lo = sb("b2_hi", [P, D], F16), sb("b2_lo", [P, D], F16)
        w1s = sb("w1s", [P, E1, P], F16)
        es = sb("es", [P, E1], F16)
        w2_hi = sb("w2_hi", [P, E1, HD], F16)
        w2_lo = sb("w2_lo", [P, E1, HD], F16)
        b1 = sb("b1", [P, E1])
        NB = {"a_b": (0, G4), "e_b": (G4, G4), "c_b": (2 * G4, D), "f_bo": (2 * G4 + D, D),
              "f_bm": (2 * G4 + 2 * D, D)}
        BR = 2 * G4 + 3 * D
        brow = sb("brow", [2, BR], F16)
        ones2 = sb("ones2", [2, CW], F16)
        ident = sb("ident", [P, P])
        gsum = sb("gsum", [P, P])
        wcos = sb("wcos", [P, B * B])
        iota = sb("iota", [P, E1])
        keep = sb("keep", [P, 4, NI])
        h0c = sb("h0c", [P, 2, KT, B], F16)
        h0e = sb("h0e", [P, 2, KT, B], F16)
        a_hh = sb("a_hh", [P, KT, CW], F16)
        a_hl = sb("a_hl", [P, KT, CW], F16)
        e_hh = sb("e_hh", [P, KT, CW], F16)
        e_hl = sb("e_hl", [P, KT, CW], F16)
        c_hh = sb("c_hh", [P, KT, CW], F16)
        c_hl = sb("c_hl", [P, KT, CW], F16)
        ga, ge = sb("ga", [P, 64]), sb("ge", [P, 64])
        pa, pe_ = sb("pa", [P, 2, 16]), sb("pe_", [P, 2, 16])
        ca, ce = sb("ca", [P, 16]), sb("ce", [P, 16])
        ta, te_ = sb("ta", [P, 16]), sb("te_", [P, 16])
        fa, fe = sb("fa", [P, 16]), sb("fe", [P, 16])
        c32 = sb("c32", [P, 16])
        rst = sb("rst", [P, 4, 16], F16)
        rstc = sb("rstc", [P, 16])
        def tile(name, dt=F16):
            return sb(name, [P, KT, CW], dt)
        x_h, x_l = tile("x_h"), tile("x_l")
        ac_h, ac_l = tile("ac_h"), tile("ac_l")
        cc_h, cc_l = tile("cc_h"), tile("cc_l")
        x1, x1_h, x1_l = tile("x1", F32), tile("x1_h"), tile("x1_l")
        x2, x2_h, x2_l = tile("x2", F32), tile("x2_h"), tile("x2_l")
        qk = sb("qk", [P, 2, KT, CW])
        vv = tile("vv", F32)
        prod = sb("prod", [P, 4, 512])
        sw = sb("sw", [P, 2, 512])
        sv = sb("sv", [P, 2, 512])
        den, num = tile("den", F32), tile("num", F32)
        dmx, rcd, att = tile("dmx", F32), tile("rcd", F32), tile("att", F32)
        at_h, at_l = tile("at_h"), tile("at_l")
        tk_h, tk_l = tile("tk_h"), tile("tk_l")
        tnew = sb("tnew", [P, NH * CW], F16)
        tst = sb("tst", [P, NH * CW], F16)
        lg = sb("lg", [P, NH, E1])
        m8 = sb("m8", [P, NH, 8])
        i8 = sb("i8", [P, NH, 8], U32)
        idf = sb("idf", [P, NH, 2])
        rt = sb("rt", [P, 8, NH, E1])
        sm = sb("sm", [P, 2, NH])
        wts = sb("wts", [P, NH, E1])
        hm32 = sb("hm32", [P, 2, NH * CW])
        hm_h = sb("hm_h", [P, 2, NH * CW], F16)
        hm_l = sb("hm_l", [P, 2, NH * CW], F16)
        tmp = sb("tmp", [P, 2, NH, HD])
        acc = sb("acc", [P, D])
        om_h, om_l = tile("om_h"), tile("om_l")
        wt_h, wt_l = sb("wt_h", [P, P], F16), sb("wt_l", [P, P], F16)

        g_a = [ctx.enter_context(nc.psum_tensor(f"g_a{h}", [P, 8, 8, B], F32)) for h in range(2)]
        g_e = [ctx.enter_context(nc.psum_tensor(f"g_e{h}", [P, 8, 8, B], F32)) for h in range(2)]
        g_c = ctx.enter_context(nc.psum_tensor("g_c", [P, C, KT, B], F32))
        xy = [ctx.enter_context(nc.psum_tensor(f"xy{h}", [P, 512], F32)) for h in range(2)]
        z = ctx.enter_context(nc.psum_tensor("z", [P, 512], F32))

        def wh(n, m):
            return (lambda k: w_hi[n][:, k, m * P:(m + 1) * P], lambda k: w_lo[n][:, k, m * P:(m + 1) * P])

        def cols(hi, lo, a, b):
            return (lambda k: hi[:, k, a:b], lambda k: lo[:, k, a:b])

        def bias(n, m):
            o = NB[n][0] + m * P
            return brow[0:2, o:o + P]

        with ExitStack() as st:
            def stage(name, shape):
                return st.enter_context(nc.sbuf_tensor("st_" + name, shape, F32))
            s_w = {"a_wx": hs1[:, :, 0:G4], "a_wh": hs1[:, :, G4:2 * G4], "wq": hs1[:, :, 2 * G4:2 * G4 + D],
                   "wk": hs1[:, :, 2 * G4 + D:2 * G4 + 2 * D], "e_wx": xs[:, :, 0:G4], "e_wh": xs[:, :, G4:2 * G4]}
            free = {"wv": prod[:, 0], "wo": prod[:, 1], "c_wx": sw[:, 0], "c_wh": sv[:, 0], "f_wm": prod[:, 2],
                    "f_wo": rt[:, 0:4].rearrange("p a h e -> p (a h e)")}
            s_w |= {n: ap.rearrange("p (k n) -> p k n", k=KT) for n, ap in free.items()}
            s_b2 = rt[:, 4:6].rearrange("p a h e -> p (a h e)")
            s_w1 = hm32[:, :, :].rearrange("p a (e i) -> p (a e) i", i=P)
            s_es = stage("es", [P, E1])
            s_w2 = prod[:, 3].rearrange("p (e d) -> p e d", d=HD)
            s_b = stage("b", [1, BR])
            s_bl = st.enter_context(nc.sbuf_tensor("st_bl", [1, BR], F16))
            s_cond = stage("cond", [P, KT, B])
            s_c2 = stage("c2", [P, KT, B])
            loaded = st.enter_context(nc.semaphore("loaded"))
            loaded_const = st.enter_context(nc.semaphore("loaded_const"))
            loaded_x = st.enter_context(nc.semaphore("loaded_x"))
            xs_cleared = st.enter_context(nc.semaphore("xs_cleared"))
            hi_done = st.enter_context(nc.semaphore("hi_done"))
            lo_done = st.enter_context(nc.semaphore("lo_done"))
            row_done = st.enter_context(nc.semaphore("row_done"))
            row_sent = st.enter_context(nc.semaphore("row_sent"))
            cleared = st.enter_context(nc.semaphore("cleared"))
            keep_set = st.enter_context(nc.semaphore("keep_set"))
            cond_2 = st.enter_context(nc.semaphore("cond_2"))
            gates = ("a_wx", "a_wh", "e_wx", "e_wh")

            def jobs():
                for n, w in names:
                    if n in gates:
                        f = S if n.endswith("wx") else S / 2
                        yield s_w[n][:, :, 0:3 * D], w_hi[n][:, :, 0:3 * D], w_lo[n][:, :, 0:3 * D], f
                        yield s_w[n][:, :, 3 * D:G4], w_hi[n][:, :, 3 * D:G4], w_lo[n][:, :, 3 * D:G4], 2 * f
                    else:
                        f = S / 2 if n in ("wq", "wk", "wv") else S
                        yield s_w[n][:, :, :], w_hi[n][:, :, :], w_lo[n][:, :, :], f
                yield s_b2, b2_hi[:, :], b2_lo[:, :], S
                yield s_w2, w2_hi[:, :, :], w2_lo[:, :, :], S
                yield s_w1, w1s[:, :, :], None, S
                yield s_es[:, :], es[:, :], None, S
                yield s_cond[:, :, :], h0c[:, 0], h0c[:, 1], 1.0
                yield s_cond[:, :, :], h0e[:, 0], h0e[:, 1], 2.0

            def bias_jobs():
                for n in ("a_b", "e_b"):
                    o = NB[n][0]
                    yield o, o + 3 * D, S
                    yield o + 3 * D, o + G4, 2 * S
                yield 2 * G4, BR, S

            NJ = len(list(jobs()))
            loads = [(s_w[n], t[n].rearrange("(k p) n -> p k n", p=P)) for n, _ in names]
            loads += [(s_b2, t["f_b2"])]
            loads += [(s_w1[r * HD:(r + 1) * HD, :, :], t["f_w1"].rearrange("e d i -> d e i")) for r in range(4)]
            loads += [(s_es[r * HD:(r + 1) * HD, :], t["f_emb"]) for r in range(4)]
            loads += [(s_w2, t["f_w2"].rearrange("e i o -> i e o")), (b1[:, :], t["f_b1"]),
                      (s_cond[:, :, :], t["cond"].rearrange("(k p) b -> p k b", p=P))]
            for n, (o, w) in NB.items():
                loads.append((s_b[0:1, o:o + w], t[n].rearrange("(a n) -> a n", a=1)))
            consts = [(ident[:, :], t["k_ident"]), (gsum[:, :], t["k_gsum"]), (wcos[:, :], t["k_wcos"]),
                      (iota[:, :], t["k_iota"])]

            block = st.enter_context(nc.Block())

            @block.sync
            def _(sp):
                for dst, src in loads[0::2]:
                    sp.dma_start(dst, src).then_inc(loaded, 16)
                for dst, src in consts:
                    sp.dma_start(dst, src).then_inc(loaded_const, 16)
                sp.wait_ge(row_done, 5)
                sp.dma_start(brow[1:2, :], s_bl[0:1, :]).then_inc(row_sent, 16)
                sp.wait_ge(row_sent, 16)
                sp.wait_ge(loaded_const, 16 * len(consts))

            @block.scalar
            def _(act):
                for dst, src in loads[1::2]:
                    act.dma_start(dst, src).then_inc(loaded, 16)
                act.wait_ge(loaded, 16 * len(loads))
                for src, hi, _lo, f in jobs():
                    act.activation(hi, src, ACT.Copy, scale=f).then_inc(hi_done, 1)
                for a, b, f in bias_jobs():
                    act.activation(brow[0:1, a:b], s_b[0:1, a:b], ACT.Copy, scale=f).then_inc(hi_done, 1)

            @block.vector
            def _(dve):
                for tl in (a_hl, c_hl, e_hl, a_hh, c_hh, e_hh, x2_h, x2_l, x1_h, x1_l, cc_h, cc_l):
                    dve.memset(tl[:, :, :], 0.0).then_inc(cleared, 1)
                for tl in (ca, ce, acc):
                    dve.memset(tl[:, :], 0.0).then_inc(cleared, 1)
                dve.memset(ones2[:, :], 1.0).then_inc(cleared, 1)
                dve.memset(keep[:, 0:3:2, :], 1.0).then_inc(keep_set, 1)
                dve.memset(keep[:, 1:4:2, :], 0.0).then_inc(keep_set, 1)
                dve.wait_ge(keep_set, 2)
                for row, it in ((0, 1), (2, LAG - 1)):
                    dve.memset(keep[:, row, it:it + 1], 0.0).then_inc(keep_set, 1)
                    dve.memset(keep[:, row + 1, it:it + 1], 1.0).then_inc(keep_set, 1)
                for n, (src, hi, lo, f) in enumerate(jobs()):
                    dve.wait_ge(hi_done, n + 1)
                    if lo is not None:
                        dve.scalar_tensor_tensor(out=lo, in0=src, scalar=f, in1=hi, op0=ALU.mult,
                                                 op1=ALU.subtract).then_inc(lo_done, 1)
                    else:
                        for a in (HD, 3 * HD):
                            dve.scalar_tensor_tensor(out=hi[a:a + HD], in0=src[a:a + HD], scalar=f,
                                                     in1=hi[a:a + HD], op0=ALU.mult,
                                                     op1=ALU.subtract).then_inc(lo_done, 1)
                for n, (a, b, f) in enumerate(bias_jobs()):
                    dve.wait_ge(hi_done, NJ + n + 1)
                    dve.scalar_tensor_tensor(out=s_bl[0:1, a:b], in0=s_b[0:1, a:b], scalar=f, in1=brow[0:1, a:b],
                                             op0=ALU.mult, op1=ALU.subtract).then_inc(row_done, 1)
                dve.wait_ge(lo_done, NJ + 2)
                dve.wait_ge(cleared, 22)
                dve.tensor_copy(a_hh[:, :, CW - B:CW], h0e[:, 0]).then_inc(lo_done, 1)
                dve.tensor_copy(a_hl[:, :, CW - B:CW], h0e[:, 1]).then_inc(lo_done, 1)

            @block.gpsimd
            def _(pool):
                for tl in (hm_h, hm_l):
                    pool.memset(tl[:, :, :], 0.0).then_inc(cleared, 1)
                pool.memset(tst[:, :], 0.0).then_inc(cleared, 1)
                pool.memset(wts[:, :, :], 0.0).then_inc(cleared, 1)
                pool.memset(ac_h[:, :, :], 0.0).then_inc(cleared, 1)
                pool.memset(ac_l[:, :, :], 0.0).then_inc(cleared, 1)
                pool.wait_ge(lo_done, 8)
                pool.wait_ge(lo_done, NJ + 2)
                pool.memset(hm32[:, :, :], 0.0).then_inc(cleared, 1)
                pool.memset(xs[:, :, :], 0.0).then_inc(xs_cleared, 1)
                pool.wait_ge(xs_cleared, 1)
                pool.dma_start(xs[:, :, LAG * CW:(LAG + NCH) * CW],
                               t["x"].rearrange("(k p) n -> p k n", p=P)).then_inc(loaded_x, 16)
                pool.wait_ge(loaded_x, 16)

        a_pe, a_act, a_part, a_cell, a_tanh = (sem("a_" + n) for n in ("pe", "act", "part", "cell", "tanh"))
        e_pe, e_act, e_part, e_cell, e_tanh = (sem("e_" + n) for n in ("pe", "act", "part", "cell", "tanh"))
        a_hi, a_h32, a_lo = (sem("a_" + n) for n in ("hi", "h32", "lo"))
        e_hi, e_h32, e_lo = (sem("e_" + n) for n in ("hi", "h32", "lo"))
        c_pe, c_hi, c_32, c_lo = (sem("c_" + n) for n in ("pe", "hi", "32", "lo"))
        x_split, ac_copied, cc_copied, c_reset, e_reset = (
            sem(n) for n in ("x_split", "ac_copied", "cc_copied", "c_reset", "e_reset"))
        z_full, z_free, xy_full = sem("z_full"), sem("z_free"), sem("xy_full")
        g_hi, g_32, g_lo = sem("g_hi"), sem("g_32"), sem("g_lo")
        acc_done = sem("acc_done")
        prod_done, s_read, b_fin, x1_done, x1_split, x1_kept = (
            sem(n) for n in ("prod_done", "s_read", "b_fin", "x1_done", "x1_split", "x1_kept"))
        tk_split, tokens_in, t_copied, route, route_t, wt_split = (
            sem(n) for n in ("tk_split", "tokens_in", "t_copied", "route", "route_t", "wt_split"))
        TIN = 16 * 16
        om_split, x2_done, x2_split, x2_sent = (sem(n) for n in ("om_split", "x2_done", "x2_split", "x2_sent"))
        ROUTE = 2 * NH + 12
        CHOSEN = 2 * NH + 2
        per = [(a_pe, 16), (a_act, 16), (a_part, 32), (a_cell, 16), (a_tanh, 16), (a_hi, 16), (a_h32, 16), (a_lo, 16),
               (e_pe, 16), (e_act, 16), (e_part, 32), (e_cell, 16), (e_tanh, 16), (e_hi, 16), (e_h32, 16), (e_lo, 16),
               (c_pe, 16), (c_hi, 16), (c_32, 16), (c_lo, 16), (x_split, 2), (ac_copied, 2), (cc_copied, 2),
               (c_reset, 4), (e_reset, 6), (z_full, Z_USES), (z_free, Z_USES - 1), (xy_full, 31), (g_hi, 32),
               (g_32, 32), (g_lo, 32), (acc_done, 16), (prod_done, 4), (s_read, 20),
               (b_fin, 3), (x1_done, 1), (x1_split, 1), (x1_kept, 1), (tk_split, 1), (tokens_in, TIN), (t_copied, 1), (wt_split, 1),
               (route, ROUTE), (route_t, 1), (om_split, 1), (x2_done, 1), (x2_split, 1), (x2_sent, 16)]

        def project_half(pe, name, bank, half, xh, xl):
            first = True
            for m in range(8):
                out = bank[half][:, :, m, :]
                pe.matmul(out, bias(name + "_b", m), ones2[0:2, 0:HALF], start=first, stop=False,
                          skip_group_check=True)
                first = False
                last = split_matmul(pe, out, wh(name + "_wx", m), cols(xh, xl, half * HALF, (half + 1) * HALF), False)
            return last

        def project_c(pe):
            for m in range(KT):
                pe.matmul(g_c[:, :, m, :], bias("c_b", m), ones2[0:2, 0:CW], start=(m == 0), stop=False,
                          skip_group_check=True)
                last = split_matmul(pe, g_c[:, :, m, :], wh("c_wx", m), cols(x1_h, x1_l, 0, CW), False)
            return last

        with ExitStack() as st:
            pad_sent = st.enter_context(nc.semaphore("pad_sent1"))
            x_first = st.enter_context(nc.semaphore("x_first"))
            primed = st.enter_context(nc.semaphore("primed"))
            block = st.enter_context(nc.Block())

            @block.vector
            def _(dve):
                first = xs[:, :, LAG * CW:(LAG + 1) * CW]
                dve.tensor_copy(x_h[:, :, :], first).then_inc(x_first, 1)
                dve.wait_ge(x_first, 1)
                dve.tensor_tensor(x_l[:, :, :], first, x_h[:, :, :], ALU.subtract).then_inc(x_first, 1)

            @block.tensor
            def _(pe):
                pe.wait_ge(x_first, 2)
                project_half(pe, "a", g_a, 0, x_h, x_l)
                project_half(pe, "e", g_e, 0, x2_h, x2_l)
                project_c(pe)
                for h in range(2):
                    pe.matmul(xy[h][:, :], w1s[:, 0, :], tst[:, 0:512], start=True, stop=True)
                pe.matmul(z[:, :], w1s[:, 0, :], tst[:, 0:512], start=True, stop=True).then_inc(primed, 1)

            @block.sync
            def _(sp):
                for s, n in per:
                    sp.sem_inc(s, n)
                sp.dma_start(x2d[:, :, NI * CW:(NI + 1) * CW], xs[:, :, 0:CW]).then_inc(pad_sent, 16)
                sp.wait_ge(pad_sent, 16)

        block = ctx.enter_context(nc.Block())

        @block.sync
        def _(sp):
            with sp.Fori(0, NI) as i:
                sp.wait_ge(z_free, at(i, Z_USES, z_use(9, False) + 1))
                for r, part in enumerate((tk_h, tk_h, tk_l, tk_l)):
                    for q in range(P // HD):
                        dst = tnew[r * HD:(r + 1) * HD, :].rearrange("p (k q n) -> p k q n", k=KT, n=CW)[:, :, q, :]
                        sp.dma_start(dst, part[q * HD:(q + 1) * HD, :, :]).then_inc(tokens_in, 16)
                sp.wait_ge(x2_done, at(i, 1, 1))
                sp.dma_start(x2d[:, :, bass.ds(i * CW, CW)], x2[:, :, :]).then_inc(x2_sent, 16)
            sp.wait_ge(x2_sent, 16 * (NI + 1))

        @block.tensor
        def _(pe):
            def lstm_step(i, slot, name, bank, hh, hl, hi_sem, lo_sem, done):
                prev = (slot - 1) % C * B
                out = bank[slot // 8]
                pe.wait_ge(hi_sem, at(i, C, slot))
                for m in range(8):
                    for k in range(KT):
                        for wt in (w_hi, w_lo):
                            pe.matmul(out[:, slot % 8, m, :], wt[name][:, k, m * P:(m + 1) * P],
                                      hh[:, k, prev:prev + B], start=False, stop=False, skip_group_check=True)
                pe.wait_ge(lo_sem, at(i, C, slot))
                for m in range(8):
                    for k in range(KT):
                        last = pe.matmul(out[:, slot % 8, m, :], w_hi[name][:, k, m * P:(m + 1) * P],
                                         hl[:, k, prev:prev + B], start=False, stop=(k == KT - 1),
                                         skip_group_check=True)
                last.then_inc(done, 1)

            def rnn_step(i, slot):
                s = (slot - C0) % C
                prev = (s - 1) % C * B
                pe.wait_ge(c_hi, at(i, C, slot))
                pe.wait_ge(c_32, at(i, C, slot))
                for m in range(KT):
                    for k in range(KT):
                        for wt in (w_hi, w_lo):
                            pe.matmul(g_c[:, s, m, :], wt["c_wh"][:, k, m * P:(m + 1) * P],
                                      c_hh[:, k, prev:prev + B], start=False, stop=False, skip_group_check=True)
                pe.wait_ge(c_lo, at(i, C, slot))
                for m in range(KT):
                    for k in range(KT):
                        last = pe.matmul(g_c[:, s, m, :], w_hi["c_wh"][:, k, m * P:(m + 1) * P],
                                         c_hl[:, k, prev:prev + B], start=False, stop=(k == KT - 1),
                                         skip_group_check=True)
                last.then_inc(c_pe, 1)

            def misc(i, slot):
                if slot == 0:
                    pe.wait_ge(ac_copied, at(i, 2, 0))
                pe_z = at(i, Z_USES, z_use(slot, False))
                if slot in (0, 1):
                    pe.wait_ge(z_free, pe_z)
                    for j, n in enumerate(("wq", "wk") if slot == 0 else ("wv",)):
                        for m in range(KT):
                            o = (2 * j + m) * P
                            last = split_matmul(pe, z[:, o:o + P], wh(n, m), cols(ac_h, ac_l, 0, CW),
                                                start=(o == 0), last=True)
                elif 2 <= slot <= 5:
                    pe.wait_ge(prod_done, at(i, 4, slot - 1))
                    pe.wait_ge(z_free, pe_z)
                    last = pe.matmul(z[:, :], gsum[:, :], prod[:, slot - 2, :], start=True, stop=True)
                elif slot == 7:
                    pe.wait_ge(b_fin, at(i, 3, 3))
                    pe.wait_ge(z_free, pe_z)
                    for m in range(KT):
                        last = split_matmul(pe, z[:, m * P:(m + 1) * P], wh("wo", m), cols(at_h, at_l, 0, CW),
                                            start=(m == 0), last=True)
                elif slot == 9:
                    pe.wait_ge(cc_copied, at(i, 2, 2))
                    pe.wait_ge(z_free, pe_z)
                    for m in range(KT):
                        o = z[:, m * P:(m + 1) * P]
                        pe.matmul(o, bias("f_bm", m), ones2[0:2, :], start=(m == 0), stop=False,
                                  skip_group_check=True)
                        last = split_matmul(pe, o, wh("f_wm", m), cols(cc_h, cc_l, 0, CW), False, last=True)
                elif slot == 11:
                    pe.wait_ge(tokens_in, at(i, TIN, TIN))
                    pe.wait_ge(z_free, pe_z)
                    for h in range(NH):
                        last = pe.matmul(z[:, h * E1:(h + 1) * E1], tnew[:, h * CW:(h + 1) * CW], es[:, :],
                                         start=(h == 0), stop=True, skip_group_check=True)
                elif slot == 12:
                    pe.wait_ge(route, at(i, ROUTE, 0))
                    pe.wait_ge(z_free, pe_z)
                    last = pe.matmul(z[:, 0:P], wts[:, :, :].rearrange("p h e -> p (h e)"), ident[:, :],
                                     is_transpose=True, start=True, stop=True, skip_group_check=True)
                elif slot == 13:
                    pe.wait_ge(acc_done, at(i, E1, 14))
                    pe.wait_ge(z_free, pe_z)
                    for m in range(KT):
                        pe.matmul(z[:, m * P:(m + 1) * P], acc[:, m * P:(m + 1) * P], ident[:, :],
                                  is_transpose=True, start=(m == 0), stop=False, skip_group_check=True)
                    for m in range(KT):
                        for b2, wt in ((b2_hi, wt_h), (b2_lo, wt_h), (b2_hi, wt_l)):
                            last = pe.matmul(z[:, m * P:(m + 1) * P], b2[:, m * P:(m + 1) * P], wt[:, :],
                                             start=False, stop=(wt is wt_l), skip_group_check=True)
                elif slot == 14:
                    pe.wait_ge(om_split, at(i, 1, 1))
                    pe.wait_ge(z_free, pe_z)
                    for m in range(KT):
                        o = z[:, m * P:(m + 1) * P]
                        pe.matmul(o, bias("f_bo", m), ones2[0:2, :], start=(m == 0), stop=False,
                                  skip_group_check=True)
                        last = split_matmul(pe, o, wh("f_wo", m), cols(om_h, om_l, 0, CW), False, last=True)
                last.then_inc(z_full, 1)

            def w1(i, slot, h):
                e = (slot - W1_0) % E1
                if slot == W1_0 and h == 0:
                    pe.wait_ge(t_copied, at(i, 1, 1))
                pe.wait_ge(g_hi, at(i, 32, 2 * slot + 1 + h))
                pe.wait_ge(g_32, at(i, 32, 2 * slot + 1 + h))
                pe.matmul(xy[h][:, :], w1s[:, e, :], tst[:, h * 512:(h + 1) * 512], start=True,
                          stop=True).then_inc(xy_full, 1)

            def w2(i, slot):
                e = (slot - W1_0 - 2) % E1
                b = (slot - 1) % 2
                pe.wait_ge(g_lo, at(i, 32, 2 * slot))
                pe.wait_ge(z_free, at(i, Z_USES, z_use(slot, True)))
                for h in range(NH):
                    o = z[:, h * HD:(h + 1) * HD]
                    hh = hm_h[:, b, h * CW:(h + 1) * CW]
                    pe.matmul(o, hh, w2_hi[:, e, :], start=(h == 0), stop=False, skip_group_check=True)
                    pe.matmul(o, hh, w2_lo[:, e, :], start=False, stop=False, skip_group_check=True)
                    last = pe.matmul(o, hm_l[:, b, h * CW:(h + 1) * CW], w2_hi[:, e, :], start=False, stop=True,
                                     skip_group_check=True)
                last.then_inc(z_full, 1)

            with pe.Fori(0, NI) as i:
                for slot in range(C):
                    lstm_step(i, slot, "a_wh", g_a, a_hh, a_hl, a_hi, a_lo, a_pe)
                    w1(i, slot - 1, 1)
                    if slot == 2:
                        pe.wait_ge(a_act, at(i, C, 0))
                        project_half(pe, "a", g_a, 1, x_h, x_l)
                    if slot == 10:
                        pe.wait_ge(x_split, at(i, 2, 2))
                        pe.wait_ge(a_act, at(i, C, 8))
                        project_half(pe, "a", g_a, 0, x_h, x_l)
                    if slot in MISC:
                        misc(i, slot)
                    if slot == 0:
                        pe.wait_ge(e_reset, at(i, 6, 0))
                    lstm_step(i, slot, "e_wh", g_e, e_hh, e_hl, e_hi, e_lo, e_pe)
                    if slot == 4:
                        pe.wait_ge(e_act, at(i, C, 0))
                        project_half(pe, "e", g_e, 1, x2_h, x2_l)
                    if slot == 15:
                        pe.wait_ge(x2_split, at(i, 1, 1))
                        pe.wait_ge(e_act, at(i, C, 8))
                        project_half(pe, "e", g_e, 0, x2_h, x2_l)
                    if slot == C0:
                        pe.wait_ge(c_reset, at(i, 4, 4))
                    rnn_step(i, slot)
                    if slot == C0 - 1:
                        pe.wait_ge(x1_split, at(i, 1, 1))
                        pe.wait_ge(c_hi, at(i, C, C0))
                        pe.wait_ge(c_32, at(i, C, C0))
                        project_c(pe)
                    w1(i, slot, 0)
                    w2(i, slot)

        @block.scalar
        def _(act):
            def gates(i, slot, bank, g, mm, done):
                act.wait_ge(mm, at(i, C, slot + 1))
                act.activation(g[:, :], bank[slot // 8][:, slot % 8].rearrange("p m b -> p (m b)"), ACT.Tanh,
                               scale=1.0 / (2 * S)).then_inc(done, 1)

            def cell_tanh(i, slot, c, tc, cell, done):
                act.wait_ge(cell, at(i, C, slot + 1))
                act.activation(tc[:, :], c[:, :], ACT.Tanh, scale=0.5).then_inc(done, 1)

            def gelu(i, slot, h, hi):
                e = (slot - W1_0 - 1) % E1
                b = slot % 2
                dst = hm_h if hi else hm32
                if hi:
                    act.wait_ge(xy_full, at(i, 32, 2 * slot - 1 + h))
                    if h == 0:
                        act.wait_ge(z_full, at(i, Z_USES, z_use(slot, False)))
                act.activation(dst[:, b, h * 512:(h + 1) * 512], xy[h][:, :], ACT.Gelu, bias=b1[:, e:e + 1],
                               scale=1.0 / S).then_inc(g_hi if hi else g_32, 1)

            def misc(i, slot):
                act.wait_ge(z_full, at(i, Z_USES, z_use(slot, False) + 1))
                if slot == 0:
                    act.activation(qk[:, :, :, :].rearrange("p a k n -> p (a k n)"), z[:, :], ACT.Relu,
                                   scale=1.0 / S).then_inc(z_free, 1)
                else:
                    act.activation(vv[:, :, :].rearrange("p k n -> p (k n)"), z[:, 0:KT * CW], ACT.Copy,
                                   scale=1.0 / S).then_inc(z_free, 1)

            act.activation(rstc[:, :], ca[:, :], ACT.Gelu)
            with act.Fori(0, NI) as i:
                for slot in range(C):
                    gates(i, slot, g_a, ga, a_pe, a_act)
                    gelu(i, slot, 0, True)
                    cell_tanh(i, slot, ca, ta, a_cell, a_tanh)
                    if slot in (0, 1):
                        misc(i, slot)
                    gelu(i, slot, 0, False)
                    gelu(i, slot, 1, True)
                    gates(i, slot, g_e, ge, e_pe, e_act)
                    gelu(i, slot, 1, False)
                    s = (slot - C0) % C
                    act.wait_ge(c_pe, at(i, C, slot + 1))
                    act.activation(c_hh[:, :, s * B:(s + 1) * B], g_c[:, s, :, :], ACT.Tanh,
                                   scale=1.0 / S).then_inc(c_hi, 1)
                    act.activation(c32[:, :].rearrange("p (k b) -> p k b", b=B), g_c[:, s, :, :], ACT.Tanh,
                                   scale=1.0 / S).then_inc(c_32, 1)
                    cell_tanh(i, slot, ce, te_, e_cell, e_tanh)
                    if slot == 12:
                        act.wait_ge(route, at(i, ROUTE, NH + 1))
                        act.activation(rt[:, 1, :, :], rt[:, 0, :, :], ACT.Tanh, scale=0.5).then_inc(route_t, 1)

        @block.gpsimd
        def _(pool):
            with pool.Fori(0, NI) as i:
                for slot in range(C):
                    b = slot % 2
                    if 1 <= slot <= 4:
                        p = slot - 1
                        m, s0 = p // 2, (p % 2) * HALF
                        if p == 0:
                            pool.wait_ge(z_free, at(i, Z_USES, 1))
                        q3 = qk[:, 0, m, s0:s0 + HALF].rearrange("p (t l) -> p t l", l=B)
                        k3 = qk[:, 1, m, s0:s0 + HALF].rearrange("p (t l) -> p t l", l=B)
                        pool.tensor_tensor(prod[:, p, :].rearrange("p (t l m) -> p t l m", l=B, m=B),
                                           q3.unsqueeze(3).to_broadcast([P, 8, B, B]),
                                           k3.unsqueeze(2).to_broadcast([P, 8, B, B]),
                                           ALU.mult).then_inc(prod_done, 1)
                    for h in range(2):
                        pool.wait_ge(g_hi, at(i, 32, 2 * slot + 1 + h))
                        pool.wait_ge(g_32, at(i, 32, 2 * slot + 1 + h))
                        r = slice(h * 512, (h + 1) * 512)
                        pool.tensor_tensor(hm_l[:, b, r], hm32[:, b, r], hm_h[:, b, r],
                                           ALU.subtract).then_inc(g_lo, 1)
                    if slot == 7:
                        pool.wait_ge(x1_done, at(i, 1, 1))
                        pool.tensor_copy(xs[:, :, bass.ds((i + (LAG - 1)) * CW, CW)], x1[:, :, :]).then_inc(x1_kept, 1)

        @block.vector
        def _(dve):
            def cell(i, slot, g, pt, c, act_sem, part, cell_sem):
                dve.wait_ge(act_sem, at(i, C, slot + 1))
                dve.scalar_tensor_tensor(out=pt[:, 0, :], in0=g[:, 16:32], scalar=1.0, in1=c[:, :], op0=ALU.add,
                                         op1=ALU.mult).then_inc(part, 1)
                dve.scalar_tensor_tensor(out=pt[:, 1, :], in0=g[:, 0:16], scalar=1.0, in1=g[:, 48:64], op0=ALU.add,
                                         op1=ALU.mult).then_inc(part, 1)
                dve.wait_ge(part, at(i, 32, 2 * slot + 2))
                dve.scalar_tensor_tensor(out=c[:, :], in0=pt[:, 0, :], scalar=0.5, in1=pt[:, 1, :], op0=ALU.mult,
                                         op1=ALU.add).then_inc(cell_sem, 1)

            def state(i, slot, g, tc, f, hh, hl, tanh_sem, hi_sem, h32_sem, lo_sem):
                k2 = "p (k b) -> p k b"
                o3, t3, f3 = (v.rearrange(k2, b=B) for v in (g[:, 32:48], tc[:, :], f[:, :]))
                r = slice(slot * B, (slot + 1) * B)
                dve.wait_ge(tanh_sem, at(i, C, slot + 1))
                dve.scalar_tensor_tensor(out=hh[:, :, r], in0=o3, scalar=1.0, in1=t3, op0=ALU.add,
                                         op1=ALU.mult).then_inc(hi_sem, 1)
                dve.scalar_tensor_tensor(out=f3, in0=o3, scalar=1.0, in1=t3, op0=ALU.add,
                                         op1=ALU.mult).then_inc(h32_sem, 1)
                dve.wait_ge(hi_sem, at(i, C, slot + 1))
                dve.wait_ge(h32_sem, at(i, C, slot + 1))
                dve.tensor_tensor(hl[:, :, r], f3, hh[:, :, r], ALU.subtract).then_inc(lo_sem, 1)

            def combine(i, slot):
                e = (slot - W1_0 - 3) % E1
                dve.wait_ge(z_full, at(i, Z_USES, z_use(slot, False)))
                zz = z[:, 0:D].rearrange("p (h d) -> p h d", d=HD)
                w = wts[:, :, e].unsqueeze(2).to_broadcast([P, NH, HD])
                a3 = acc[:, :].rearrange("p (h d) -> p h d", d=HD)
                dve.wait_ge(acc_done, at(i, E1, slot))
                if e == 0:
                    dve.wait_ge(route, at(i, ROUTE, ROUTE))
                dve.tensor_tensor(tmp[:, slot % 2, :, :], zz, w, ALU.mult).then_inc(z_free, 1)
                dve.wait_ge(z_free, at(i, Z_USES, z_use(slot, False)))
                if e == 0:
                    dve.tensor_copy(a3, tmp[:, slot % 2, :, :]).then_inc(acc_done, 1)
                else:
                    dve.tensor_tensor(a3, a3, tmp[:, slot % 2, :, :], ALU.add).then_inc(acc_done, 1)

            def scores(i, slot):
                def z_wait():
                    dve.wait_ge(z_full, at(i, Z_USES, z_use(slot, False) + 1))
                z_read = at(i, Z_USES, z_use(slot, False) + 1)
                if 2 <= slot <= 5:
                    p = slot - 2
                    m, s0 = p // 2, (p % 2) * HALF
                    b = p % 2
                    z_wait()
                    dve.tensor_tensor(sw[:, b, :].rearrange("p (t c) -> p t c", c=B * B),
                                      z[:, :].rearrange("p (t c) -> p t c", c=B * B),
                                      wcos[:, :].unsqueeze(1).to_broadcast([P, 8, B * B]), ALU.mult).then_inc(z_free, 1)
                    dve.wait_ge(z_free, z_read)
                    dve.tensor_reduce(den[:, m, s0:s0 + HALF], sw[:, b, :].rearrange("p (c m) -> p c m", m=B), AX_X,
                                      ALU.add).then_inc(s_read, 1)

            def between_a(i, slot):
                if 3 <= slot <= 6:
                    p = slot - 3
                    m, s0 = p // 2, (p % 2) * HALF
                    dve.wait_ge(s_read, at(i, 20, 5 * p + 3))
                    dve.tensor_scalar(dmx[:, m, s0:s0 + HALF], den[:, m, s0:s0 + HALF], EPS_Z, None,
                                      ALU.max).then_inc(s_read, 1)
                    dve.wait_ge(s_read, at(i, 20, 5 * p + 4))
                    dve.reciprocal(rcd[:, m, s0:s0 + HALF], dmx[:, m, s0:s0 + HALF]).then_inc(s_read, 1)
                elif slot == 13:
                    dve.wait_ge(route_t, at(i, 1, 1))
                    dve.tensor_scalar(rt[:, 4, :, :], rt[:, 1, :, :], -1.0, 1.0, ALU.mult, ALU.add).then_inc(route, 1)
                    dve.wait_ge(route, at(i, ROUTE, CHOSEN + 4))
                    dve.reciprocal(rt[:, 5, :, :], rt[:, 4, :, :]).then_inc(route, 1)

            def between_e(i, slot):
                if 2 <= slot <= 5:
                    p = slot - 2
                    m, s0 = p // 2, (p % 2) * HALF
                    b = p % 2
                    v3 = vv[:, m, s0:s0 + HALF].rearrange("p (t l) -> p t l", l=B)
                    dve.tensor_tensor(sv[:, b, :].rearrange("p (t l m) -> p t l m", l=B, m=B),
                                      sw[:, b, :].rearrange("p (t l m) -> p t l m", l=B, m=B),
                                      v3.unsqueeze(2).to_broadcast([P, 8, B, B]), ALU.mult).then_inc(s_read, 1)
                elif slot == 12:
                    dve.wait_ge(route, at(i, ROUTE, NH))
                    dve.tensor_tensor(rt[:, 0, :, :], lg[:, :, :], m8[:, :, 0].unsqueeze(2).to_broadcast([P, NH, E1]),
                                      ALU.subtract).then_inc(route, 1)
                elif slot == 13:
                    dve.wait_ge(route, at(i, ROUTE, CHOSEN + 5))
                    dve.scalar_tensor_tensor(out=rt[:, 6, :, :], in0=rt[:, 1, :, :], scalar=1.0, in1=rt[:, 5, :, :],
                                             op0=ALU.add, op1=ALU.mult).then_inc(route, 1)

            def late(i, slot):
                if 2 <= slot <= 5:
                    p = slot - 2
                    m, s0 = p // 2, (p % 2) * HALF
                    b = p % 2
                    dve.wait_ge(s_read, at(i, 20, 5 * p + 2))
                    dve.tensor_reduce(num[:, m, s0:s0 + HALF], sv[:, b, :].rearrange("p (c m) -> p c m", m=B), AX_X,
                                      ALU.add).then_inc(s_read, 1)
                elif slot == 8:
                    nxt = xs[:, :, bass.ds((i + (LAG + 1)) * CW, CW)]
                    dve.tensor_scalar(x_h[:, :, :], nxt, 1.0, None, ALU.mult).then_inc(x_split, 1)
                    dve.wait_ge(x_split, at(i, 2, 1))
                    dve.tensor_tensor(x_l[:, :, :], nxt, x_h[:, :, :], ALU.subtract).then_inc(x_split, 1)
                elif slot == 11:
                    for h in range(NH):
                        dve.max(m8[:, h, :], lg[:, h, :]).then_inc(route, 1)
                elif slot == 12:
                    for h in range(NH):
                        dve.max_index(i8[:, h, :], m8[:, h, :], lg[:, h, :]).then_inc(route, 1)
                    dve.wait_ge(route, at(i, ROUTE, 2 * NH + 1))
                    dve.tensor_copy(idf[:, :, :], i8[:, :, 0:2]).then_inc(route, 1)
                    dve.wait_ge(route, at(i, ROUTE, CHOSEN))
                    io = iota[:, :].unsqueeze(1).to_broadcast([P, NH, E1])
                    for j in range(2):
                        dve.tensor_tensor(rt[:, 2 + j, :, :], io, idf[:, :, j].unsqueeze(2).to_broadcast([P, NH, E1]),
                                          ALU.is_equal).then_inc(route, 1)
                    dve.wait_ge(route, at(i, ROUTE, CHOSEN + 2))
                    dve.tensor_tensor(rt[:, 2, :, :], rt[:, 2, :, :], rt[:, 3, :, :], ALU.add).then_inc(route, 1)
                elif slot == 13:
                    dve.wait_ge(route, at(i, ROUTE, CHOSEN + 6))
                    dve.tensor_reduce(sm[:, 0, :], rt[:, 6, :, :], AX_X, ALU.add).then_inc(route, 1)
                    dve.tensor_tensor(rt[:, 7, :, :], rt[:, 6, :, :], rt[:, 2, :, :], ALU.mult).then_inc(route, 1)
                    dve.wait_ge(route, at(i, ROUTE, CHOSEN + 8))
                    dve.reciprocal(sm[:, 1, :], sm[:, 0, :]).then_inc(route, 1)
                    dve.wait_ge(route, at(i, ROUTE, CHOSEN + 9))
                    dve.tensor_tensor(wts[:, :, :], rt[:, 7, :, :], sm[:, 1, :].unsqueeze(2).to_broadcast([P, NH, E1]),
                                      ALU.mult).then_inc(route, 1)

            def misc(i, slot):
                def z_wait():
                    dve.wait_ge(z_full, at(i, Z_USES, z_use(slot, False) + 1))
                z_read = at(i, Z_USES, z_use(slot, False) + 1)
                if slot == 6:
                    dve.wait_ge(s_read, at(i, 20, 20))
                    dve.tensor_tensor(att[:, :, :], num[:, :, :], rcd[:, :, :], ALU.mult).then_inc(b_fin, 1)
                    dve.wait_ge(b_fin, at(i, 3, 1))
                    dve.tensor_copy(at_h[:, :, :], att[:, :, :]).then_inc(b_fin, 1)
                    dve.wait_ge(b_fin, at(i, 3, 2))
                    dve.tensor_tensor(at_l[:, :, :], att[:, :, :], at_h[:, :, :], ALU.subtract).then_inc(b_fin, 1)
                elif slot == 7:
                    z_wait()
                    dve.wait_ge(x1_kept, at(i, 1, 0))
                    dve.scalar_tensor_tensor(out=x1[:, :, :], in0=z[:, 0:KT * CW].rearrange("p (k n) -> p k n", n=CW),
                                             scalar=1.0 / S, in1=xs[:, :, bass.ds((i + (LAG - 1)) * CW, CW)],
                                             op0=ALU.mult, op1=ALU.add).then_inc(x1_done, 1)
                    dve.wait_ge(x1_done, at(i, 1, 1))
                    dve.tensor_copy(x1_h[:, :, :], x1[:, :, :]).then_inc(z_free, 1)
                    dve.wait_ge(z_free, z_read)
                    dve.tensor_tensor(x1_l[:, :, :], x1[:, :, :], x1_h[:, :, :], ALU.subtract).then_inc(x1_split, 1)
                elif slot == 9:
                    z_wait()
                    z3 = z[:, 0:KT * CW].rearrange("p (k n) -> p k n", n=CW)
                    dve.tensor_scalar(tk_h[:, :, :], z3, 1.0 / S, None, ALU.mult).then_inc(tk_split, 1)
                    dve.wait_ge(tk_split, at(i, 1, 1))
                    dve.scalar_tensor_tensor(out=tk_l[:, :, :], in0=z3, scalar=1.0 / S, in1=tk_h[:, :, :], op0=ALU.mult,
                                             op1=ALU.subtract).then_inc(z_free, 1)
                elif slot == 11:
                    dve.wait_ge(tokens_in, at(i, TIN, TIN))
                    dve.wait_ge(xy_full, at(i, 32, 2 * slot))
                    z_wait()
                    dve.tensor_scalar(lg[:, :, :].rearrange("p h e -> p (h e)"), z[:, 0:NH * E1], 1.0 / S, None,
                                      ALU.mult).then_inc(z_free, 1)
                    dve.wait_ge(z_free, z_read)
                    dve.tensor_copy(tst[:, :], tnew[:, :]).then_inc(t_copied, 1)
                elif slot == 12:
                    z_wait()
                    dve.tensor_copy(wt_h[:, :], z[:, 0:P]).then_inc(wt_split, 1)
                    dve.wait_ge(wt_split, at(i, 1, 1))
                    dve.tensor_tensor(wt_l[:, :], z[:, 0:P], wt_h[:, :], ALU.subtract).then_inc(z_free, 1)
                elif slot == 13:
                    z_wait()
                    z3 = z[:, 0:KT * CW].rearrange("p (k n) -> p k n", n=CW)
                    dve.tensor_scalar(om_h[:, :, :], z3, 1.0 / S, None, ALU.mult).then_inc(om_split, 1)
                    dve.wait_ge(om_split, at(i, 1, 1))
                    dve.scalar_tensor_tensor(out=om_l[:, :, :], in0=z3, scalar=1.0 / S, in1=om_h[:, :, :], op0=ALU.mult,
                                             op1=ALU.subtract).then_inc(z_free, 1)
                elif slot == 14:
                    z_wait()
                    dve.wait_ge(x2_sent, at(i, 16, 0))
                    dve.scalar_tensor_tensor(out=x2[:, :, :], in0=z[:, 0:KT * CW].rearrange("p (k n) -> p k n", n=CW),
                                             scalar=1.0 / S, in1=xs[:, :, bass.ds((i + (LAG - 3)) * CW, CW)],
                                             op0=ALU.mult, op1=ALU.add).then_inc(x2_done, 1)
                    dve.wait_ge(x2_done, at(i, 1, 1))
                    dve.tensor_copy(x2_h[:, :, :], x2[:, :, :]).then_inc(z_free, 1)
                    dve.wait_ge(z_free, z_read)
                    dve.tensor_tensor(x2_l[:, :, :], x2[:, :, :], x2_h[:, :, :], ALU.subtract).then_inc(x2_split, 1)

            with dve.Fori(0, NI) as i:
                for slot in range(C):
                    combine(i, slot)
                    cell(i, slot, ga, pa, ca, a_act, a_part, a_cell)
                    between_a(i, slot)
                    state(i, slot, ga, ta, fa, a_hh, a_hl, a_tanh, a_hi, a_h32, a_lo)
                    if 2 <= slot <= 5:
                        scores(i, slot)
                    elif slot in MISC[2:] or slot == 6:
                        misc(i, slot)
                    if slot == 15:
                        dve.wait_ge(a_lo, at(i, C, C))
                        dve.tensor_copy(ac_h[:, :, :], a_hh[:, :, :]).then_inc(ac_copied, 1)
                        dve.tensor_copy(ac_l[:, :, :], a_hl[:, :, :]).then_inc(ac_copied, 1)
                    if slot == 0:
                        dve.wait_ge(e_reset, at(i, 6, 0))
                    cell(i, slot, ge, pe_, ce, e_act, e_part, e_cell)
                    between_e(i, slot)
                    s = (slot - C0) % C
                    dve.wait_ge(c_hi, at(i, C, slot + 1))
                    dve.wait_ge(c_32, at(i, C, slot + 1))
                    dve.tensor_tensor(c_hl[:, :, s * B:(s + 1) * B], c32[:, :].rearrange("p (k b) -> p k b", b=B),
                                      c_hh[:, :, s * B:(s + 1) * B], ALU.subtract).then_inc(c_lo, 1)
                    state(i, slot, ge, te_, fe, e_hh, e_hl, e_tanh, e_hi, e_h32, e_lo)
                    late(i, slot)
                    if slot == C0 - 1:
                        dve.wait_ge(c_lo, at(i, C, C0))
                        dve.tensor_copy(cc_h[:, :, :], c_hh[:, :, :]).then_inc(cc_copied, 1)
                        dve.tensor_copy(cc_l[:, :, :], c_hl[:, :, :]).then_inc(cc_copied, 1)
                        dve.wait_ge(cc_copied, at(i, 2, 2))
                        for j, hist in enumerate((c_hh, c_hl)):
                            dve.tensor_scalar(rst[:, j, :].rearrange("p (k b) -> p k b", b=B), hist[:, :, CW - B:CW],
                                              keep[:, 0, bass.ds(i, 1)], None, ALU.mult).then_inc(c_reset, 1)
                        dve.wait_ge(c_reset, at(i, 4, 2))
                        for j, hist in enumerate((c_hh, c_hl)):
                            dve.scalar_tensor_tensor(out=hist[:, :, CW - B:CW], in0=h0c[:, j], scalar=keep[:, 1, bass.ds(i, 1)],
                                                     in1=rst[:, j, :].rearrange("p (k b) -> p k b", b=B), op0=ALU.mult,
                                                     op1=ALU.add).then_inc(c_reset, 1)
                    if slot == 15:
                        dve.wait_ge(e_lo, at(i, C, C))
                        dve.tensor_tensor(hs1[:, :, bass.ds(i * CW, CW)], e_hh[:, :, :], e_hl[:, :, :],
                                          ALU.add).then_inc(e_reset, 1)
                        for j, hist in enumerate((e_hh, e_hl)):
                            dve.tensor_scalar(rst[:, 2 + j, :].rearrange("p (k b) -> p k b", b=B),
                                              hist[:, :, CW - B:CW], keep[:, 2, bass.ds(i, 1)], None,
                                              ALU.mult).then_inc(e_reset, 1)
                        dve.wait_ge(e_reset, at(i, 6, 3))
                        for j, hist in enumerate((e_hh, e_hl)):
                            dve.scalar_tensor_tensor(out=hist[:, :, CW - B:CW], in0=h0e[:, j],
                                                     scalar=keep[:, 3, bass.ds(i, 1)],
                                                     in1=rst[:, 2 + j, :].rearrange("p (k b) -> p k b", b=B),
                                                     op0=ALU.mult, op1=ALU.add).then_inc(e_reset, 1)
                        dve.tensor_scalar(ce[:, :], ce[:, :], keep[:, 2, bass.ds(i, 1)], None,
                                          ALU.mult).then_inc(e_reset, 1)


BT = T
TT = T // P
HV = D // B
LN_EPS = 1e-5
DK = D // NH


def layernorm(nc, hs1, mean_w, gamma, beta, mean, var):
    W = 512
    with ExitStack() as ctx:
        def sb(name, shape, dt=F32):
            return ctx.enter_context(nc.sbuf_tensor(name, shape, dt))

        def sem(name):
            return ctx.enter_context(nc.semaphore(name))

        dd, sq, xg = (sb("ln_" + n, [P, KT, W]) for n in ("dd", "sq", "xg"))
        va, root, y, yy, vy, rstd = (sb("ln_" + n, [P, W]) for n in ("va", "root", "y", "yy", "vy", "rstd"))
        first_root = sb("ln_first_root", [P, 1])
        mean_pe, var_pe, d_ready, sq_ready, root_ready, steps, kept = (
            sem("ln_" + n) for n in ("mean_pe", "var_pe", "d_ready", "sq_ready", "root_ready", "steps", "kept"))
        NST = 5
        per = [(mean_pe, 1), (var_pe, 1), (d_ready, 1), (sq_ready, 1), (root_ready, 1), (steps, NST), (kept, 4)]
        with nc.Block() as block:
            @block.sync
            def _(sp):
                for s, n in per:
                    sp.sem_inc(s, n)

        with nc.Block() as block:
            @block.tensor
            def _(pe):
                with pe.Fori(0, T * B // W) as j:
                    x = hs1[:, :, bass.ds(j * W + LAG * CW, W)]
                    pe.wait_ge(kept, at(j, 4, 0))
                    for k in range(KT):
                        last = pe.matmul(mean[:, :], mean_w[:, :], x[:, k, :], start=(k == 0), stop=(k == KT - 1))
                    last.then_inc(mean_pe, 1)
                    pe.wait_ge(sq_ready, at(j, 1, 1))
                    for k in range(KT):
                        last = pe.matmul(var[:, :], mean_w[:, :], sq[:, k, :], start=(k == 0), stop=(k == KT - 1))
                    last.then_inc(var_pe, 1)

            @block.scalar
            def _(act):
                act.activation(first_root[:, :], mean_w[:, 0:1], ACT.Sqrt)
                with act.Fori(0, T * B // W) as j:
                    act.wait_ge(d_ready, at(j, 1, 1))
                    act.activation(sq[:, :, :], dd[:, :, :], ACT.Square).then_inc(sq_ready, 1)
                    act.wait_ge(steps, at(j, NST, 1))
                    act.activation(root[:, :], va[:, :], ACT.Sqrt).then_inc(root_ready, 1)

            @block.vector
            def _(dve):
                with dve.Fori(0, T * B // W) as j:
                    x = hs1[:, :, bass.ds(j * W + LAG * CW, W)]
                    dve.wait_ge(mean_pe, at(j, 1, 1))
                    dve.tensor_tensor(dd[:, :, :], x, mean[:, :].unsqueeze(1).to_broadcast([P, KT, W]),
                                      ALU.subtract).then_inc(d_ready, 1)
                    dve.wait_ge(var_pe, at(j, 1, 1))
                    dve.tensor_scalar(va[:, :], var[:, :], 4 * LN_EPS, None, ALU.add).then_inc(steps, 1)
                    dve.wait_ge(root_ready, at(j, 1, 1))
                    dve.reciprocal(y[:, :], root[:, :]).then_inc(steps, 1)
                    dve.wait_ge(steps, at(j, NST, 2))
                    dve.tensor_tensor(yy[:, :], y[:, :], y[:, :], ALU.mult).then_inc(steps, 1)
                    dve.wait_ge(steps, at(j, NST, 3))
                    dve.scalar_tensor_tensor(out=vy[:, :], in0=yy[:, :], scalar=-0.5, in1=va[:, :], op0=ALU.mult,
                                             op1=ALU.mult).then_inc(steps, 1)
                    dve.wait_ge(steps, at(j, NST, 4))
                    dve.scalar_tensor_tensor(out=rstd[:, :], in0=vy[:, :], scalar=1.5, in1=y[:, :], op0=ALU.add,
                                             op1=ALU.mult).then_inc(steps, 1)
                    dve.wait_ge(steps, at(j, NST, 5))
                    for k in range(KT):
                        dve.scalar_tensor_tensor(out=xg[:, k, :], in0=dd[:, k, :], scalar=gamma[:, k:k + 1],
                                                 in1=rstd[:, :], op0=ALU.mult, op1=ALU.mult).then_inc(kept, 1)
                    dve.wait_ge(kept, at(j, 4, 2))
                    for k in range(KT):
                        dve.tensor_scalar(x[:, k, :], xg[:, k, :], beta[:, k:k + 1], None, ALU.add).then_inc(kept, 1)


def attention_two(nc, t, hs1, attd, m12_h, m12_l):
    with ExitStack() as ctx:
        def sb(name, shape, dt=F32):
            return ctx.enter_context(nc.sbuf_tensor(name, shape, dt))

        def sem(name):
            return ctx.enter_context(nc.semaphore(name))

        w_hi = {n: sb(n + "2_hi", [P, KT, D], F16) for n in ("q", "k", "v")}
        w_lo = {n: sb(n + "2_lo", [P, KT, D], F16) for n in ("q", "k", "v")}
        brow = sb("brow2", [2, 3 * D], F16)
        ones2 = sb("ones2b", [2, BT], F16)
        mean_w = sb("mean_w", [P, P])
        ident = sb("ident2", [P, P])
        gamma, beta = sb("gamma", [P, KT]), sb("beta", [P, KT])
        xn_h, xn_l = sb("xn_h", [P, KT, BT], F16), sb("xn_l", [P, KT, BT], F16)
        q_h, q_l, k_h, k_l = (sb(n, [P, KT, BT], F16) for n in ("q_h", "q_l", "k_h", "k_l"))
        v_h, v_l = sb("v_h", [P, TT, D], F16), sb("v_l", [P, TT, D], F16)
        first_exp = sb("first_exp", [P, 1])
        nmax = sb("nmax", [P, 2, TT])
        prob = sb("prob", [P, 2, TT, BT])
        sums, rinv = sb("sums", [P, NH, TT]), sb("rinv", [P, NH, TT])
        pt_h, pt_l = sb("pt_h", [P, 2, TT, BT], F16), sb("pt_l", [P, 2, TT, BT], F16)
        att = sb("att2", [P, NH, TT, HV])

        sc = [ctx.enter_context(nc.psum_tensor(f"sc{j}", [P, TT, BT], F32)) for j in range(2)]
        pt = [ctx.enter_context(nc.psum_tensor(f"pt{j}", [P, TT, BT], F32)) for j in range(2)]
        po = ctx.enter_context(nc.psum_tensor("po", [P, NH, TT, HV], F32))
        pq, pk, pv = (ctx.enter_context(nc.psum_tensor(n, [P, TT, BT], F32)) for n in ("pq", "pk", "pv"))

        with ExitStack() as st:
            s_q = st.enter_context(nc.sbuf_tensor("s_q", [P, KT, D], F32))
            s_k = st.enter_context(nc.sbuf_tensor("s_k", [P, KT, D], F32))
            s_v8 = st.enter_context(nc.sbuf_tensor("s_v8", [P, KT, D, 8], F32))
            s_v = st.enter_context(nc.sbuf_tensor("s_v", [P, KT, D], F32))
            s_b8 = st.enter_context(nc.sbuf_tensor("s_b8", [1, D, 8], F32))
            s_b = st.enter_context(nc.sbuf_tensor("s_b2", [1, 3 * D], F32))
            s_bl = st.enter_context(nc.sbuf_tensor("s_b2l", [1, 3 * D], F16))
            loaded, v_sum, hi_done, lo_done, row_sent = (
                st.enter_context(nc.semaphore("at_" + n)) for n in ("loaded", "v_sum", "hi", "lo", "row"))
            jobs = [(s_q[:, :, :], w_hi["q"][:, :, :], w_lo["q"][:, :, :]),
                    (s_k[:, :, :], w_hi["k"][:, :, :], w_lo["k"][:, :, :]),
                    (s_v[:, :, :], w_hi["v"][:, :, :], w_lo["v"][:, :, :]),
                    (s_b[0:1, :], brow[0:1, :], s_bl[0:1, :])]
            kp = "(k p) n -> p k n"
            loads = [(s_q[:, :, :], t["l_wq"].rearrange(kp, p=P)), (s_k[:, :, :], t["l_wk"].rearrange(kp, p=P)),
                     (s_v8[:, :, :, :].rearrange("p k n u -> p k (n u)"), t["l_wv"].rearrange(kp, p=P)),
                     (s_b8[:, :, :].rearrange("a n u -> a (n u)"), t["l_bv"].rearrange("(a n) -> a n", a=1)),
                     (s_b[0:1, 0:D], t["l_bq"].rearrange("(a n) -> a n", a=1)),
                     (s_b[0:1, D:2 * D], t["l_bk"].rearrange("(a n) -> a n", a=1)),
                     (gamma[:, :], t["l_gamma"]), (beta[:, :], t["l_beta"]), (ident[:, :], t["k_ident"])]
            block = st.enter_context(nc.Block())

            @block.sync
            def _(sp):
                for dst, src in loads:
                    sp.dma_start(dst, src).then_inc(loaded, 16)
                sp.wait_ge(lo_done, len(jobs))
                sp.dma_start(brow[1:2, :], s_bl[0:1, :]).then_inc(row_sent, 16)
                sp.wait_ge(row_sent, 16)

            @block.scalar
            def _(act):
                act.wait_ge(loaded, 16 * len(loads))
                act.wait_ge(v_sum, KT + 1)
                for src, hi, _lo in jobs:
                    act.activation(hi, src, ACT.Copy, scale=S).then_inc(hi_done, 1)

            @block.vector
            def _(dve):
                dve.memset(mean_w[:, :], 1.0 / D)
                dve.memset(ones2[:, :], 1.0)
                dve.memset(hs1[:, :, NI * CW:NI * CW + B], 0.0)
                dve.memset(sums[:, :, :], 1.0)
                for tl in (prob, pt_h, pt_l):
                    dve.memset(tl[:, :, :, :], 0.0)
                for tl in (v_h, v_l):
                    dve.memset(tl[:, :, :], 0.0)
                dve.wait_ge(loaded, 16 * len(loads))
                for k in range(KT):
                    dve.tensor_reduce(s_v[:, k, :], s_v8[:, k, :, :], AX_X, ALU.add).then_inc(v_sum, 1)
                dve.tensor_reduce(s_b[0:1, 2 * D:3 * D], s_b8[0:1, :, :], AX_X, ALU.add).then_inc(v_sum, 1)
                for n, (src, hi, lo) in enumerate(jobs):
                    dve.wait_ge(hi_done, n + 1)
                    dve.scalar_tensor_tensor(out=lo, in0=src, scalar=S, in1=hi, op0=ALU.mult,
                                             op1=ALU.subtract).then_inc(lo_done, 1)

        layernorm(nc, hs1, mean_w, gamma, beta, *(b[:, :, :].rearrange("p s n -> p (s n)") for b in (pq, pk)))

        xn_steps, proj_pe = sem("xn_steps"), sem("proj_pe")
        proj_read, qk_split, v_split = sem("proj_read2"), sem("qk_split"), sem("v_split")
        sc_pe, neg_max, exp_done, t_pe, pt_hi, pt_lo, pv_pe = (
            sem(n) for n in ("sc_pe", "neg_max", "exp_done", "t_pe", "pt_hi", "pt_lo", "pv_pe"))
        r_done, att_done, att_sent = sem("r_done"), sem("att_done"), sem("att_sent")
        XN = 2
        per = [(xn_steps, XN), (proj_pe, 3), (proj_read, 3), (qk_split, 2),
               (v_split, 1), (sc_pe, NH), (neg_max, NH), (exp_done, 2 * NH), (t_pe, NH), (pt_hi, NH), (pt_lo, NH),
               (pv_pe, NH), (r_done, 1), (att_done, 1), (att_sent, 2 * 16 * TT)]
        with nc.Block() as block:
            @block.sync
            def _(sp):
                for s, n in per:
                    sp.sem_inc(s, n)

            @block.tensor
            def _(pe):
                for bank in (pt[0][:, :, :].rearrange("p s n -> p (s n)"), pt[1][:, :, :].rearrange("p s n -> p (s n)"),
                             po[:, :, :, :].rearrange("p h s j -> p (h s j)")):
                    for j in range(4):
                        pe.matmul(bank[:, j * P:(j + 1) * P], pt_h[:, 0, 0, 0:P], v_h[:, 0, 0:P], start=(j == 0),
                                  stop=True, skip_group_check=True)

        m_stage = [sb(f"m_stage{j}", [P, 3, HF]) for j in range(2)]
        m_staged = [sem(f"m_staged{j}") for j in range(2)]
        m_split = sem("m_split")
        block = ctx.enter_context(nc.Block())

        @block.gpsimd
        def _(pool):
            work = [(m, k, e) for m in range(2) for k in range(KT) for e in range(0, EA, 3)]

            def load(n):
                m, k, e = work[n]
                pool.dma_start(m_stage[n % 2][:, :, :], t[("m_w1", "m_w2")[m]][k * P:(k + 1) * P, e:e + 3, :])\
                    .then_inc(m_staged[n % 2], 16)

            load(0)
            load(1)
            for n, (m, k, e) in enumerate(work):
                hi, lo = m12_h[:, m, k, e:e + 3, :], m12_l[:, m, k, e:e + 3, :]
                pool.wait_ge(m_staged[n % 2], 16 * (n // 2 + 1))
                w = m_stage[n % 2][:, :, :]
                pool.tensor_scalar(w, w, S / 2, None, ALU.mult).then_inc(m_split, 1)
                pool.wait_ge(m_split, 3 * n + 1)
                pool.tensor_copy(hi, w).then_inc(m_split, 1)
                pool.wait_ge(m_split, 3 * n + 2)
                pool.tensor_tensor(lo, w, hi, ALU.subtract).then_inc(m_split, 1)
                if n + 2 < len(work):
                    pool.wait_ge(m_split, 3 * n + 3)
                    load(n + 2)

        @block.sync
        def _(sp):
            rows = attd[0:B * T * D].rearrange("(b h s p j) -> b p h s j", h=NH, s=TT, p=P, j=HV)
            with sp.Fori(0, B) as b:
                sp.wait_ge(att_done, at(b, 1, 2))
                for s_ in range(TT):
                    sp.dma_start(rows[bass.ds(b, 1), :, :, s_, :].rearrange("o p h j -> (o p) h j"),
                                 att[:, :, s_, :]).then_inc(att_sent, 16)
            sp.wait_ge(att_sent, 16 * TT * (B + 2))

        @block.tensor
        def _(pe):
            def project(b):
                pe.wait_ge(xn_steps, at(b, XN, XN))
                pe.wait_ge(qk_split, at(b, 2, 0))
                pe.wait_ge(v_split, at(b, 1, 0))
                for j, (n, bank) in enumerate((("q", pq), ("k", pk))):
                    for m in range(KT):
                        o = bank[:, m, :]
                        pe.matmul(o, brow[0:2, j * D + m * P:j * D + (m + 1) * P], ones2[0:2, :], start=(m == 0),
                                  stop=False, skip_group_check=True)
                        w = (lambda k, n=n, m=m: w_hi[n][:, k, m * P:(m + 1) * P],
                             lambda k, n=n, m=m: w_lo[n][:, k, m * P:(m + 1) * P])
                        last = split_matmul(pe, o, w, (lambda k: xn_h[:, k, :], lambda k: xn_l[:, k, :]), False,
                                            last=True)
                    last.then_inc(proj_pe, 1)
                for u in range(TT):
                    o = pv[:, u, :]
                    pe.matmul(o, ones2[0:2, 0:P], brow[0:2, 2 * D:3 * D], start=(u == 0), stop=False,
                              skip_group_check=True)
                    w = (lambda k, u=u: xn_h[:, k, u * P:(u + 1) * P], lambda k, u=u: xn_l[:, k, u * P:(u + 1) * P])
                    last = split_matmul(pe, o, w, (lambda k: w_hi["v"][:, k, :], lambda k: w_lo["v"][:, k, :]), False,
                                        last=True)
                last.then_inc(proj_pe, 1)

            def scores(b, h):
                r0, m = DK * (h % 4), h // 4
                if h == 0:
                    pe.wait_ge(qk_split, at(b, 2, 2))
                pe.wait_ge(exp_done, at(b, 2 * NH, 2 * (h - 1)))
                for s_ in range(TT):
                    for q, k in ((q_h, k_h), (q_l, k_h), (q_h, k_l)):
                        last = pe.matmul(sc[h % 2][:, s_, :], q[r0:r0 + DK, m, s_ * P:(s_ + 1) * P],
                                         k[r0:r0 + DK, m, :], start=(s_ == 0 and k is k_h and q is q_h),
                                         stop=(k is k_l), skip_group_check=True, tile_position=(r0, 0))
                last.then_inc(sc_pe, 1)

            def turn(b, h):
                pe.wait_ge(exp_done, at(b, 2 * NH, 2 * (h + 1)))
                pe.wait_ge(pt_lo, at(b, NH, h + 1))
                first = True
                for s_ in range(TT):
                    for u in range(TT):
                        last = pe.matmul(pt[h % 2][:, u, s_ * P:(s_ + 1) * P], prob[:, h % 2, s_, u * P:(u + 1) * P],
                                         ident[:, :], is_transpose=True, start=first, stop=True,
                                         skip_group_check=True)
                        first = False
                last.then_inc(t_pe, 1)

            def values(b, h):
                pe.wait_ge(pt_lo, at(b, NH, h + 3))
                if h == 0:
                    pe.wait_ge(v_split, at(b, 1, 1))
                    pe.wait_ge(att_done, at(b, 1, 1))
                hd = h % NH
                for s_ in range(TT):
                    o = po[:, hd, s_, :]
                    for u in range(TT):
                        for pp, vp in ((pt_h, v_h), (pt_h, v_l), (pt_l, v_h)):
                            last = pe.matmul(o, pp[:, h % 2, u, s_ * P:(s_ + 1) * P], vp[:, u, hd * HV:(hd + 1) * HV],
                                             start=(h == 0 and s_ == 0 and u == 0 and pp is pt_h and vp is v_h),
                                             stop=(u == TT - 1 and pp is pt_l), skip_group_check=True)
                last.then_inc(pv_pe, 1)

            project(0)
            with pe.Fori(0, B) as b:
                for h in range(NH):
                    if h > 0:
                        scores(b, h)
                    turn(b, h - 1)
                    values(b, h - 3)
                    if h == 0:
                        scores(b, h)
                    if h == 4:
                        project(b + 1)
            turn(B, -1)
            for h in (-3, -2, -1):
                values(B, h)

        @block.scalar
        def _(act):
            def flat(a):
                return a.rearrange("p k n -> p (k n)")

            def exps(b, h):
                act.wait_ge(neg_max, at(b, NH, h + 1))
                act.wait_ge(t_pe, at(b, NH, h))
                if h == 0:
                    act.wait_ge(r_done, at(b, 1, 1))
                for s_ in range(TT):
                    act.activation(prob[:, h % 2, s_, :], sc[h % 2][:, s_, :], ACT.Exp, bias=nmax[:, h % 2, s_:s_ + 1],
                                   accum_out=sums[:, h, s_:s_ + 1]).then_inc(exp_done, 1)

            def high(b, h):
                act.wait_ge(t_pe, at(b, NH, h + 2))
                act.wait_ge(pv_pe, at(b, NH, h + 2))
                act.activation(flat(pt_h[:, h % 2]), flat(pt[h % 2][:, :, :]), ACT.Copy).then_inc(pt_hi, 1)

            act.activation(first_exp[:, :], mean_w[:, 0:1], ACT.Exp)
            with act.Fori(0, B) as b:
                for h in range(NH):
                    if h == 0:
                        act.wait_ge(sc_pe, at(b, NH, 0))
                        act.wait_ge(proj_pe, at(b, 3, 1))
                        act.activation(flat(q_h[:, :, :]), flat(pq[:, :, :]), ACT.Copy,
                                       scale=float(DK) ** -0.5 / S).then_inc(proj_read, 1)
                        act.wait_ge(proj_pe, at(b, 3, 2))
                        act.activation(flat(k_h[:, :, :]), flat(pk[:, :, :]), ACT.Copy,
                                       scale=1.0 / S).then_inc(proj_read, 1)
                    high(b, h - 2)
                    exps(b, h)
                    if h == 2:
                        act.wait_ge(pv_pe, at(b, NH, 3))
                        act.wait_ge(proj_pe, at(b, 3, 3))
                        act.activation(flat(v_h[:, :, :]), flat(pv[:, :, :]), ACT.Copy,
                                       scale=1.0 / S).then_inc(proj_read, 1)
            high(B, -2)
            high(B, -1)

        @block.vector
        def _(dve):
            def split_x(b, row):
                dve.wait_ge(proj_pe, at(b, 3, 0))
                dve.tensor_scalar(xn_h[:, :, :], row, 1.0, None, ALU.mult).then_inc(xn_steps, 1)
                dve.wait_ge(xn_steps, at(b, XN, 1))
                dve.tensor_tensor(xn_l[:, :, :], row, xn_h[:, :, :], ALU.subtract).then_inc(xn_steps, 1)

            def low(b, h):
                dve.wait_ge(pt_hi, at(b, NH, h + 3))
                dve.tensor_tensor(pt_l[:, h % 2], pt[h % 2][:, :, :], pt_h[:, h % 2], ALU.subtract).then_inc(pt_lo, 1)

            def inverse(b):
                dve.wait_ge(exp_done, at(b, 2 * NH, 0))
                dve.wait_ge(att_done, at(b, 1, 0))
                dve.reciprocal(rinv[:, :, :], sums[:, :, :]).then_inc(r_done, 1)

            def finish(b):
                dve.wait_ge(r_done, at(b, 1, 1))
                dve.wait_ge(pv_pe, at(b, NH, 3))
                dve.wait_ge(att_sent, at(b, 16 * TT, 0))
                dve.tensor_tensor(att[:, :, :, :].rearrange("p h s j -> p (h s) j"),
                                  po[:, :, :, :].rearrange("p h s j -> p (h s) j"),
                                  rinv[:, :, :].rearrange("p h s -> p (h s)").unsqueeze(2)
                                  .to_broadcast([P, NH * TT, HV]), ALU.mult).then_inc(att_done, 1)

            def rows(first):
                o = LAG * CW + first
                return hs1[:, :, o:o + NCH * CW].rearrange("p k (t b) -> p k t b", b=B)

            split_x(0, rows(0)[:, :, :, 0])
            with dve.Fori(0, B) as b:
                for h in range(NH):
                    if h == 0:
                        for j, (lo, hi, bank, f) in enumerate(((q_l, q_h, pq, float(DK) ** -0.5 / S),
                                                               (k_l, k_h, pk, 1.0 / S))):
                            dve.wait_ge(proj_read, at(b, 3, j + 1))
                            dve.scalar_tensor_tensor(out=lo[:, :, :], in0=bank[:, :, :], scalar=f, in1=hi[:, :, :],
                                                     op0=ALU.mult, op1=ALU.subtract).then_inc(qk_split, 1)
                        inverse(b)
                    dve.wait_ge(sc_pe, at(b, NH, h + 1))
                    dve.wait_ge(exp_done, at(b, 2 * NH, 2 * (h - 1)))
                    dve.tensor_reduce(nmax[:, h % 2, :], sc[h % 2][:, :, :], AX_X, ALU.max,
                                      negate=True).then_inc(neg_max, 1)
                    low(b, h - 2)
                    if h == 2:
                        finish(b)
                        dve.wait_ge(proj_read, at(b, 3, 3))
                        dve.scalar_tensor_tensor(out=v_l[:, :, :], in0=pv[:, :, :], scalar=1.0 / S, in1=v_h[:, :, :],
                                                 op0=ALU.mult, op1=ALU.subtract).then_inc(v_split, 1)
                    if h == 2:
                        split_x(b + 1, rows(1)[:, :, :, bass.ds(b, 1)].rearrange("p k t o -> p k (t o)"))
            inverse(B)
            low(B, -2)
            low(B, -1)
            finish(B)


M_OFF = [min(m * P, HF - P) for m in range(HM)]
G3 = 3 * D
GRP = 2 * EA
GM = HM // 2
NI3 = NCH + 1
OLAG = 2
SLOT_GROUPS = [[0], [1], [2], [3], [4], [5], [6], [7, 8], [9], [10], [11], [12], [13], [14], [15], [16, 17]]
MISC3 = (0, 3, 6)


def pipeline_two(nc, t, arena, attd, x2d, m12_h, m12_l, out):
    with ExitStack() as ctx:
        def sb(name, shape, dt=F32):
            return ctx.enter_context(nc.sbuf_tensor(name, shape, dt))

        def sem(name):
            return ctx.enter_context(nc.semaphore(name))

        m3_h, m3_l = sb("m3_h", [P, EA, HM, D], F16), sb("m3_l", [P, EA, HM, D], F16)
        gx_w = [sb(f"gx_w{p}", [P, KT, G3], F16) for p in range(2)]
        gu_w = [sb(f"gu_w{p}", [P, KT, G3], F16) for p in range(2)]
        wg = [sb(f"wg{p}", [P, KT, E2], F16) for p in range(2)]
        vt_h, vt_l = sb("vt_h", [P, 6, B], F16), sb("vt_l", [P, 6, B], F16)
        rrow = sb("rrow", [2, E2], F16)
        ones2 = sb("ones2c", [2, P], F16)
        ident = sb("ident3", [P, P])
        ident_h = sb("ident_h", [P, P], F16)
        iota = sb("iota3", [P, E2, TOP2])
        k2 = "(k p) n -> p k n"

        with ExitStack() as st:
            s_x = st.enter_context(nc.sbuf_tensor("s_x", [P, KT, G3], F32))
            s_u = st.enter_context(nc.sbuf_tensor("s_u", [P, KT, G3], F32))
            s_c = arena[:, 0, 0:KT * G3].rearrange("p (k n) -> p k n", k=KT)
            s_row = st.enter_context(nc.sbuf_tensor("s_row", [1, G3 + E2], F32))
            s_rl = st.enter_context(nc.sbuf_tensor("s_rl", [1, E2], F16))
            s_wg = st.enter_context(nc.sbuf_tensor("s_wg", [P, KT, E2], F32))
            s_cond = st.enter_context(nc.sbuf_tensor("s_cond3", [P, KT, B], F32))
            s_one = st.enter_context(nc.sbuf_tensor("s_one", [1, B], F32))
            vps = st.enter_context(nc.psum_tensor("vps", [P, 6, B], F32))
            loaded, ready, vt_pe, vt_read, cast, low, low_m, row_sent = (
                st.enter_context(nc.semaphore("g_" + n)) for n in
                ("loaded", "ready", "vt_pe", "vt_read", "cast", "low", "low_m", "row_sent"))
            staged = [st.enter_context(nc.semaphore(f"staged{j}")) for j in range(2)]
            stage = [arena[:, j, 0:E2 * D] for j in range(2)]
            work = []
            for m in range(HM):
                for e in range(0, EA, 8):
                    n = min(8, EA - e)
                    src = t["m_w3"][m * P:(m + 1) * P, e:e + n, :]
                    work.append((src, (n, D), m3_h[:, e:e + n, m, :], m3_l[:, e:e + n, m, :], S))

            def staged_at(n):
                _src, (a, b), _hi, _lo, _f = work[n]
                return stage[n % 2][:, 0:a * b].rearrange("p (a b) -> p a b", b=b)

            smalls = [(s_x[:, :, :], gx_w[0][:, :, :], gx_w[1][:, :, :], S),
                      (s_u[:, :, 0:2 * D], gu_w[0][:, :, 0:2 * D], gu_w[1][:, :, 0:2 * D], S / 2),
                      (s_u[:, :, 2 * D:G3], gu_w[0][:, :, 2 * D:G3], gu_w[1][:, :, 2 * D:G3], S / 4),
                      (s_wg[:, :, :], wg[0][:, :, :], wg[1][:, :, :], S / 2),
                      (s_row[0:1, G3:G3 + E2], rrow[0:1, :], s_rl[0:1, :], S),
                      (ident[:, :], ident_h[:, :], None, 1.0)]
            row = "(a n) -> a n"
            loads = [(s_c[:, :, g * D:(g + 1) * D], t["g_c" + n].rearrange(k2, p=P)) for g, n in enumerate("zrh")]
            loads += [(s_x[:, :, g * D:(g + 1) * D], t["g_w" + n].rearrange(k2, p=P)) for g, n in enumerate("zrh")]
            loads += [(s_u[:, :, g * D:(g + 1) * D], t["g_u" + n].rearrange(k2, p=P)) for g, n in enumerate("zrh")]
            loads += [(s_row[0:1, g * D:(g + 1) * D], t["g_b" + n].rearrange(row, a=1)) for g, n in enumerate("zrh")]
            loads += [(s_row[0:1, G3:G3 + E2], t["m_rb"].rearrange(row, a=1)), (s_wg[:, :, :], t["m_wg"].rearrange(k2, p=P)),
                      (s_cond[:, :, :], t["cond"].rearrange("(k p) b -> p k b", p=P)), (ident[:, :], t["k_ident"]),
                      (iota[:, :, :].rearrange("p e j -> p (e j)"), t["k_iota4"])]
            block = st.enter_context(nc.Block())

            @block.sync
            def _(sp):
                for dst, src in loads:
                    sp.dma_start(dst, src).then_inc(loaded, 16)
                sp.wait_ge(vt_pe, 1)
                for n, (src, *_rest) in enumerate(work):
                    if n >= 2:
                        sp.wait_ge(cast, len(smalls) + n - 1)
                        sp.wait_ge(low_m, n - 1)
                    sp.dma_start(staged_at(n), src).then_inc(staged[n % 2], 16)
                sp.wait_ge(low, 5)
                sp.dma_start(rrow[1:2, :], s_rl[0:1, :]).then_inc(row_sent, 16)
                sp.wait_ge(row_sent, 16)

            @block.gpsimd
            def _(pool):
                pool.memset(s_one[0:1, :], 1.0).then_inc(ready, 1)
                pool.memset(ones2[:, :], 1.0).then_inc(ready, 1)

            @block.tensor
            def _(pe):
                pe.wait_ge(loaded, 16 * len(loads))
                pe.wait_ge(ready, 2)
                for m in range(6):
                    pe.matmul(vps[:, m, :], s_row[0:1, m * P:(m + 1) * P], s_one[0:1, :], start=(m == 0), stop=False,
                              skip_group_check=True)
                    for k in range(KT):
                        last = pe.matmul(vps[:, m, :], s_c[:, k, m * P:(m + 1) * P], s_cond[:, k, :], start=False,
                                         stop=(k == KT - 1), skip_group_check=True)
                last.then_inc(vt_pe, 1)

            @block.scalar
            def _(act):
                act.wait_ge(loaded, 16 * len(loads))
                for src, hi, _lo, f in smalls:
                    act.activation(hi, src, ACT.Copy, scale=f).then_inc(cast, 1)
                for n, (_src, _shape, hi, _lo, f) in enumerate(work):
                    act.wait_ge(staged[n % 2], 16 * (n // 2 + 1))
                    act.activation(hi, staged_at(n), ACT.Copy, scale=f).then_inc(cast, 1)

            @block.vector
            def _(dve):
                for n, (src, hi, lo, f) in enumerate(smalls[:5]):
                    dve.wait_ge(cast, n + 1)
                    dve.scalar_tensor_tensor(out=lo, in0=src, scalar=f, in1=hi, op0=ALU.mult,
                                             op1=ALU.subtract).then_inc(low, 1)
                dve.wait_ge(vt_pe, 1)
                dve.tensor_scalar(vt_h[:, :, :], vps[:, :, :], S, None, ALU.mult).then_inc(vt_read, 1)
                dve.wait_ge(vt_read, 1)
                dve.scalar_tensor_tensor(out=vt_l[:, :, :], in0=vps[:, :, :], scalar=S, in1=vt_h[:, :, :],
                                         op0=ALU.mult, op1=ALU.subtract).then_inc(vt_read, 1)
                for n, (_src, _shape, hi, lo, f) in enumerate(work):
                    dve.wait_ge(cast, len(smalls) + n + 1)
                    dve.scalar_tensor_tensor(out=lo, in0=staged_at(n), scalar=f, in1=hi, op0=ALU.mult,
                                             op1=ALU.subtract).then_inc(low_m, 1)

        x3 = arena[:, :, 0:(NCH + OLAG + 2) * CW]
        def tile(name, dt=F16):
            return sb(name, [P, KT, CW], dt)
        g_hh, g_hl = tile("g_hh"), tile("g_hl")
        hc_h, hc_l = tile("hc_h"), tile("hc_l")
        gx_h, gx_l = tile("gx_h"), tile("gx_l")
        attr = sb("attr", [P, D])
        x2r = tile("x2r", F32)
        outc = tile("outc", F32)
        zr = sb("zr", [P, 32])
        cand = sb("cand", [P, 16])
        h32 = sb("h32", [P, 16])
        rh32 = sb("rh32", [P, 16])
        rh_h, rh_l = sb("rh_h", [P, KT, B], F16), sb("rh_l", [P, KT, B], F16)
        zc, zm = sb("zc", [P, 16]), sb("zm", [P, 16])
        th = sb("th", [P, 2, GM * CW])
        uu = sb("uu", [P, GM * CW])
        a32 = sb("a32", [P, 2, GM * CW])
        a_h, a_l = sb("a_h", [P, 2, GM * CW], F16), sb("a_l", [P, 2, GM * CW], F16)
        acc = sb("acc3", [P, D])
        lg = sb("lg3", [P, E2])
        m8 = sb("m83", [P, 8])
        i8 = sb("i83", [P, 8], U32)
        idf = sb("idf3", [P, TOP2])
        eq = sb("eq", [P, E2, TOP2])
        rt = sb("rt3", [P, 4, E2])
        sm = sb("sm3", [P, 3])
        wts = sb("wts3", [P, EA])

        g_b = [ctx.enter_context(nc.psum_tensor(f"g_b{h}", [P, 8, 6, B], F32)) for h in range(2)]
        p1 = [ctx.enter_context(nc.psum_tensor(f"p1{h}", [P, 512], F32)) for h in range(2)]
        p2 = [ctx.enter_context(nc.psum_tensor(f"p2{h}", [P, 512], F32)) for h in range(2)]
        po = ctx.enter_context(nc.psum_tensor("po3", [P, D], F32))
        z = ctx.enter_context(nc.psum_tensor("z3", [P, 512], F32))

        zr_pe, zr_act, u_pe, u_act = (sem(n) for n in ("zr_pe", "zr_act", "u_pe", "u_act"))
        rh_hi, rh_32, rh_lo, z_parts, z_mix, h_new, h_hi, h_lo = (
            sem(n) for n in ("rh_hi", "rh_32", "rh_lo", "z_parts", "z_mix", "h_new", "h_hi3", "h_lo3"))
        hid_pe, th_act, u_done, a_done, a_hi, a_lo, w3_pe, po_free = (
            sem(n) for n in ("hid_pe", "th_act", "u_done", "a_done", "a_hi3", "a_lo3", "w3_pe", "po_free"))
        z_full, gate_read = sem("z_full3"), sem("gate_read")
        hc_copied, route, x3_done, x3_split, out_done = (
            sem(n) for n in ("hc_copied", "route3", "x3_done", "x3_split", "out_done"))
        exp_done = sem("exp3")
        rows_in, out_sent = sem("rows_in"), sem("out_sent")
        RIN = 16 * (B + 1)
        NR = 10
        per = [(zr_pe, 16), (zr_act, 16), (u_pe, 16), (u_act, 16), (rh_hi, 16), (rh_32, 16), (rh_lo, 16),
               (z_parts, 16), (z_mix, 16), (h_new, 16), (h_hi, 16), (h_lo, 16), (hid_pe, GRP), (th_act, GRP), (u_done, GRP),
               (a_done, GRP), (a_hi, GRP), (a_lo, GRP), (w3_pe, GRP), (po_free, EA), (z_full, 3), (gate_read, 1),
               (hc_copied, 2), (route, NR), (x3_done, 1), (x3_split, 2), (out_done, 1), (exp_done, 1),
               (rows_in, RIN), (out_sent, 16)]

        def project_half(pe, half):
            first = True
            for m in range(6):
                o = g_b[half][:, :, m, :]
                for v in (vt_h, vt_l):
                    pe.matmul(o, ident_h[:, :], v[:, m, :].unsqueeze(1).to_broadcast([P, 8, B]), start=first,
                              stop=False, skip_group_check=True)
                    first = False
                w = (lambda k, m=m: gx_w[0][:, k, m * P:(m + 1) * P], lambda k, m=m: gx_w[1][:, k, m * P:(m + 1) * P])
                r = slice(half * HALF, (half + 1) * HALF)
                last = split_matmul(pe, o, w, (lambda k: gx_h[:, k, r], lambda k: gx_l[:, k, r]), False)
            return last

        def load_rows(sp, c, done):
            for b in range(B):
                sp.dma_start(attr[b * C:(b + 1) * C, :],
                             attd[bass.ds(c * (C * D) + b * T * D, C * D)].rearrange("(t d) -> t d", d=D))\
                    .then_inc(done, 16)
            sp.dma_start(x2r[:, :, :], x2d[:, :, bass.ds((c + (LAG - 1)) * CW, CW)]).then_inc(done, 16)

        def turn_rows(pe):
            for k in range(KT):
                last = pe.matmul(z[:, k * P:(k + 1) * P], attr[:, k * P:(k + 1) * P], ident[:, :], is_transpose=True,
                                 start=(k == 0), stop=True, skip_group_check=True)
            return last

        def add_rows(dve, dst):
            return dve.tensor_tensor(dst.rearrange("p k (t b) -> p k t b", b=B),
                                     z[:, 0:D].rearrange("p (k b t) -> p k t b", k=KT, b=B),
                                     x2r[:, :, :].rearrange("p k (t b) -> p k t b", b=B), ALU.add)

        with ExitStack() as st:
            cleared, hid_zero, pad_sent, x_in, x_tr, x_out, x_first = (
                st.enter_context(nc.semaphore("f_" + n)) for n in
                ("cleared", "hid_zero", "pad_sent", "x_in", "x_tr", "x_out", "x_first"))
            block = st.enter_context(nc.Block())

            @block.gpsimd
            def _(pool):
                for tl in (g_hh, g_hl, hc_l):
                    pool.memset(tl[:, :, :], 0.0)
                pool.memset(hc_h[:, :, :], 0.0).then_inc(hid_zero, 1)
                pool.memset(x3[:, :, 0:OLAG * CW], 0.0)
                for tl in (a_h, a_l, th):
                    pool.memset(tl[:, :, :], 0.0)
                pool.memset(h32[:, :], 0.0)
                pool.memset(acc[:, :], 0.0).then_inc(cleared, 1)
                pool.memset(wts[:, 0:E2], 0.0)
                pool.memset(wts[:, E2:EA], 1.0 / S)

            @block.sync
            def _(sp):
                load_rows(sp, 0, x_in)
                sp.wait_ge(cleared, 1)
                sp.dma_start(attd[B * T * D:(B * T + 2 * C) * D].rearrange("(r d) -> r d", d=D),
                             acc[0:2 * C, :]).then_inc(pad_sent, 16)
                sp.wait_ge(pad_sent, 16)
                for s, n in per:
                    sp.sem_inc(s, n)

            @block.tensor
            def _(pe):
                pe.wait_ge(x_in, 16 * (B + 1))
                turn_rows(pe).then_inc(x_tr, 1)
                pe.wait_ge(x_first, 2)
                project_half(pe, 0)
                pe.wait_ge(hid_zero, 1)
                for bank in (*p1, *p2):
                    for j in range(GM):
                        pe.matmul(bank[:, j * CW:(j + 1) * CW], gx_w[0][:, 0, 0:P], hc_h[:, 0, :], start=(j == 0),
                                  stop=True, skip_group_check=True)
                for k in range(KT):
                    pe.matmul(po[:, k * CW:(k + 1) * CW], gx_w[0][:, 0, 0:P], hc_h[:, 0, :], start=(k == 0),
                              stop=True, skip_group_check=True)

            @block.vector
            def _(dve):
                dve.wait_ge(x_in, 16 * (B + 1))
                dve.wait_ge(x_tr, 1)
                c0 = x3[:, :, OLAG * CW:(OLAG + 1) * CW]
                add_rows(dve, c0).then_inc(x_out, 1)
                dve.wait_ge(x_out, 1)
                dve.tensor_copy(gx_h[:, :, :], c0).then_inc(x_first, 1)
                dve.wait_ge(x_first, 1)
                dve.tensor_tensor(gx_l[:, :, :], c0, gx_h[:, :, :], ALU.subtract).then_inc(x_first, 1)

        block = ctx.enter_context(nc.Block())

        @block.sync
        def _(sp):
            with sp.Fori(0, NI3) as i:
                sp.wait_ge(x3_done, at(i, 1, 0))
                load_rows(sp, i + 1, rows_in)
                sp.wait_ge(out_done, at(i, 1, 1))
                sp.dma_start(out[:, :, bass.ds(i * CW, CW)], outc[:, :, :]).then_inc(out_sent, 16)
            sp.wait_ge(out_done, at(NI3, 1, 1))
            sp.dma_start(out[:, :, NI3 * CW:(NI3 + 1) * CW], outc[:, :, :]).then_inc(out_sent, 16)
            sp.wait_ge(out_sent, 16 + 16 * (NI3 + 1))

        def before(slot):
            return [(g, (g + 2) % GRP) for g in SLOT_GROUPS[(slot - 1) % C]]

        @block.tensor
        def _(pe):
            def zr_gates(i, slot):
                prev = (slot - 1) % C * B
                o = g_b[slot // 8]
                pe.wait_ge(h_hi, at(i, C, slot))
                for m in range(4):
                    for k in range(KT):
                        for w in gu_w:
                            pe.matmul(o[:, slot % 8, m, :], w[:, k, m * P:(m + 1) * P], g_hh[:, k, prev:prev + B],
                                      start=False, stop=False, skip_group_check=True)
                pe.wait_ge(h_lo, at(i, C, slot))
                for m in range(4):
                    for k in range(KT):
                        last = pe.matmul(o[:, slot % 8, m, :], gu_w[0][:, k, m * P:(m + 1) * P],
                                         g_hl[:, k, prev:prev + B], start=False, stop=(k == KT - 1),
                                         skip_group_check=True)
                last.then_inc(zr_pe, 1)

            def candidate(i, slot):
                o = g_b[slot // 8]
                pe.wait_ge(rh_hi, at(i, C, slot + 1))
                for m in (4, 5):
                    for k in range(KT):
                        for w in gu_w:
                            pe.matmul(o[:, slot % 8, m, :], w[:, k, m * P:(m + 1) * P], rh_h[:, k, :],
                                      start=False, stop=False, skip_group_check=True)
                pe.wait_ge(rh_lo, at(i, C, slot + 1))
                for m in (4, 5):
                    for k in range(KT):
                        last = pe.matmul(o[:, slot % 8, m, :], gu_w[0][:, k, m * P:(m + 1) * P], rh_l[:, k, :],
                                         start=False, stop=(k == KT - 1), skip_group_check=True)
                last.then_inc(u_pe, 1)

            def hidden(i, g):
                e = g // 2
                pe.wait_ge(a_done, at(i, GRP, g + 1))
                for mat, bank in enumerate((p1[g % 2], p2[g % 2])):
                    for j in range(GM):
                        c = M_OFF[g % 2 * GM + j]
                        w = (lambda k: m12_h[:, mat, k, e, c:c + P], lambda k: m12_l[:, mat, k, e, c:c + P])
                        last = split_matmul(pe, bank[:, j * CW:(j + 1) * CW], w,
                                            (lambda k: hc_h[:, k, :], lambda k: hc_l[:, k, :]), j == 0, last=True)
                last.then_inc(hid_pe, 1)

            def down(i, k):
                g = (k - 2) % GRP
                e = g // 2
                pe.wait_ge(a_hi, at(i, GRP, k + 1))
                pe.wait_ge(a_lo, at(i, GRP, k + 1))
                if g % 2 == 0:
                    pe.wait_ge(po_free, at(i, EA, k // 2 + 1))
                for j in range(GM):
                    m = g % 2 * GM + j
                    r = slice(j * CW, (j + 1) * CW)
                    for x, w in ((a_h, m3_h), (a_h, m3_l), (a_l, m3_h)):
                        last = pe.matmul(po[:, :], x[:, g % 2, r], w[:, e, m, :],
                                         start=(m == 0 and x is a_h and w is m3_h), stop=(m == HM - 1 and x is a_l),
                                         skip_group_check=True)
                last.then_inc(w3_pe, 1)

            def misc(i, slot):
                if slot == 0:
                    pe.wait_ge(hc_copied, at(i, 2, 0))
                    pe.wait_ge(x3_done, at(i, 1, 0))
                    pe.matmul(z[:, 0:E2], ones2[0:2, :], rrow[0:2, :], start=True, stop=False, skip_group_check=True)
                    last = split_matmul(pe, z[:, 0:E2], (lambda k: hc_h[:, k, :], lambda k: hc_l[:, k, :]),
                                        (lambda k: wg[0][:, k, :], lambda k: wg[1][:, k, :]), False, last=True)
                elif slot == 3:
                    pe.wait_ge(po_free, at(i, EA, 2))
                    if isinstance(i, int):
                        pe.wait_ge(x3_done, at(i, 1, 0))
                    else:
                        pe.wait_ge(gate_read, at(i, 1, 1))
                    for k in range(KT):
                        last = pe.matmul(z[:, k * P:(k + 1) * P], acc[:, k * P:(k + 1) * P], ident[:, :],
                                         is_transpose=True, start=(k == 0), stop=True, skip_group_check=True)
                else:
                    pe.wait_ge(rows_in, at(i, RIN, RIN))
                    pe.wait_ge(out_done, at(i, 1, 1))
                    last = turn_rows(pe)
                last.then_inc(z_full, 1)

            with pe.Fori(0, NI3) as i:
                for slot in range(C):
                    zr_gates(i, slot)
                    if slot == 2:
                        pe.wait_ge(u_act, at(i, C, 0))
                        project_half(pe, 1)
                    if slot == 12:
                        pe.wait_ge(x3_split, at(i, 2, 2))
                        pe.wait_ge(u_act, at(i, C, 8))
                        project_half(pe, 0)
                    if slot in MISC3:
                        misc(i, slot)
                    for n, k in enumerate(SLOT_GROUPS[slot]):
                        hidden(i, k)
                        if n == 0:
                            candidate(i, slot)
                        down(i, k)
            down(NI3, 0)
            down(NI3, 1)
            misc(NI3, 3)

        @block.scalar
        def _(act):
            def high(i, slot):
                for g, n in before(slot):
                    act.wait_ge(a_done, at(i, GRP, n + 1))
                    act.wait_ge(w3_pe, at(i, GRP, n - 1))
                    act.activation(a_h[:, g % 2, :], a32[:, g % 2, :], ACT.Copy).then_inc(a_hi, 1)

            act.activation(cand[:, 0:1], wts[:, 0:1], ACT.Exp)
            with act.Fori(0, NI3) as i:
                for slot in range(C):
                    bank = g_b[slot // 8]
                    act.wait_ge(zr_pe, at(i, C, slot + 1))
                    act.activation(zr[:, :], bank[:, slot % 8, 0:4].rearrange("p m b -> p (m b)"), ACT.Tanh,
                                   scale=0.5 / S).then_inc(zr_act, 1)
                    high(i, slot)
                    act.wait_ge(u_pe, at(i, C, slot + 1))
                    act.activation(cand[:, :], bank[:, slot % 8, 4:6].rearrange("p m b -> p (m b)"), ACT.Tanh,
                                   scale=1.0 / S).then_inc(u_act, 1)
                    for k in SLOT_GROUPS[slot]:
                        act.wait_ge(hid_pe, at(i, GRP, k + 1))
                        act.wait_ge(u_done, at(i, GRP, k + 1))
                        act.activation(th[:, k % 2, :], p1[k % 2][:, 0:GM * CW], ACT.Tanh,
                                       scale=0.5 / S).then_inc(th_act, 1)
                    if slot == 1:
                        act.wait_ge(route, at(i, NR, 2))
                        act.activation(rt[:, 1, :], rt[:, 0, :], ACT.Exp).then_inc(exp_done, 1)
            high(NI3, 0)

        @block.gpsimd
        def _(pool):
            def low(i, slot):
                for g, n in before(slot):
                    pool.wait_ge(a_hi, at(i, GRP, n + 1))
                    pool.tensor_tensor(a_l[:, g % 2, :], a32[:, g % 2, :], a_h[:, g % 2, :],
                                       ALU.subtract).then_inc(a_lo, 1)

            with pool.Fori(0, NI3) as i:
                for slot in range(C):
                    low(i, slot)
            low(NI3, 0)

        @block.vector
        def _(dve):
            def swiglu(i, slot):
                for g, n in before(slot):
                    dve.wait_ge(th_act, at(i, GRP, n - 1))
                    dve.wait_ge(a_done, at(i, GRP, n))
                    dve.scalar_tensor_tensor(out=uu[:, :], in0=th[:, g % 2, :], scalar=1.0,
                                             in1=p1[g % 2][:, 0:GM * CW], op0=ALU.add, op1=ALU.mult).then_inc(u_done, 1)
                    dve.wait_ge(u_done, at(i, GRP, n + 1))
                    dve.wait_ge(a_lo, at(i, GRP, n - 1))
                    dve.scalar_tensor_tensor(out=a32[:, g % 2, :], in0=uu[:, :], scalar=0.5 / S / S,
                                             in1=p2[g % 2][:, 0:GM * CW], op0=ALU.mult, op1=ALU.mult).then_inc(a_done, 1)

            def add_expert(i, slot):
                for k, _n in before(slot):
                    if k % 2 == 0:
                        continue
                    e = (k - 2) % GRP // 2
                    dve.wait_ge(w3_pe, at(i, GRP, k + 1 - (GRP if slot == 0 else 0)))
                    dve.wait_ge(po_free, at(i, EA, (k // 2 + 1) % EA))
                    if e == 0:
                        dve.wait_ge(route, at(i, NR, NR))
                        dve.tensor_scalar(acc[:, :], po[:, :], wts[:, 0:1], None, ALU.mult).then_inc(po_free, 1)
                    else:
                        dve.scalar_tensor_tensor(out=acc[:, :], in0=po[:, :], scalar=wts[:, e:e + 1], in1=acc[:, :],
                                                 op0=ALU.mult, op1=ALU.add).then_inc(po_free, 1)

            def misc(i, slot):
                if slot == 0:
                    dve.wait_ge(z_full, at(i, 3, 1))
                    dve.tensor_scalar(lg[:, :], z[:, 0:E2], 1.0 / S, None, ALU.mult).then_inc(gate_read, 1)
                elif slot == 1:
                    dve.max(m8[:, :], lg[:, :]).then_inc(route, 1)
                    dve.wait_ge(route, at(i, NR, 1))
                    dve.tensor_tensor(rt[:, 0, :], lg[:, :], m8[:, 0:1].to_broadcast([P, E2]),
                                      ALU.subtract).then_inc(route, 1)
                    dve.max_index(i8[:, :], m8[:, :], lg[:, :]).then_inc(route, 1)
                    dve.wait_ge(route, at(i, NR, 3))
                    dve.tensor_copy(idf[:, :], i8[:, 0:TOP2]).then_inc(route, 1)
                elif slot == 2:
                    dve.wait_ge(route, at(i, NR, 4))
                    dve.tensor_tensor(eq[:, :, :], iota[:, :, :], idf[:, :].unsqueeze(1).to_broadcast([P, E2, TOP2]),
                                      ALU.is_equal).then_inc(route, 1)
                    dve.wait_ge(route, at(i, NR, 5))
                    dve.tensor_reduce(rt[:, 2, :], eq[:, :, :], AX_X, ALU.add).then_inc(route, 1)
                    dve.wait_ge(route, at(i, NR, 6))
                    dve.wait_ge(exp_done, at(i, 1, 1))
                    dve.tensor_tensor(rt[:, 3, :], rt[:, 1, :], rt[:, 2, :], ALU.mult).then_inc(route, 1)
                    dve.wait_ge(route, at(i, NR, 7))
                    dve.tensor_reduce(sm[:, 0:1], rt[:, 3, :], AX_X, ALU.add).then_inc(route, 1)
                    dve.wait_ge(route, at(i, NR, 8))
                    dve.reciprocal(sm[:, 1:2], sm[:, 0:1]).then_inc(route, 1)
                    dve.wait_ge(route, at(i, NR, 9))
                    dve.tensor_scalar(wts[:, 0:E2], rt[:, 3, :], sm[:, 1:2], 1.0 / S, ALU.mult,
                                      ALU.mult).then_inc(route, 1)
                elif slot == 3:
                    dve.wait_ge(z_full, at(i, 3, 1 if isinstance(i, int) else 2))
                    dve.wait_ge(out_sent, at(i, 16, 0))
                    x = x3[:, :, i * CW:(i + 1) * CW] if isinstance(i, int) else x3[:, :, bass.ds(i * CW, CW)]
                    dve.tensor_tensor(outc[:, :, :], z[:, 0:D].rearrange("p (k n) -> p k n", n=CW), x,
                                      ALU.add).then_inc(out_done, 1)
                elif slot == 6:
                    dve.wait_ge(z_full, at(i, 3, 3))
                    x = x3[:, :, bass.ds((i + (OLAG + 1)) * CW, CW)]
                    add_rows(dve, x).then_inc(x3_done, 1)
                    dve.wait_ge(x3_done, at(i, 1, 1))
                    dve.tensor_scalar(gx_h[:, :, :], x, 1.0, None, ALU.mult).then_inc(x3_split, 1)
                    dve.wait_ge(x3_split, at(i, 2, 1))
                    dve.tensor_tensor(gx_l[:, :, :], x, gx_h[:, :, :], ALU.subtract).then_inc(x3_split, 1)

            kb = "p (k b) -> p k b"
            with dve.Fori(0, NI3) as i:
                for slot in range(C):
                    swiglu(i, slot)
                    add_expert(i, slot)
                    dve.wait_ge(zr_act, at(i, C, slot + 1))
                    dve.wait_ge(h_new, at(i, C, slot))
                    r3, h3 = zr[:, 16:32].rearrange(kb, b=B), h32[:, :].rearrange(kb, b=B)
                    dve.scalar_tensor_tensor(out=rh_h[:, :, :], in0=r3, scalar=1.0, in1=h3, op0=ALU.add,
                                             op1=ALU.mult).then_inc(rh_hi, 1)
                    dve.scalar_tensor_tensor(out=rh32[:, :].rearrange(kb, b=B), in0=r3, scalar=1.0, in1=h3,
                                             op0=ALU.add, op1=ALU.mult).then_inc(rh_32, 1)
                    dve.wait_ge(rh_hi, at(i, C, slot + 1))
                    dve.wait_ge(rh_32, at(i, C, slot + 1))
                    dve.tensor_tensor(rh_l[:, :, :], rh32[:, :].rearrange(kb, b=B), rh_h[:, :, :],
                                      ALU.subtract).then_inc(rh_lo, 1)
                    if slot == 0:
                        misc(i, slot)
                        dve.wait_ge(gate_read, at(i, 1, 1))
                    dve.scalar_tensor_tensor(out=zc[:, :], in0=zr[:, 0:16], scalar=1.0, in1=h32[:, :],
                                             op0=ALU.subtract, op1=ALU.mult).then_inc(z_parts, 1)
                    if slot in (1, 2, 3, 6):
                        misc(i, slot)
                    dve.wait_ge(u_act, at(i, C, slot + 1))
                    dve.scalar_tensor_tensor(out=zm[:, :], in0=zr[:, 0:16], scalar=1.0, in1=cand[:, :], op0=ALU.add,
                                             op1=ALU.mult).then_inc(z_mix, 1)
                    dve.wait_ge(z_mix, at(i, C, slot + 1))
                    dve.wait_ge(z_parts, at(i, C, slot + 1))
                    rr = slice(slot * B, (slot + 1) * B)
                    dve.scalar_tensor_tensor(out=g_hh[:, :, rr], in0=zc[:, :].rearrange(kb, b=B), scalar=-0.5,
                                             in1=zm[:, :].rearrange(kb, b=B), op0=ALU.mult, op1=ALU.add).then_inc(h_hi, 1)
                    dve.scalar_tensor_tensor(out=h32[:, :], in0=zc[:, :], scalar=-0.5, in1=zm[:, :], op0=ALU.mult,
                                             op1=ALU.add).then_inc(h_new, 1)
                    dve.wait_ge(h_hi, at(i, C, slot + 1))
                    dve.wait_ge(h_new, at(i, C, slot + 1))
                    dve.tensor_tensor(g_hl[:, :, rr], h32[:, :].rearrange(kb, b=B), g_hh[:, :, rr],
                                      ALU.subtract).then_inc(h_lo, 1)
                    if slot == C - 1:
                        dve.wait_ge(h_lo, at(i, C, C))
                        dve.wait_ge(hid_pe, at(i, GRP, GRP))
                        dve.tensor_copy(hc_h[:, :, :], g_hh[:, :, :]).then_inc(hc_copied, 1)
                        dve.tensor_copy(hc_l[:, :, :], g_hl[:, :, :]).then_inc(hc_copied, 1)
            swiglu(NI3, 0)
            add_expert(NI3, 0)
            add_expert(NI3, 2)
            misc(NI3, 3)


def build_kernel(nc, t, out):
    x2d = nc.dram_tensor("x2_dram", (P, KT, (NI + 1) * CW), F32).ap()
    attd = nc.dram_tensor("attention_dram", ((B * T + 2 * C) * D,), F32).ap()
    with nc.sbuf_tensor("hs1", [P, KT, NI * CW + B], F32) as hs1:
        with nc.sbuf_tensor("xs", [P, KT, (NCH + 2 * LAG + 1) * CW], F32) as xs:
            pipeline_one(nc, t, xs, hs1, x2d)
        with (nc.sbuf_tensor("m12_h", [P, 2, KT, EA, HF], F16) as m12_h,
              nc.sbuf_tensor("m12_l", [P, 2, KT, EA, HF], F16) as m12_l):
            attention_two(nc, t, hs1, attd, m12_h, m12_l)
            pipeline_two(nc, t, hs1, attd, x2d, m12_h, m12_l, out)


def _layout(d):
    f = np.float32
    head = np.arange(P) // 16
    th = np.pi / 2 * np.arange(1, B + 1) / B
    tr = lambda a: np.ascontiguousarray(np.transpose(a))
    hidden = lambda r, s: np.ascontiguousarray(np.concatenate([d[r], d[s][None]]).transpose(2, 0, 1))
    down = np.concatenate([d["L1_ffn_W3"], d["L1_ffn_Ws3"][None]]).transpose(2, 0, 1)
    cut = (HM - 1) * P
    return {
        "x": np.ascontiguousarray(np.transpose(d["x"], (2, 1, 0)).reshape(D, T * B)),
        "cond": tr(d["cond_1024"]),
        "a_wx": d["L0_cond_Wx"], "a_wh": d["L0_cond_Wh"], "a_b": d["L0_cond_b"],
        "e_wx": d["L1_cond_Wx"], "e_wh": d["L1_cond_Wh"], "e_b": d["L1_cond_b"],
        "wq": tr(d["L0_attn_Wq"]), "wk": tr(d["L0_attn_Wk"]), "wv": tr(d["L0_attn_Wv"]), "wo": tr(d["L0_attn_Wo"]),
        "c_wx": d["L0_cond2_Wx"], "c_wh": d["L0_cond2_Wh"], "c_b": d["L0_cond2_b"],
        "f_wm": d["L0_ffn_Wm"], "f_bm": d["L0_ffn_bm"], "f_emb": d["L0_ffn_expert_emb"],
        "f_w1": d["L0_ffn_W1"], "f_b1": tr(d["L0_ffn_b1"]), "f_w2": d["L0_ffn_W2"],
        "f_b2": np.ascontiguousarray(np.concatenate(
            [np.pad(d["L0_ffn_b2"], ((0, 0), (h * HD, D - (h + 1) * HD))) for h in range(NH)])), "f_wo": d["L0_ffn_Wo"], "f_bo": d["L0_ffn_bo"],
        "g_cz": d["L1_cond2_C_z"], "g_cr": d["L1_cond2_C_r"], "g_ch": d["L1_cond2_C"],
        "g_wz": d["L1_cond2_W_z"], "g_wr": d["L1_cond2_W_r"], "g_wh": d["L1_cond2_W"],
        "g_uz": d["L1_cond2_U_z"], "g_ur": d["L1_cond2_U_r"], "g_uh": d["L1_cond2_U"],
        "g_bz": d["L1_cond2_b_z"], "g_br": d["L1_cond2_b_r"], "g_bh": d["L1_cond2_b"],
        "m_wg": tr(d["L1_ffn_Wg"]), "m_rb": d["L1_ffn_routing_bias"],
        "m_w1": hidden("L1_ffn_W1", "L1_ffn_Ws1"), "m_w2": hidden("L1_ffn_W2", "L1_ffn_Ws2"),
        "m_w3": np.concatenate([down[:cut], np.zeros((HM * P - HF, EA, D), f), down[cut:]]),
        "k_iota4": np.tile(np.repeat(np.arange(E2), TOP2)[None], (P, 1)).astype(f),
        "l_wq": d["L1_attn_Wq"], "l_wk": d["L1_attn_Wk"], "l_wv": d["L1_attn_Wv"], "l_bq": d["L1_attn_bq"],
        "l_bk": d["L1_attn_bk"], "l_bv": d["L1_attn_bv"],
        "l_gamma": tr(d["L1_attn_gamma"].reshape(KT, P)), "l_beta": tr(d["L1_attn_beta"].reshape(KT, P)),
        "k_ident": np.eye(P, dtype=f), "k_gsum": (head[:, None] == head[None]).astype(f),
        "k_wcos": np.tile(np.cos(th[:, None] - th[None]).reshape(1, -1), (P, 1)).astype(f),
        "k_iota": np.tile(np.arange(E1)[None], (P, 1)).astype(f),
    }


def kernel(**inputs):
    import concourse.bacc as _bacc
    from concourse.bass_utils import run_bass_kernel_spmd as _run

    nc = _bacc.Bacc("TRN2", target_bir_lowering=False, num_devices=1)
    arrays = {"in_" + k: np.ascontiguousarray(v)
              for k, v in _layout({k: np.asarray(v) for k, v in inputs.items()}).items()}
    t = {k[3:]: nc.dram_tensor(k, v.shape, mybir.dt.from_np(v.dtype), kind="ExternalInput").ap()
         for k, v in arrays.items()}
    out = nc.dram_tensor("out_dram", (P, KT, (NCH + OLAG) * CW), F32, kind="ExternalOutput").ap()
    build_kernel(nc, t, out)
    r = _run(nc, [arrays], core_ids=[0]).results[0]["out_dram"]
    r = r[:, :, OLAG * CW:].transpose(1, 0, 2).reshape(D, T, B)
    return np.ascontiguousarray(r.transpose(2, 1, 0))
```

```python
from contextlib import ExitStack

import numpy as np

import concourse.bass as bass
from concourse import mybir

F32 = mybir.dt.float32
F16 = mybir.dt.float16
U32 = mybir.dt.uint32
ALU = mybir.AluOpType
ACT = mybir.ActivationFunctionType
AX_X = mybir.AxisListType.X

P = 128
B = 8
T = 256
D = 256
KT = D // P
C = 16
CW = C * B
HALF = CW // 2
NCH = T // C
LAG = 4
NI = NCH + LAG
M_FIRST = 2
M_LAST = NI - 2
E_FIRST = LAG - 1
S = 64.0
G4 = 4 * D
HD = 32
NH = D // HD
E1 = 16
EPS_Z = 1e-6
E2 = 8
EA = E2 + 1
TOP2 = 4
HF = D * 2 * 4 // 3
HM = 6

C0 = 9
W1_0 = 11
MISC = (0, 1, 2, 3, 4, 5, 7, 9, 11, 12, 13, 14)


def z_use(slot):
    return sum(1 for m in MISC if m < slot)


Z_USES = len(MISC)


def at(i, per, k):
    return (i + 1) * per + k


def split_matmul(pe, out, w, x, start, last=False):
    ins = None
    for k in range(KT):
        for wp, xp in ((0, 0), (1, 0), (0, 1)):
            ins = pe.matmul(out, w[wp](k), x[xp](k), start=start, stop=last and k == KT - 1 and xp == 1,
                            skip_group_check=True)
            start = False
    return ins


def pipeline_one(nc, t, xs, hs1, x2d):
    with ExitStack() as ctx:
        def sb(name, shape, dt=F32):
            return ctx.enter_context(nc.sbuf_tensor(name, shape, dt))

        def sem(name):
            return ctx.enter_context(nc.semaphore(name))

        names = (("a_wx", G4), ("a_wh", G4), ("e_wx", G4), ("e_wh", G4), ("wq", D), ("wk", D), ("wv", D), ("wo", D),
                 ("c_wx", D), ("c_wh", D), ("f_wm", D), ("f_wo", D))
        w_hi = {n: sb(n + "_hi", [P, KT, w], F16) for n, w in names}
        w_lo = {n: sb(n + "_lo", [P, KT, w], F16) for n, w in names}
        b2_hi, b2_lo = sb("b2_hi", [P, D], F16), sb("b2_lo", [P, D], F16)
        w1s = sb("w1s", [P, E1, P], F16)
        es = sb("es", [P, E1], F16)
        w2_hi = sb("w2_hi", [P, E1, HD], F16)
        w2_lo = sb("w2_lo", [P, E1, HD], F16)
        b1 = sb("b1", [P, E1])
        NB = {"a_b": (0, G4), "e_b": (G4, G4), "c_b": (2 * G4, D), "f_bo": (2 * G4 + D, D),
              "f_bm": (2 * G4 + 2 * D, D)}
        BR = 2 * G4 + 3 * D
        brow = sb("brow", [2, BR], F16)
        ones2 = sb("ones2", [2, CW], F16)
        ident = sb("ident", [P, P])
        gsum = sb("gsum", [P, P])
        wcos = sb("wcos", [P, B * B])
        iota = sb("iota", [P, E1])
        keep = sb("keep", [P, 4, NI])
        h0c = sb("h0c", [P, 2, KT, B], F16)
        h0e = sb("h0e", [P, 2, KT, B], F16)
        a_hh = sb("a_hh", [P, KT, CW], F16)
        a_hl = sb("a_hl", [P, KT, CW], F16)
        e_hh = sb("e_hh", [P, KT, CW], F16)
        e_hl = sb("e_hl", [P, KT, CW], F16)
        c_hh = sb("c_hh", [P, KT, CW], F16)
        c_hl = sb("c_hl", [P, KT, CW], F16)
        ga, ge = sb("ga", [P, 64]), sb("ge", [P, 64])
        pa, pe_ = sb("pa", [P, 2, 16]), sb("pe_", [P, 2, 16])
        ca, ce = sb("ca", [P, 16]), sb("ce", [P, 16])
        ta, te_ = sb("ta", [P, 16]), sb("te_", [P, 16])
        fa, fe = sb("fa", [P, 16]), sb("fe", [P, 16])
        c32 = sb("c32", [P, 16])
        rst = sb("rst", [P, 4, 16], F16)
        rstc = sb("rstc", [P, 16])
        def tile(name, dt=F16):
            return sb(name, [P, KT, CW], dt)
        x_h, x_l = tile("x_h"), tile("x_l")
        ac_h, ac_l = tile("ac_h"), tile("ac_l")
        cc_h, cc_l = tile("cc_h"), tile("cc_l")
        x1, x1_h, x1_l = tile("x1", F32), tile("x1_h"), tile("x1_l")
        x2, x2_h, x2_l = tile("x2", F32), tile("x2_h"), tile("x2_l")
        qk = sb("qk", [P, 2, KT, CW])
        vv = tile("vv", F32)
        prod = sb("prod", [P, 4, 512])
        sw = sb("sw", [P, 2, 512])
        sv = sb("sv", [P, 2, 512])
        den, num = tile("den", F32), tile("num", F32)
        dmx, rcd, att = tile("dmx", F32), tile("rcd", F32), tile("att", F32)
        at_h, at_l = tile("at_h"), tile("at_l")
        tk_h, tk_l = tile("tk_h"), tile("tk_l")
        tnew = sb("tnew", [P, NH * CW], F16)
        tst = sb("tst", [P, NH * CW], F16)
        lg = sb("lg", [P, NH, E1])
        m8 = sb("m8", [P, NH, 8])
        i8 = sb("i8", [P, NH, 8], U32)
        idf = sb("idf", [P, NH, 2])
        rt = sb("rt", [P, 8, NH, E1])
        sm = sb("sm", [P, 2, NH])
        wts = sb("wts", [P, NH, E1])
        hm32 = sb("hm32", [P, 2, NH * CW])
        hm_h = sb("hm_h", [P, 2, NH * CW], F16)
        hm_l = sb("hm_l", [P, 2, NH * CW], F16)
        tmp = sb("tmp", [P, 2, NH, HD])
        acc = sb("acc", [P, D])
        om_h, om_l = tile("om_h"), tile("om_l")
        wt_h, wt_l = sb("wt_h", [P, P], F16), sb("wt_l", [P, P], F16)

        g_a = [ctx.enter_context(nc.psum_tensor(f"g_a{h}", [P, 8, 8, B], F32)) for h in range(2)]
        g_e = [ctx.enter_context(nc.psum_tensor(f"g_e{h}", [P, 8, 8, B], F32)) for h in range(2)]
        g_c = ctx.enter_context(nc.psum_tensor("g_c", [P, C, KT, B], F32))
        xy = [ctx.enter_context(nc.psum_tensor(f"xy{h}", [P, 512], F32)) for h in range(2)]
        z = ctx.enter_context(nc.psum_tensor("z", [P, 512], F32))

        def out_bank(slot, a_on, e_on):
            spare = g_e[1] if not e_on else g_a[0] if not a_on else None
            return z if spare is None or slot % C == C - 1 else spare[:, :, :, :].rearrange("p s m b -> p (s m b)")

        def wh(n, m):
            return (lambda k: w_hi[n][:, k, m * P:(m + 1) * P], lambda k: w_lo[n][:, k, m * P:(m + 1) * P])

        def cols(hi, lo, a, b):
            return (lambda k: hi[:, k, a:b], lambda k: lo[:, k, a:b])

        def bias(n, m):
            o = NB[n][0] + m * P
            return brow[0:2, o:o + P]

        with ExitStack() as st:
            def stage(name, shape):
                return st.enter_context(nc.sbuf_tensor("st_" + name, shape, F32))
            s_w = {"a_wx": hs1[:, :, 0:G4], "a_wh": hs1[:, :, G4:2 * G4], "wq": hs1[:, :, 2 * G4:2 * G4 + D],
                   "wk": hs1[:, :, 2 * G4 + D:2 * G4 + 2 * D], "e_wx": xs[:, :, 0:G4], "e_wh": xs[:, :, G4:2 * G4]}
            free = {"wv": prod[:, 0], "wo": prod[:, 1], "c_wx": sw[:, 0], "c_wh": sv[:, 0], "f_wm": prod[:, 2],
                    "f_wo": rt[:, 0:4].rearrange("p a h e -> p (a h e)")}
            s_w |= {n: ap.rearrange("p (k n) -> p k n", k=KT) for n, ap in free.items()}
            s_b2 = rt[:, 4:6].rearrange("p a h e -> p (a h e)")
            s_w1 = hm32[:, :, :].rearrange("p a (e i) -> p (a e) i", i=P)
            s_es = stage("es", [P, E1])
            s_w2 = prod[:, 3].rearrange("p (e d) -> p e d", d=HD)
            s_b = stage("b", [1, BR])
            s_bl = st.enter_context(nc.sbuf_tensor("st_bl", [1, BR], F16))
            s_cond = stage("cond", [P, KT, B])
            s_c2 = stage("c2", [P, KT, B])
            loaded = st.enter_context(nc.semaphore("loaded"))
            loaded_const = st.enter_context(nc.semaphore("loaded_const"))
            loaded_x = st.enter_context(nc.semaphore("loaded_x"))
            xs_cleared = st.enter_context(nc.semaphore("xs_cleared"))
            hi_done = st.enter_context(nc.semaphore("hi_done"))
            lo_done = st.enter_context(nc.semaphore("lo_done"))
            row_done = st.enter_context(nc.semaphore("row_done"))
            row_sent = st.enter_context(nc.semaphore("row_sent"))
            cleared = st.enter_context(nc.semaphore("cleared"))
            keep_set = st.enter_context(nc.semaphore("keep_set"))
            cond_2 = st.enter_context(nc.semaphore("cond_2"))
            gates = ("a_wx", "a_wh", "e_wx", "e_wh")

            def jobs():
                for n, w in names:
                    if n in gates:
                        f = S if n.endswith("wx") else S / 2
                        yield s_w[n][:, :, 0:3 * D], w_hi[n][:, :, 0:3 * D], w_lo[n][:, :, 0:3 * D], f
                        yield s_w[n][:, :, 3 * D:G4], w_hi[n][:, :, 3 * D:G4], w_lo[n][:, :, 3 * D:G4], 2 * f
                    else:
                        f = S / 2 if n in ("wq", "wk", "wv") else S
                        yield s_w[n][:, :, :], w_hi[n][:, :, :], w_lo[n][:, :, :], f
                yield s_b2, b2_hi[:, :], b2_lo[:, :], S
                yield s_w2, w2_hi[:, :, :], w2_lo[:, :, :], S
                yield s_w1, w1s[:, :, :], None, S
                yield s_es[:, :], es[:, :], None, S
                yield s_cond[:, :, :], h0c[:, 0], h0c[:, 1], 1.0
                yield s_cond[:, :, :], h0e[:, 0], h0e[:, 1], 2.0

            def bias_jobs():
                for n in ("a_b", "e_b"):
                    o = NB[n][0]
                    yield o, o + 3 * D, S
                    yield o + 3 * D, o + G4, 2 * S
                yield 2 * G4, BR, S

            NJ = len(list(jobs()))
            loads = [(s_w[n], t[n].rearrange("(k p) n -> p k n", p=P)) for n, _ in names]
            loads += [(s_b2, t["f_b2"])]
            loads += [(s_w1[r * HD:(r + 1) * HD, :, :], t["f_w1"].rearrange("e d i -> d e i")) for r in range(4)]
            loads += [(s_es[r * HD:(r + 1) * HD, :], t["f_emb"]) for r in range(4)]
            loads += [(s_w2, t["f_w2"].rearrange("e i o -> i e o")), (b1[:, :], t["f_b1"]),
                      (s_cond[:, :, :], t["cond"].rearrange("(k p) b -> p k b", p=P))]
            for n, (o, w) in NB.items():
                loads.append((s_b[0:1, o:o + w], t[n].rearrange("(a n) -> a n", a=1)))
            consts = [(ident[:, :], t["k_ident"]), (gsum[:, :], t["k_gsum"]), (wcos[:, :], t["k_wcos"]),
                      (iota[:, :], t["k_iota"])]

            block = st.enter_context(nc.Block())

            @block.sync
            def _(sp):
                for dst, src in loads[0::2]:
                    sp.dma_start(dst, src).then_inc(loaded, 16)
                for dst, src in consts:
                    sp.dma_start(dst, src).then_inc(loaded_const, 16)
                sp.wait_ge(row_done, 5)
                sp.dma_start(brow[1:2, :], s_bl[0:1, :]).then_inc(row_sent, 16)
                sp.wait_ge(row_sent, 16)
                sp.wait_ge(loaded_const, 16 * len(consts))

            @block.scalar
            def _(act):
                for dst, src in loads[1::2]:
                    act.dma_start(dst, src).then_inc(loaded, 16)
                act.wait_ge(loaded, 16 * len(loads))
                for src, hi, _lo, f in jobs():
                    act.activation(hi, src, ACT.Copy, scale=f).then_inc(hi_done, 1)
                for a, b, f in bias_jobs():
                    act.activation(brow[0:1, a:b], s_b[0:1, a:b], ACT.Copy, scale=f).then_inc(hi_done, 1)

            @block.vector
            def _(dve):
                for tl in (a_hl, c_hl, e_hl, a_hh, c_hh, e_hh, x2_h, x2_l, x1_h, x1_l, cc_h, cc_l):
                    dve.memset(tl[:, :, :], 0.0).then_inc(cleared, 1)
                for tl in (ca, ce, acc):
                    dve.memset(tl[:, :], 0.0).then_inc(cleared, 1)
                dve.memset(ones2[:, :], 1.0).then_inc(cleared, 1)
                dve.memset(keep[:, 0:3:2, :], 1.0).then_inc(keep_set, 1)
                dve.memset(keep[:, 1:4:2, :], 0.0).then_inc(keep_set, 1)
                dve.wait_ge(keep_set, 2)
                for row, it in ((0, 1), (2, LAG - 1)):
                    dve.memset(keep[:, row, it:it + 1], 0.0).then_inc(keep_set, 1)
                    dve.memset(keep[:, row + 1, it:it + 1], 1.0).then_inc(keep_set, 1)
                for n, (src, hi, lo, f) in enumerate(jobs()):
                    dve.wait_ge(hi_done, n + 1)
                    if lo is not None:
                        dve.scalar_tensor_tensor(out=lo, in0=src, scalar=f, in1=hi, op0=ALU.mult,
                                                 op1=ALU.subtract).then_inc(lo_done, 1)
                    else:
                        for a in (HD, 3 * HD):
                            dve.scalar_tensor_tensor(out=hi[a:a + HD], in0=src[a:a + HD], scalar=f,
                                                     in1=hi[a:a + HD], op0=ALU.mult,
                                                     op1=ALU.subtract).then_inc(lo_done, 1)
                for n, (a, b, f) in enumerate(bias_jobs()):
                    dve.wait_ge(hi_done, NJ + n + 1)
                    dve.scalar_tensor_tensor(out=s_bl[0:1, a:b], in0=s_b[0:1, a:b], scalar=f, in1=brow[0:1, a:b],
                                             op0=ALU.mult, op1=ALU.subtract).then_inc(row_done, 1)
                dve.wait_ge(lo_done, NJ + 2)
                dve.wait_ge(cleared, 22)
                dve.tensor_copy(a_hh[:, :, CW - B:CW], h0e[:, 0]).then_inc(lo_done, 1)
                dve.tensor_copy(a_hl[:, :, CW - B:CW], h0e[:, 1]).then_inc(lo_done, 1)

            @block.gpsimd
            def _(pool):
                for tl in (hm_h, hm_l):
                    pool.memset(tl[:, :, :], 0.0).then_inc(cleared, 1)
                pool.memset(tst[:, :], 0.0).then_inc(cleared, 1)
                pool.memset(wts[:, :, :], 0.0).then_inc(cleared, 1)
                pool.memset(ac_h[:, :, :], 0.0).then_inc(cleared, 1)
                pool.memset(ac_l[:, :, :], 0.0).then_inc(cleared, 1)
                pool.wait_ge(lo_done, 8)
                pool.dma_start(xs[:, :, LAG * CW:(LAG + NCH) * CW],
                               t["x"].rearrange("(k p) n -> p k n", p=P)).then_inc(loaded_x, 16)
                pool.memset(xs[:, :, 0:LAG * CW], 0.0).then_inc(xs_cleared, 1)
                pool.memset(xs[:, :, (LAG + NCH) * CW:], 0.0).then_inc(xs_cleared, 1)
                pool.wait_ge(lo_done, NJ + 2)
                pool.memset(hm32[:, :, :], 0.0).then_inc(cleared, 1)
                pool.wait_ge(loaded_x, 16)

        a_pe, a_act, a_part, a_cell, a_tanh = (sem("a_" + n) for n in ("pe", "act", "part", "cell", "tanh"))
        e_pe, e_act, e_part, e_cell, e_tanh = (sem("e_" + n) for n in ("pe", "act", "part", "cell", "tanh"))
        a_hi, a_h32, a_lo = (sem("a_" + n) for n in ("hi", "h32", "lo"))
        e_hi, e_h32, e_lo = (sem("e_" + n) for n in ("hi", "h32", "lo"))
        c_pe, c_hi, c_32, c_lo = (sem("c_" + n) for n in ("pe", "hi", "32", "lo"))
        x_split, ac_copied, cc_copied, c_reset, e_reset = (
            sem(n) for n in ("x_split", "ac_copied", "cc_copied", "c_reset", "e_reset"))
        z_full, z_free, xy_full = sem("z_full"), sem("z_free"), sem("xy_full")
        w_full, w_free = sem("w_full"), sem("w_free")
        g_hi, g_32, g_lo = sem("g_hi"), sem("g_32"), sem("g_lo")
        acc_done = sem("acc_done")
        prod_done, s_read, b_fin, x1_done, x1_split, x1_kept = (
            sem(n) for n in ("prod_done", "s_read", "b_fin", "x1_done", "x1_split", "x1_kept"))
        tk_split, tokens_in, t_copied, route, route_t, wt_split = (
            sem(n) for n in ("tk_split", "tokens_in", "t_copied", "route", "route_t", "wt_split"))
        TIN = 16 * 16
        om_split, x2_done, x2_split, x2_sent = (sem(n) for n in ("om_split", "x2_done", "x2_split", "x2_sent"))
        ROUTE = 2 * NH + 12
        CHOSEN = 2 * NH + 2
        per = [(a_pe, 16), (a_act, 16), (a_part, 32), (a_cell, 16), (a_tanh, 16), (a_hi, 16), (a_h32, 16), (a_lo, 16),
               (e_pe, 16), (e_act, 16), (e_part, 32), (e_cell, 16), (e_tanh, 16), (e_hi, 16), (e_h32, 16), (e_lo, 16),
               (c_pe, 16), (c_hi, 16), (c_32, 16), (c_lo, 16), (x_split, 2), (ac_copied, 2), (cc_copied, 2),
               (c_reset, 4), (e_reset, 6), (z_full, Z_USES), (z_free, Z_USES), (w_full, 16), (w_free, 17),
               (xy_full, 31), (g_hi, 32),
               (g_32, 32), (g_lo, 32), (acc_done, 17), (prod_done, 4), (s_read, 20),
               (b_fin, 3), (x1_done, 1), (x1_split, 1), (x1_kept, 1), (tk_split, 1),
               (tokens_in, TIN), (t_copied, 1), (wt_split, 1),
               (route, ROUTE), (route_t, 1), (om_split, 1), (x2_done, 1), (x2_split, 1), (x2_sent, 16)]

        def project_half(pe, name, bank, half, xh, xl):
            first = True
            for m in range(8):
                out = bank[half][:, :, m, :]
                pe.matmul(out, bias(name + "_b", m), ones2[0:2, 0:HALF], start=first, stop=False,
                          skip_group_check=True)
                first = False
                last = split_matmul(pe, out, wh(name + "_wx", m), cols(xh, xl, half * HALF, (half + 1) * HALF), False)
            return last

        def project_c(pe):
            for m in range(KT):
                pe.matmul(g_c[:, :, m, :], bias("c_b", m), ones2[0:2, 0:CW], start=(m == 0), stop=False,
                          skip_group_check=True)
                last = split_matmul(pe, g_c[:, :, m, :], wh("c_wx", m), cols(x1_h, x1_l, 0, CW), False)
            return last

        with ExitStack() as st:
            pad_sent = st.enter_context(nc.semaphore("pad_sent1"))
            x_first = st.enter_context(nc.semaphore("x_first"))
            primed = st.enter_context(nc.semaphore("primed"))
            block = st.enter_context(nc.Block())

            @block.vector
            def _(dve):
                first = xs[:, :, LAG * CW:(LAG + 1) * CW]
                dve.tensor_copy(x_h[:, :, :], first).then_inc(x_first, 1)
                dve.wait_ge(x_first, 1)
                dve.tensor_tensor(x_l[:, :, :], first, x_h[:, :, :], ALU.subtract).then_inc(x_first, 1)

            @block.tensor
            def _(pe):
                pe.wait_ge(x_first, 2)
                project_half(pe, "a", g_a, 0, x_h, x_l)
                project_half(pe, "e", g_e, 0, x2_h, x2_l)
                project_c(pe)
                for h in range(2):
                    pe.matmul(xy[h][:, :], w1s[:, 0, :], tst[:, 0:512], start=True, stop=True)
                pe.matmul(z[:, :], w1s[:, 0, :], tst[:, 0:512], start=True, stop=True).then_inc(primed, 1)

            @block.sync
            def _(sp):
                for s, n in per:
                    sp.sem_inc(s, n)
                sp.dma_start(x2d[:, :, NI * CW:(NI + 1) * CW], xs[:, :, 0:CW]).then_inc(pad_sent, 16)
                sp.wait_ge(pad_sent, 16)

        block = ctx.enter_context(nc.Block())
        CUTS = (0, M_FIRST, E_FIRST, NCH, M_LAST + 1, NI)
        RANGES = list(zip(CUTS, CUTS[1:]))

        @block.sync
        def _(sp):
            with sp.Fori(0, NI) as i:
                sp.wait_ge(z_free, at(i, Z_USES, z_use(9) + 1))
                for r, part in enumerate((tk_h, tk_h, tk_l, tk_l)):
                    for q in range(P // HD):
                        dst = tnew[r * HD:(r + 1) * HD, :].rearrange("p (k q n) -> p k q n", k=KT, n=CW)[:, :, q, :]
                        sp.dma_start(dst, part[q * HD:(q + 1) * HD, :, :]).then_inc(tokens_in, 16)
                sp.wait_ge(x2_done, at(i, 1, 1))
                sp.dma_start(x2d[:, :, bass.ds(i * CW, CW)], x2[:, :, :]).then_inc(x2_sent, 16)
            sp.wait_ge(x2_sent, 16 * (NI + 1))

        @block.tensor
        def _(pe):
            def lstm_step(i, slot, name, bank, hh, hl, hi_sem, lo_sem, done):
                prev = (slot - 1) % C * B
                out = bank[slot // 8]
                pe.wait_ge(hi_sem, at(i, C, slot))
                for m in range(8):
                    for k in range(KT):
                        for wt in (w_hi, w_lo):
                            pe.matmul(out[:, slot % 8, m, :], wt[name][:, k, m * P:(m + 1) * P],
                                      hh[:, k, prev:prev + B], start=False, stop=False, skip_group_check=True)
                pe.wait_ge(lo_sem, at(i, C, slot))
                for m in range(8):
                    for k in range(KT):
                        last = pe.matmul(out[:, slot % 8, m, :], w_hi[name][:, k, m * P:(m + 1) * P],
                                         hl[:, k, prev:prev + B], start=False, stop=(k == KT - 1),
                                         skip_group_check=True)
                last.then_inc(done, 1)

            def rnn_step(i, slot):
                s = (slot - C0) % C
                prev = (s - 1) % C * B
                pe.wait_ge(c_hi, at(i, C, slot))
                pe.wait_ge(c_32, at(i, C, slot))
                for m in range(KT):
                    for k in range(KT):
                        for wt in (w_hi, w_lo):
                            pe.matmul(g_c[:, s, m, :], wt["c_wh"][:, k, m * P:(m + 1) * P],
                                      c_hh[:, k, prev:prev + B], start=False, stop=False, skip_group_check=True)
                pe.wait_ge(c_lo, at(i, C, slot))
                for m in range(KT):
                    for k in range(KT):
                        last = pe.matmul(g_c[:, s, m, :], w_hi["c_wh"][:, k, m * P:(m + 1) * P],
                                         c_hl[:, k, prev:prev + B], start=False, stop=(k == KT - 1),
                                         skip_group_check=True)
                last.then_inc(c_pe, 1)

            def misc(i, slot, a_on, e_on, m_on):
                if slot == 0:
                    pe.wait_ge(ac_copied, at(i if a_on else NCH, 2, 0))
                pe_z = at(i, Z_USES, z_use(slot))
                if m_on and out_bank(slot - 1, a_on, e_on) is z:
                    pe.wait_ge(w_free, at(i - M_FIRST, C, slot + 1))
                elif slot == 0 and not a_on:
                    pe.wait_ge(w_free, at(M_LAST + 1 - M_FIRST, C, 1))
                if slot in (0, 1):
                    pe.wait_ge(z_free, pe_z)
                    for j, n in enumerate(("wq", "wk") if slot == 0 else ("wv",)):
                        for m in range(KT):
                            o = (2 * j + m) * P
                            last = split_matmul(pe, z[:, o:o + P], wh(n, m), cols(ac_h, ac_l, 0, CW),
                                                start=(o == 0), last=True)
                elif 2 <= slot <= 5:
                    pe.wait_ge(prod_done, at(i, 4, slot - 1))
                    pe.wait_ge(z_free, pe_z)
                    last = pe.matmul(z[:, :], gsum[:, :], prod[:, slot - 2, :], start=True, stop=True)
                elif slot == 7:
                    pe.wait_ge(b_fin, at(i, 3, 3))
                    pe.wait_ge(z_free, pe_z)
                    for m in range(KT):
                        last = split_matmul(pe, z[:, m * P:(m + 1) * P], wh("wo", m), cols(at_h, at_l, 0, CW),
                                            start=(m == 0), last=True)
                elif slot == 9:
                    pe.wait_ge(cc_copied, at(i, 2, 2))
                    pe.wait_ge(z_free, pe_z)
                    for m in range(KT):
                        o = z[:, m * P:(m + 1) * P]
                        pe.matmul(o, bias("f_bm", m), ones2[0:2, :], start=(m == 0), stop=False,
                                  skip_group_check=True)
                        last = split_matmul(pe, o, wh("f_wm", m), cols(cc_h, cc_l, 0, CW), False, last=True)
                elif slot == 11:
                    pe.wait_ge(tokens_in, at(i, TIN, TIN))
                    pe.wait_ge(z_free, pe_z)
                    for h in range(NH):
                        last = pe.matmul(z[:, h * E1:(h + 1) * E1], tnew[:, h * CW:(h + 1) * CW], es[:, :],
                                         start=(h == 0), stop=True, skip_group_check=True)
                elif slot == 12:
                    pe.wait_ge(route, at(i, ROUTE, 0))
                    pe.wait_ge(z_free, pe_z)
                    last = pe.matmul(z[:, 0:P], wts[:, :, :].rearrange("p h e -> p (h e)"), ident[:, :],
                                     is_transpose=True, start=True, stop=True, skip_group_check=True)
                elif slot == 13:
                    if m_on:
                        pe.wait_ge(acc_done, at(i - M_FIRST, E1, 14))
                    pe.wait_ge(z_free, pe_z)
                    for m in range(KT):
                        pe.matmul(z[:, m * P:(m + 1) * P], acc[:, m * P:(m + 1) * P], ident[:, :],
                                  is_transpose=True, start=(m == 0), stop=False, skip_group_check=True)
                    for m in range(KT):
                        for b2, wt in ((b2_hi, wt_h), (b2_lo, wt_h), (b2_hi, wt_l)):
                            last = pe.matmul(z[:, m * P:(m + 1) * P], b2[:, m * P:(m + 1) * P], wt[:, :],
                                             start=False, stop=(wt is wt_l), skip_group_check=True)
                elif slot == 14:
                    pe.wait_ge(om_split, at(i, 1, 1))
                    pe.wait_ge(z_free, pe_z)
                    for m in range(KT):
                        o = z[:, m * P:(m + 1) * P]
                        pe.matmul(o, bias("f_bo", m), ones2[0:2, :], start=(m == 0), stop=False,
                                  skip_group_check=True)
                        last = split_matmul(pe, o, wh("f_wo", m), cols(om_h, om_l, 0, CW), False, last=True)
                last.then_inc(z_full, 1)

            def w1(i, slot, h):
                e = (slot - W1_0) % E1
                if slot == W1_0 and h == 0:
                    pe.wait_ge(t_copied, at(i, 1, 1))
                pe.wait_ge(g_hi, at(i - M_FIRST, 32, 2 * slot + 1 + h))
                pe.wait_ge(g_32, at(i - M_FIRST, 32, 2 * slot + 1 + h))
                pe.matmul(xy[h][:, :], w1s[:, e, :], tst[:, h * 512:(h + 1) * 512], start=True,
                          stop=True).then_inc(xy_full, 1)

            def w2(i, slot, a_on, e_on):
                e = (slot - W1_0 - 2) % E1
                b = (slot - 1) % 2
                pe.wait_ge(g_lo, at(i - M_FIRST, 32, 2 * slot))
                bank = out_bank(slot, a_on, e_on)
                pe.wait_ge(w_free, at(i - M_FIRST, C, slot + 1))
                if bank is z:
                    pe.wait_ge(z_free, at(i, Z_USES, z_use(slot + 1)))
                for h in range(NH):
                    o = bank[:, h * HD:(h + 1) * HD]
                    hh = hm_h[:, b, h * CW:(h + 1) * CW]
                    pe.matmul(o, hh, w2_hi[:, e, :], start=(h == 0), stop=False, skip_group_check=True)
                    pe.matmul(o, hh, w2_lo[:, e, :], start=False, stop=False, skip_group_check=True)
                    last = pe.matmul(o, hm_l[:, b, h * CW:(h + 1) * CW], w2_hi[:, e, :], start=False, stop=True,
                                     skip_group_check=True)
                last.then_inc(w_full, 1)

            for start, end in RANGES:
                a_on, e_on = start < NCH, start >= E_FIRST
                m_on = M_FIRST <= start <= M_LAST
                with pe.Fori(start, end) as i:
                    for slot in range(C):
                        if a_on:
                            lstm_step(i, slot, "a_wh", g_a, a_hh, a_hl, a_hi, a_lo, a_pe)
                        if m_on:
                            w1(i, slot - 1, 1)
                        if slot == 2 and a_on:
                            pe.wait_ge(a_act, at(i, C, 0))
                            project_half(pe, "a", g_a, 1, x_h, x_l)
                        if slot == 10 and a_on:
                            pe.wait_ge(x_split, at(i, 2, 2))
                            pe.wait_ge(a_act, at(i, C, 8))
                            project_half(pe, "a", g_a, 0, x_h, x_l)
                        if slot in MISC and slot != 11:
                            misc(i, slot, a_on, e_on, m_on)
                        if slot == 0 and e_on:
                            pe.wait_ge(e_reset, at(i - E_FIRST, 6, 0))
                        if e_on:
                            lstm_step(i - E_FIRST, slot, "e_wh", g_e, e_hh, e_hl, e_hi, e_lo, e_pe)
                        if slot == 4 and e_on:
                            pe.wait_ge(e_act, at(i - E_FIRST, C, 0))
                            project_half(pe, "e", g_e, 1, x2_h, x2_l)
                        if slot == 15 and e_on:
                            pe.wait_ge(x2_split, at(i, 1, 1))
                            pe.wait_ge(e_act, at(i - E_FIRST, C, 8))
                            project_half(pe, "e", g_e, 0, x2_h, x2_l)
                        if slot == C0:
                            pe.wait_ge(c_reset, at(i, 4, 4))
                        rnn_step(i, slot)
                        if slot == 11:
                            misc(i, slot, a_on, e_on, m_on)
                        if m_on:
                            w1(i, slot, 0)
                            w2(i, slot, a_on, e_on)
                        if slot == C0 - 1:
                            pe.wait_ge(x1_split, at(i, 1, 1))
                            pe.wait_ge(c_hi, at(i, C, C0))
                            pe.wait_ge(c_32, at(i, C, C0))
                            project_c(pe)

        @block.scalar
        def _(act):
            def gates(i, slot, bank, g, mm, done):
                act.wait_ge(mm, at(i, C, slot + 1))
                act.activation(g[:, :], bank[slot // 8][:, slot % 8].rearrange("p m b -> p (m b)"), ACT.Tanh,
                               scale=1.0 / (2 * S)).then_inc(done, 1)

            def cell_tanh(i, slot, c, tc, cell, done):
                act.wait_ge(cell, at(i, C, slot + 1))
                act.activation(tc[:, :], c[:, :], ACT.Tanh, scale=0.5).then_inc(done, 1)

            def gelu(i, slot, h, hi):
                e = (slot - W1_0 - 1) % E1
                b = slot % 2
                dst = hm_h if hi else hm32
                if hi:
                    act.wait_ge(xy_full, at(i - M_FIRST, 32, 2 * slot - 1 + h))
                    if h == 0:
                        act.wait_ge(w_full, at(i - M_FIRST, C, slot))
                act.activation(dst[:, b, h * 512:(h + 1) * 512], xy[h][:, :], ACT.Gelu, bias=b1[:, e:e + 1],
                               scale=1.0 / S).then_inc(g_hi if hi else g_32, 1)

            def misc(i, slot):
                act.wait_ge(z_full, at(i, Z_USES, z_use(slot) + 1))
                if slot == 0:
                    act.activation(qk[:, :, :, :].rearrange("p a k n -> p (a k n)"), z[:, :], ACT.Relu,
                                   scale=1.0 / S).then_inc(z_free, 1)
                else:
                    act.activation(vv[:, :, :].rearrange("p k n -> p (k n)"), z[:, 0:KT * CW], ACT.Copy,
                                   scale=1.0 / S).then_inc(z_free, 1)

            act.activation(rstc[:, :], ca[:, :], ACT.Gelu)
            for start, end in RANGES:
                a_on, e_on = start < NCH, start >= E_FIRST
                m_on = M_FIRST <= start <= M_LAST
                with act.Fori(start, end) as i:
                    for slot in range(C):
                        if a_on:
                            gates(i, slot, g_a, ga, a_pe, a_act)
                        if m_on:
                            gelu(i, slot, 0, True)
                        if a_on:
                            cell_tanh(i, slot, ca, ta, a_cell, a_tanh)
                        if slot in (0, 1):
                            misc(i, slot)
                        if m_on:
                            gelu(i, slot, 0, False)
                            gelu(i, slot, 1, True)
                        if e_on:
                            gates(i - E_FIRST, slot, g_e, ge, e_pe, e_act)
                        if m_on:
                            gelu(i, slot, 1, False)
                        s = (slot - C0) % C
                        act.wait_ge(c_pe, at(i, C, slot + 1))
                        act.activation(c_hh[:, :, s * B:(s + 1) * B], g_c[:, s, :, :], ACT.Tanh,
                                       scale=1.0 / S).then_inc(c_hi, 1)
                        act.activation(c32[:, :].rearrange("p (k b) -> p k b", b=B), g_c[:, s, :, :], ACT.Tanh,
                                       scale=1.0 / S).then_inc(c_32, 1)
                        if e_on:
                            cell_tanh(i - E_FIRST, slot, ce, te_, e_cell, e_tanh)
                        if slot == 12:
                            act.wait_ge(route, at(i, ROUTE, NH + 1))
                            act.activation(rt[:, 1, :, :], rt[:, 0, :, :], ACT.Tanh, scale=0.5).then_inc(route_t, 1)

        @block.gpsimd
        def _(pool):
            for start, end in RANGES:
                m_on = M_FIRST <= start <= M_LAST
                with pool.Fori(start, end) as i:
                    for slot in range(C):
                        b = slot % 2
                        if 1 <= slot <= 4:
                            p = slot - 1
                            m, s0 = p // 2, (p % 2) * HALF
                            if p == 0:
                                pool.wait_ge(z_free, at(i, Z_USES, 1))
                            q3 = qk[:, 0, m, s0:s0 + HALF].rearrange("p (t l) -> p t l", l=B)
                            k3 = qk[:, 1, m, s0:s0 + HALF].rearrange("p (t l) -> p t l", l=B)
                            pool.tensor_tensor(prod[:, p, :].rearrange("p (t l m) -> p t l m", l=B, m=B),
                                               q3.unsqueeze(3).to_broadcast([P, 8, B, B]),
                                               k3.unsqueeze(2).to_broadcast([P, 8, B, B]),
                                               ALU.mult).then_inc(prod_done, 1)
                        for h in range(2) if m_on else ():
                            pool.wait_ge(g_hi, at(i - M_FIRST, 32, 2 * slot + 1 + h))
                            pool.wait_ge(g_32, at(i - M_FIRST, 32, 2 * slot + 1 + h))
                            r = slice(h * 512, (h + 1) * 512)
                            pool.tensor_tensor(hm_l[:, b, r], hm32[:, b, r], hm_h[:, b, r],
                                               ALU.subtract).then_inc(g_lo, 1)
                        if slot == 7:
                            pool.wait_ge(x1_done, at(i, 1, 1))
                            pool.tensor_copy(xs[:, :, bass.ds((i + (LAG - 1)) * CW, CW)], x1[:, :, :]).then_inc(x1_kept, 1)

        @block.vector
        def _(dve):
            def cell(i, slot, g, pt, c, act_sem, part, cell_sem):
                dve.wait_ge(act_sem, at(i, C, slot + 1))
                dve.scalar_tensor_tensor(out=pt[:, 0, :], in0=g[:, 16:32], scalar=1.0, in1=c[:, :], op0=ALU.add,
                                         op1=ALU.mult).then_inc(part, 1)
                dve.scalar_tensor_tensor(out=pt[:, 1, :], in0=g[:, 0:16], scalar=1.0, in1=g[:, 48:64], op0=ALU.add,
                                         op1=ALU.mult).then_inc(part, 1)
                dve.wait_ge(part, at(i, 32, 2 * slot + 2))
                dve.scalar_tensor_tensor(out=c[:, :], in0=pt[:, 0, :], scalar=0.5, in1=pt[:, 1, :], op0=ALU.mult,
                                         op1=ALU.add).then_inc(cell_sem, 1)

            def state(i, slot, g, tc, f, hh, hl, tanh_sem, hi_sem, h32_sem, lo_sem):
                k2 = "p (k b) -> p k b"
                o3, t3, f3 = (v.rearrange(k2, b=B) for v in (g[:, 32:48], tc[:, :], f[:, :]))
                r = slice(slot * B, (slot + 1) * B)
                dve.wait_ge(tanh_sem, at(i, C, slot + 1))
                dve.scalar_tensor_tensor(out=hh[:, :, r], in0=o3, scalar=1.0, in1=t3, op0=ALU.add,
                                         op1=ALU.mult).then_inc(hi_sem, 1)
                dve.scalar_tensor_tensor(out=f3, in0=o3, scalar=1.0, in1=t3, op0=ALU.add,
                                         op1=ALU.mult).then_inc(h32_sem, 1)
                dve.wait_ge(hi_sem, at(i, C, slot + 1))
                dve.wait_ge(h32_sem, at(i, C, slot + 1))
                dve.tensor_tensor(hl[:, :, r], f3, hh[:, :, r], ALU.subtract).then_inc(lo_sem, 1)

            def combine(i, slot, a_on, e_on):
                e = (slot - W1_0 - 3) % E1
                dve.wait_ge(w_full, at(i - M_FIRST, C, slot))
                zz = out_bank(slot - 1, a_on, e_on)[:, 0:D].rearrange("p (h d) -> p h d", d=HD)
                w = wts[:, :, e].unsqueeze(2).to_broadcast([P, NH, HD])
                a3 = acc[:, :].rearrange("p (h d) -> p h d", d=HD)
                dve.wait_ge(acc_done, at(i - M_FIRST, E1, slot))
                if e == 0:
                    dve.wait_ge(route, at(i, ROUTE, ROUTE))
                dve.tensor_tensor(tmp[:, slot % 2, :, :], zz, w, ALU.mult).then_inc(w_free, 1)
                dve.wait_ge(w_free, at(i - M_FIRST, C, slot + 1))
                if e == 0:
                    dve.tensor_copy(a3, tmp[:, slot % 2, :, :]).then_inc(acc_done, 1)
                else:
                    dve.tensor_tensor(a3, a3, tmp[:, slot % 2, :, :], ALU.add).then_inc(acc_done, 1)

            def scores(i, slot):
                def z_wait():
                    dve.wait_ge(z_full, at(i, Z_USES, z_use(slot) + 1))
                z_read = at(i, Z_USES, z_use(slot) + 1)
                if 2 <= slot <= 5:
                    p = slot - 2
                    m, s0 = p // 2, (p % 2) * HALF
                    b = p % 2
                    z_wait()
                    dve.tensor_tensor(sw[:, b, :].rearrange("p (t c) -> p t c", c=B * B),
                                      z[:, :].rearrange("p (t c) -> p t c", c=B * B),
                                      wcos[:, :].unsqueeze(1).to_broadcast([P, 8, B * B]), ALU.mult).then_inc(z_free, 1)
                    dve.wait_ge(z_free, z_read)
                    dve.tensor_reduce(den[:, m, s0:s0 + HALF], sw[:, b, :].rearrange("p (c m) -> p c m", m=B), AX_X,
                                      ALU.add).then_inc(s_read, 1)

            def between_a(i, slot):
                if 3 <= slot <= 6:
                    p = slot - 3
                    m, s0 = p // 2, (p % 2) * HALF
                    dve.wait_ge(s_read, at(i, 20, 5 * p + 3))
                    dve.tensor_scalar(dmx[:, m, s0:s0 + HALF], den[:, m, s0:s0 + HALF], EPS_Z, None,
                                      ALU.max).then_inc(s_read, 1)
                    dve.wait_ge(s_read, at(i, 20, 5 * p + 4))
                    dve.reciprocal(rcd[:, m, s0:s0 + HALF], dmx[:, m, s0:s0 + HALF]).then_inc(s_read, 1)
                elif slot == 12:
                    for h in range(NH):
                        dve.max(m8[:, h, :], lg[:, h, :]).then_inc(route, 1)
                elif slot == 13:
                    dve.wait_ge(route_t, at(i, 1, 1))
                    dve.tensor_scalar(rt[:, 4, :, :], rt[:, 1, :, :], -1.0, 1.0, ALU.mult, ALU.add).then_inc(route, 1)
                    dve.wait_ge(route, at(i, ROUTE, CHOSEN + 4))
                    dve.reciprocal(rt[:, 5, :, :], rt[:, 4, :, :]).then_inc(route, 1)
                    dve.wait_ge(route, at(i, ROUTE, CHOSEN + 5))
                    dve.scalar_tensor_tensor(out=rt[:, 6, :, :], in0=rt[:, 1, :, :], scalar=1.0, in1=rt[:, 5, :, :],
                                             op0=ALU.add, op1=ALU.mult).then_inc(route, 1)

            def between_e(i, slot):
                if 2 <= slot <= 5:
                    p = slot - 2
                    m, s0 = p // 2, (p % 2) * HALF
                    b = p % 2
                    v3 = vv[:, m, s0:s0 + HALF].rearrange("p (t l) -> p t l", l=B)
                    dve.tensor_tensor(sv[:, b, :].rearrange("p (t l m) -> p t l m", l=B, m=B),
                                      sw[:, b, :].rearrange("p (t l m) -> p t l m", l=B, m=B),
                                      v3.unsqueeze(2).to_broadcast([P, 8, B, B]), ALU.mult).then_inc(s_read, 1)
                elif slot == 11:
                    dve.wait_ge(z_full, at(i, Z_USES, z_use(slot) + 1))
                    dve.tensor_scalar(lg[:, :, :].rearrange("p h e -> p (h e)"), z[:, 0:NH * E1], 1.0 / S, None,
                                      ALU.mult).then_inc(z_free, 1)
                elif slot == 12:
                    dve.wait_ge(route, at(i, ROUTE, NH))
                    dve.tensor_tensor(rt[:, 0, :, :], lg[:, :, :], m8[:, :, 0].unsqueeze(2).to_broadcast([P, NH, E1]),
                                      ALU.subtract).then_inc(route, 1)
                elif slot == 13:
                    dve.wait_ge(route, at(i, ROUTE, CHOSEN + 6))
                    dve.tensor_reduce(sm[:, 0, :], rt[:, 6, :, :], AX_X, ALU.add).then_inc(route, 1)
                    dve.tensor_tensor(rt[:, 7, :, :], rt[:, 6, :, :], rt[:, 2, :, :], ALU.mult).then_inc(route, 1)

            def late(i, slot, a_on):
                if 2 <= slot <= 5:
                    p = slot - 2
                    m, s0 = p // 2, (p % 2) * HALF
                    b = p % 2
                    dve.wait_ge(s_read, at(i, 20, 5 * p + 2))
                    dve.tensor_reduce(num[:, m, s0:s0 + HALF], sv[:, b, :].rearrange("p (c m) -> p c m", m=B), AX_X,
                                      ALU.add).then_inc(s_read, 1)
                elif slot == 8 and a_on:
                    nxt = xs[:, :, bass.ds((i + (LAG + 1)) * CW, CW)]
                    dve.tensor_scalar(x_h[:, :, :], nxt, 1.0, None, ALU.mult).then_inc(x_split, 1)
                    dve.wait_ge(x_split, at(i, 2, 1))
                    dve.tensor_tensor(x_l[:, :, :], nxt, x_h[:, :, :], ALU.subtract).then_inc(x_split, 1)
                elif slot == 12:
                    for h in range(NH):
                        dve.max_index(i8[:, h, :], m8[:, h, :], lg[:, h, :]).then_inc(route, 1)
                    dve.wait_ge(route, at(i, ROUTE, 2 * NH + 1))
                    dve.tensor_copy(idf[:, :, :], i8[:, :, 0:2]).then_inc(route, 1)
                    dve.wait_ge(route, at(i, ROUTE, CHOSEN))
                    io = iota[:, :].unsqueeze(1).to_broadcast([P, NH, E1])
                    for j in range(2):
                        dve.tensor_tensor(rt[:, 2 + j, :, :], io, idf[:, :, j].unsqueeze(2).to_broadcast([P, NH, E1]),
                                          ALU.is_equal).then_inc(route, 1)
                    dve.wait_ge(route, at(i, ROUTE, CHOSEN + 2))
                    dve.tensor_tensor(rt[:, 2, :, :], rt[:, 2, :, :], rt[:, 3, :, :], ALU.add).then_inc(route, 1)
                elif slot == 13:
                    dve.wait_ge(route, at(i, ROUTE, CHOSEN + 8))
                    dve.reciprocal(sm[:, 1, :], sm[:, 0, :]).then_inc(route, 1)
                    dve.wait_ge(route, at(i, ROUTE, CHOSEN + 9))
                    dve.tensor_tensor(wts[:, :, :], rt[:, 7, :, :], sm[:, 1, :].unsqueeze(2).to_broadcast([P, NH, E1]),
                                      ALU.mult).then_inc(route, 1)

            def misc(i, slot, m_on):
                def z_wait():
                    dve.wait_ge(z_full, at(i, Z_USES, z_use(slot) + 1))
                z_read = at(i, Z_USES, z_use(slot) + 1)
                if slot == 6:
                    dve.wait_ge(s_read, at(i, 20, 20))
                    dve.tensor_tensor(att[:, :, :], num[:, :, :], rcd[:, :, :], ALU.mult).then_inc(b_fin, 1)
                    dve.wait_ge(b_fin, at(i, 3, 1))
                    dve.tensor_copy(at_h[:, :, :], att[:, :, :]).then_inc(b_fin, 1)
                    dve.wait_ge(b_fin, at(i, 3, 2))
                    dve.tensor_tensor(at_l[:, :, :], att[:, :, :], at_h[:, :, :], ALU.subtract).then_inc(b_fin, 1)
                elif slot == 7:
                    z_wait()
                    dve.wait_ge(x1_kept, at(i, 1, 0))
                    dve.scalar_tensor_tensor(out=x1[:, :, :], in0=z[:, 0:KT * CW].rearrange("p (k n) -> p k n", n=CW),
                                             scalar=1.0 / S, in1=xs[:, :, bass.ds((i + (LAG - 1)) * CW, CW)],
                                             op0=ALU.mult, op1=ALU.add).then_inc(x1_done, 1)
                    dve.wait_ge(x1_done, at(i, 1, 1))
                    dve.tensor_copy(x1_h[:, :, :], x1[:, :, :]).then_inc(z_free, 1)
                    dve.wait_ge(z_free, z_read)
                    dve.tensor_tensor(x1_l[:, :, :], x1[:, :, :], x1_h[:, :, :], ALU.subtract).then_inc(x1_split, 1)
                elif slot == 9:
                    z_wait()
                    z3 = z[:, 0:KT * CW].rearrange("p (k n) -> p k n", n=CW)
                    dve.tensor_scalar(tk_h[:, :, :], z3, 1.0 / S, None, ALU.mult).then_inc(tk_split, 1)
                    dve.wait_ge(tk_split, at(i, 1, 1))
                    dve.scalar_tensor_tensor(out=tk_l[:, :, :], in0=z3, scalar=1.0 / S, in1=tk_h[:, :, :], op0=ALU.mult,
                                             op1=ALU.subtract).then_inc(z_free, 1)
                elif slot == 11:
                    dve.wait_ge(tokens_in, at(i, TIN, TIN))
                    if m_on:
                        dve.wait_ge(xy_full, at(i - M_FIRST, 32, 2 * slot))
                    dve.tensor_copy(tst[:, :], tnew[:, :]).then_inc(t_copied, 1)
                elif slot == 12:
                    z_wait()
                    dve.tensor_copy(wt_h[:, :], z[:, 0:P]).then_inc(wt_split, 1)
                    dve.wait_ge(wt_split, at(i, 1, 1))
                    dve.tensor_tensor(wt_l[:, :], z[:, 0:P], wt_h[:, :], ALU.subtract).then_inc(z_free, 1)
                elif slot == 13:
                    z_wait()
                    z3 = z[:, 0:KT * CW].rearrange("p (k n) -> p k n", n=CW)
                    dve.tensor_scalar(om_h[:, :, :], z3, 1.0 / S, None, ALU.mult).then_inc(om_split, 1)
                    dve.wait_ge(om_split, at(i, 1, 1))
                    dve.scalar_tensor_tensor(out=om_l[:, :, :], in0=z3, scalar=1.0 / S, in1=om_h[:, :, :], op0=ALU.mult,
                                             op1=ALU.subtract).then_inc(z_free, 1)
                elif slot == 14:
                    z_wait()
                    dve.wait_ge(x2_sent, at(i, 16, 0))
                    dve.scalar_tensor_tensor(out=x2[:, :, :], in0=z[:, 0:KT * CW].rearrange("p (k n) -> p k n", n=CW),
                                             scalar=1.0 / S, in1=xs[:, :, bass.ds((i + (LAG - 3)) * CW, CW)],
                                             op0=ALU.mult, op1=ALU.add).then_inc(x2_done, 1)
                    dve.wait_ge(x2_done, at(i, 1, 1))
                    dve.tensor_copy(x2_h[:, :, :], x2[:, :, :]).then_inc(z_free, 1)
                    dve.wait_ge(z_free, z_read)
                    dve.tensor_tensor(x2_l[:, :, :], x2[:, :, :], x2_h[:, :, :], ALU.subtract).then_inc(x2_split, 1)

            for start, end in RANGES:
                a_on, e_on = start < NCH, start >= E_FIRST
                m_on = M_FIRST <= start <= M_LAST
                with dve.Fori(start, end) as i:
                    for slot in range(C):
                        if slot == 12:
                            dve.wait_ge(z_free, at(i, Z_USES, z_use(slot)))
                        if slot > 0 and m_on:
                            combine(i, slot, a_on, e_on)
                        if a_on:
                            cell(i, slot, ga, pa, ca, a_act, a_part, a_cell)
                        between_a(i, slot)
                        if a_on:
                            state(i, slot, ga, ta, fa, a_hh, a_hl, a_tanh, a_hi, a_h32, a_lo)
                        if 2 <= slot <= 5:
                            scores(i, slot)
                        elif slot in MISC[2:] or slot == 6:
                            misc(i, slot, m_on)
                        if slot == 15 and a_on:
                            dve.wait_ge(a_lo, at(i, C, C))
                            dve.tensor_copy(ac_h[:, :, :], a_hh[:, :, :]).then_inc(ac_copied, 1)
                            dve.tensor_copy(ac_l[:, :, :], a_hl[:, :, :]).then_inc(ac_copied, 1)
                        if slot == 0 and e_on:
                            dve.wait_ge(e_reset, at(i - E_FIRST, 6, 0))
                        if e_on:
                            cell(i - E_FIRST, slot, ge, pe_, ce, e_act, e_part, e_cell)
                        between_e(i, slot)
                        s = (slot - C0) % C
                        dve.wait_ge(c_hi, at(i, C, slot + 1))
                        dve.wait_ge(c_32, at(i, C, slot + 1))
                        dve.tensor_tensor(c_hl[:, :, s * B:(s + 1) * B], c32[:, :].rearrange("p (k b) -> p k b", b=B),
                                          c_hh[:, :, s * B:(s + 1) * B], ALU.subtract).then_inc(c_lo, 1)
                        if e_on:
                            state(i - E_FIRST, slot, ge, te_, fe, e_hh, e_hl, e_tanh, e_hi, e_h32, e_lo)
                        late(i, slot, a_on)
                        if slot == C0 - 1:
                            dve.wait_ge(c_lo, at(i, C, C0))
                            dve.tensor_copy(cc_h[:, :, :], c_hh[:, :, :]).then_inc(cc_copied, 1)
                            dve.tensor_copy(cc_l[:, :, :], c_hl[:, :, :]).then_inc(cc_copied, 1)
                            dve.wait_ge(cc_copied, at(i, 2, 2))
                            for j, hist in enumerate((c_hh, c_hl)):
                                dve.tensor_scalar(rst[:, j, :].rearrange("p (k b) -> p k b", b=B), hist[:, :, CW - B:CW],
                                                  keep[:, 0, bass.ds(i, 1)], None, ALU.mult).then_inc(c_reset, 1)
                            dve.wait_ge(c_reset, at(i, 4, 2))
                            for j, hist in enumerate((c_hh, c_hl)):
                                dve.scalar_tensor_tensor(out=hist[:, :, CW - B:CW], in0=h0c[:, j], scalar=keep[:, 1, bass.ds(i, 1)],
                                                         in1=rst[:, j, :].rearrange("p (k b) -> p k b", b=B), op0=ALU.mult,
                                                         op1=ALU.add).then_inc(c_reset, 1)
                        if slot == 15 and m_on:
                            combine(i + 1, 0, a_on, e_on)
                        if slot == 15 and e_on:
                            dve.wait_ge(e_lo, at(i - E_FIRST, C, C))
                            dve.tensor_tensor(hs1[:, :, bass.ds(i * CW, CW)], e_hh[:, :, :], e_hl[:, :, :],
                                              ALU.add).then_inc(e_reset, 1)
                            for j, hist in enumerate((e_hh, e_hl)):
                                dve.tensor_scalar(rst[:, 2 + j, :].rearrange("p (k b) -> p k b", b=B),
                                                  hist[:, :, CW - B:CW], keep[:, 2, bass.ds(i, 1)], None,
                                                  ALU.mult).then_inc(e_reset, 1)
                            dve.wait_ge(e_reset, at(i - E_FIRST, 6, 3))
                            for j, hist in enumerate((e_hh, e_hl)):
                                dve.scalar_tensor_tensor(out=hist[:, :, CW - B:CW], in0=h0e[:, j],
                                                         scalar=keep[:, 3, bass.ds(i, 1)],
                                                         in1=rst[:, 2 + j, :].rearrange("p (k b) -> p k b", b=B),
                                                         op0=ALU.mult, op1=ALU.add).then_inc(e_reset, 1)
                            dve.tensor_scalar(ce[:, :], ce[:, :], keep[:, 2, bass.ds(i, 1)], None,
                                              ALU.mult).then_inc(e_reset, 1)


BT = T
TT = T // P
HV = D // B
LN_EPS = 1e-5
DK = D // NH


def attention_two(nc, t, hs1, attd, m12_h, m12_l):
    with ExitStack() as ctx:
        def sb(name, shape, dt=F32):
            return ctx.enter_context(nc.sbuf_tensor(name, shape, dt))

        def sem(name):
            return ctx.enter_context(nc.semaphore(name))

        w_hi = {n: sb(n + "2_hi", [P, KT, D], F16) for n in ("q", "k", "v")}
        w_lo = {n: sb(n + "2_lo", [P, KT, D], F16) for n in ("q", "k", "v")}
        brow = sb("brow2", [2, 3 * D], F16)
        ones2 = sb("ones2b", [2, BT], F16)
        mean_w = sb("mean_w", [P, P])
        ident = sb("ident2", [P, P])
        gamma, beta = sb("gamma", [P, KT]), sb("beta", [P, KT])
        xn_h, xn_l = sb("xn_h", [P, KT, BT], F16), sb("xn_l", [P, KT, BT], F16)
        q_h, q_l, k_h, k_l = (sb(n, [P, KT, BT], F16) for n in ("q_h", "q_l", "k_h", "k_l"))
        v_h, v_l = sb("v_h", [P, TT, D], F16), sb("v_l", [P, TT, D], F16)
        first_exp = sb("first_exp", [P, 1])
        nmax = sb("nmax", [P, 2, TT])
        prob = sb("prob", [P, 2, TT, BT])
        sums, rinv = sb("sums", [P, NH, TT]), sb("rinv", [P, NH, TT])
        pt_h, pt_l = sb("pt_h", [P, 2, TT, BT], F16), sb("pt_l", [P, 2, TT, BT], F16)
        att = sb("att2", [P, NH, TT, HV])

        sc = [ctx.enter_context(nc.psum_tensor(f"sc{j}", [P, TT, BT], F32)) for j in range(2)]
        pt = [ctx.enter_context(nc.psum_tensor(f"pt{j}", [P, TT, BT], F32)) for j in range(2)]
        po = ctx.enter_context(nc.psum_tensor("po", [P, NH, TT, HV], F32))
        pq, pk, pv = (ctx.enter_context(nc.psum_tensor(n, [P, TT, BT], F32)) for n in ("pq", "pk", "pv"))

        with ExitStack() as st:
            s_q = st.enter_context(nc.sbuf_tensor("s_q", [P, KT, D], F32))
            s_k = st.enter_context(nc.sbuf_tensor("s_k", [P, KT, D], F32))
            s_v8 = st.enter_context(nc.sbuf_tensor("s_v8", [P, KT, D, 8], F32))
            s_v = st.enter_context(nc.sbuf_tensor("s_v", [P, KT, D], F32))
            s_b8 = st.enter_context(nc.sbuf_tensor("s_b8", [1, D, 8], F32))
            s_b = st.enter_context(nc.sbuf_tensor("s_b2", [1, 3 * D], F32))
            s_bl = st.enter_context(nc.sbuf_tensor("s_b2l", [1, 3 * D], F16))
            loaded, v_sum, hi_done, lo_done, row_sent = (
                st.enter_context(nc.semaphore("at_" + n)) for n in ("loaded", "v_sum", "hi", "lo", "row"))
            jobs = [(s_q[:, :, :], w_hi["q"][:, :, :], w_lo["q"][:, :, :]),
                    (s_k[:, :, :], w_hi["k"][:, :, :], w_lo["k"][:, :, :]),
                    (s_v[:, :, :], w_hi["v"][:, :, :], w_lo["v"][:, :, :]),
                    (s_b[0:1, :], brow[0:1, :], s_bl[0:1, :])]
            kp = "(k p) n -> p k n"
            loads = [(s_q[:, :, :], t["l_wq"].rearrange(kp, p=P)), (s_k[:, :, :], t["l_wk"].rearrange(kp, p=P)),
                     (s_v8[:, :, :, :].rearrange("p k n u -> p k (n u)"), t["l_wv"].rearrange(kp, p=P)),
                     (s_b8[:, :, :].rearrange("a n u -> a (n u)"), t["l_bv"].rearrange("(a n) -> a n", a=1)),
                     (s_b[0:1, 0:D], t["l_bq"].rearrange("(a n) -> a n", a=1)),
                     (s_b[0:1, D:2 * D], t["l_bk"].rearrange("(a n) -> a n", a=1)), (ident[:, :], t["k_ident"])]

            W = 512
            NJ = T * B // W
            dd = st.enter_context(nc.sbuf_tensor("ln_dd", [P, 2, KT, W], F32))
            sq, xg = (st.enter_context(nc.sbuf_tensor("ln_" + n, [P, KT, W], F32)) for n in ("sq", "xg"))
            va, root = (st.enter_context(nc.sbuf_tensor("ln_" + n, [P, 2, W], F32)) for n in ("va", "root"))
            y, yy = (st.enter_context(nc.sbuf_tensor("ln_" + n, [P, W], F32)) for n in ("y", "yy"))
            eps = st.enter_context(nc.sbuf_tensor("ln_eps", [P, 1], F32))
            mean = [b[:, :, :].rearrange("p s n -> p (s n)") for b in (pq, pk)]
            var = [b[:, :, :].rearrange("p s n -> p (s n)") for b in (pv, sc[0])]
            affine, ready, mean_pe, var_pe, d_ready, sq_ready, va_ready, root_ready, steps, scaled, kept = (
                st.enter_context(nc.semaphore("ln_" + n)) for n in
                ("affine", "ready", "mean_pe", "var_pe", "d_ready", "sq_ready", "va_ready", "root_ready", "steps",
                 "scaled", "kept"))
            NST = 4

            def x(j):
                return hs1[:, :, LAG * CW + j * W:LAG * CW + (j + 1) * W]

            block = st.enter_context(nc.Block())

            @block.sync
            def _(sp):
                sp.dma_start(gamma[:, :], t["l_gamma"]).then_inc(affine, 16)
                sp.dma_start(beta[:, :], t["l_beta"]).then_inc(affine, 16)
                for dst, src in loads:
                    sp.dma_start(dst, src).then_inc(loaded, 16)
                sp.wait_ge(lo_done, len(jobs))
                sp.dma_start(brow[1:2, :], s_bl[0:1, :]).then_inc(row_sent, 16)
                sp.wait_ge(row_sent, 16)

            @block.tensor
            def _(pe):
                def means(j):
                    if j >= 2:
                        pe.wait_ge(d_ready, j - 1)
                    for k in range(KT):
                        last = pe.matmul(mean[j % 2], mean_w[:, :], x(j)[:, k, :], start=(k == 0), stop=(k == KT - 1))
                    last.then_inc(mean_pe, 1)

                pe.wait_ge(ready, 2)
                means(0)
                for j in range(NJ):
                    if j + 1 < NJ:
                        means(j + 1)
                    pe.wait_ge(sq_ready, j + 1)
                    if j >= 2:
                        pe.wait_ge(va_ready, j - 1)
                    for k in range(KT):
                        last = pe.matmul(var[j % 2], mean_w[:, :], sq[:, k, :], start=(k == 0), stop=(k == KT - 1))
                    last.then_inc(var_pe, 1)

            @block.scalar
            def _(act):
                act.wait_ge(ready, 2)
                act.activation(first_exp[:, :], mean_w[:, 0:1], ACT.Sqrt)
                for j in range(NJ):
                    act.wait_ge(d_ready, j + 1)
                    if j >= 1:
                        act.wait_ge(var_pe, j)
                    act.activation(sq[:, :, :], dd[:, j % 2], ACT.Square).then_inc(sq_ready, 1)
                    act.wait_ge(var_pe, j + 1)
                    if j >= 2:
                        act.wait_ge(scaled, 2 * (j - 1))
                    act.activation(va[:, j % 2, :], var[j % 2], ACT.Relu, bias=eps[:, :]).then_inc(va_ready, 1)
                    act.wait_ge(va_ready, j + 1)
                    act.activation(root[:, j % 2, :], va[:, j % 2, :], ACT.Sqrt).then_inc(root_ready, 1)
                act.wait_ge(loaded, 16 * len(loads))
                act.wait_ge(v_sum, KT + 1)
                for src, hi, _lo in jobs:
                    act.activation(hi, src, ACT.Copy, scale=S).then_inc(hi_done, 1)

            @block.gpsimd
            def _(pool):
                pool.wait_ge(affine, 32)
                for j in range(NJ):
                    for k in range(KT):
                        pool.wait_ge(scaled, 2 * j + k + 1)
                        pool.tensor_scalar(x(j)[:, k, :], xg[:, k, :], beta[:, k:k + 1], None, ALU.add).then_inc(kept, 1)

            @block.vector
            def _(dve):
                def centre(j):
                    if j >= 2:
                        dve.wait_ge(sq_ready, j - 1)
                        dve.wait_ge(scaled, 2 * (j - 1))
                    dve.wait_ge(mean_pe, j + 1)
                    dve.tensor_tensor(dd[:, j % 2], x(j), mean[j % 2].unsqueeze(1).to_broadcast([P, KT, W]),
                                      ALU.subtract).then_inc(d_ready, 1)

                dve.memset(mean_w[:, :], 1.0 / D).then_inc(ready, 1)
                dve.memset(eps[:, :], 4 * LN_EPS).then_inc(ready, 1)
                dve.memset(ones2[:, :], 1.0)
                dve.memset(hs1[:, :, NI * CW:NI * CW + B], 0.0)
                dve.memset(sums[:, :, :], 1.0)
                for tl in (prob, pt_h, pt_l):
                    dve.memset(tl[:, :, :, :], 0.0)
                for tl in (v_h, v_l):
                    dve.memset(tl[:, :, :], 0.0)
                dve.wait_ge(affine, 32)
                centre(0)
                for j in range(NJ):
                    if j + 1 < NJ:
                        centre(j + 1)
                    v = va[:, j % 2, :]
                    dve.wait_ge(root_ready, j + 1)
                    if j >= 1:
                        dve.wait_ge(scaled, 2 * j)
                    dve.reciprocal(y[:, :], root[:, j % 2, :]).then_inc(steps, 1)
                    dve.wait_ge(steps, NST * j + 1)
                    dve.tensor_tensor(yy[:, :], y[:, :], y[:, :], ALU.mult).then_inc(steps, 1)
                    dve.wait_ge(steps, NST * j + 2)
                    dve.scalar_tensor_tensor(out=yy[:, :], in0=yy[:, :], scalar=-0.5, in1=v, op0=ALU.mult,
                                             op1=ALU.mult).then_inc(steps, 1)
                    dve.wait_ge(steps, NST * j + 3)
                    dve.scalar_tensor_tensor(out=y[:, :], in0=yy[:, :], scalar=1.5, in1=y[:, :], op0=ALU.add,
                                             op1=ALU.mult).then_inc(steps, 1)
                    dve.wait_ge(steps, NST * j + 4)
                    if j >= 1:
                        dve.wait_ge(kept, 2 * j)
                    for k in range(KT):
                        dve.scalar_tensor_tensor(out=xg[:, k, :], in0=dd[:, j % 2, k, :], scalar=gamma[:, k:k + 1],
                                                 in1=y[:, :], op0=ALU.mult, op1=ALU.mult).then_inc(scaled, 1)
                dve.wait_ge(loaded, 16 * len(loads))
                for k in range(KT):
                    dve.tensor_reduce(s_v[:, k, :], s_v8[:, k, :, :], AX_X, ALU.add).then_inc(v_sum, 1)
                dve.tensor_reduce(s_b[0:1, 2 * D:3 * D], s_b8[0:1, :, :], AX_X, ALU.add).then_inc(v_sum, 1)
                for n, (src, hi, lo) in enumerate(jobs):
                    dve.wait_ge(hi_done, n + 1)
                    dve.scalar_tensor_tensor(out=lo, in0=src, scalar=S, in1=hi, op0=ALU.mult,
                                             op1=ALU.subtract).then_inc(lo_done, 1)

        xn_steps, proj_pe = sem("xn_steps"), sem("proj_pe")
        proj_read, qk_split, v_split = sem("proj_read2"), sem("qk_split"), sem("v_split")
        sc_pe, neg_max, exp_done, t_pe, pt_hi, pt_lo, pv_pe = (
            sem(n) for n in ("sc_pe", "neg_max", "exp_done", "t_pe", "pt_hi", "pt_lo", "pv_pe"))
        r_done, att_done, att_sent = sem("r_done"), sem("att_done"), sem("att_sent")
        XN = 2
        per = [(xn_steps, XN), (proj_pe, 3), (proj_read, 3), (qk_split, 2),
               (v_split, 1), (sc_pe, NH), (neg_max, NH), (exp_done, 2 * NH), (t_pe, NH), (pt_hi, NH), (pt_lo, NH),
               (pv_pe, NH), (r_done, 1), (att_done, 1), (att_sent, 2 * 16 * TT)]
        with nc.Block() as block:
            @block.sync
            def _(sp):
                for s, n in per:
                    sp.sem_inc(s, n)

            @block.tensor
            def _(pe):
                for bank in (pt[0][:, :, :].rearrange("p s n -> p (s n)"), pt[1][:, :, :].rearrange("p s n -> p (s n)"),
                             po[:, :, :, :].rearrange("p h s j -> p (h s j)")):
                    for j in range(4):
                        pe.matmul(bank[:, j * P:(j + 1) * P], pt_h[:, 0, 0, 0:P], v_h[:, 0, 0:P], start=(j == 0),
                                  stop=True, skip_group_check=True)

        m_stage = [sb(f"m_stage{j}", [P, 3, HF]) for j in range(2)]
        m_staged = [sem(f"m_staged{j}") for j in range(2)]
        m_split = sem("m_split")
        block = ctx.enter_context(nc.Block())

        @block.gpsimd
        def _(pool):
            work = [(m, k, e) for m in range(2) for k in range(KT) for e in range(0, EA, 3)]

            def load(n):
                m, k, e = work[n]
                pool.dma_start(m_stage[n % 2][:, :, :], t[("m_w1", "m_w2")[m]][k * P:(k + 1) * P, e:e + 3, :])\
                    .then_inc(m_staged[n % 2], 16)

            load(0)
            load(1)
            for n, (m, k, e) in enumerate(work):
                hi, lo = m12_h[:, m, k, e:e + 3, :], m12_l[:, m, k, e:e + 3, :]
                pool.wait_ge(m_staged[n % 2], 16 * (n // 2 + 1))
                w = m_stage[n % 2][:, :, :]
                pool.tensor_scalar(w, w, S / 2, None, ALU.mult).then_inc(m_split, 1)
                pool.wait_ge(m_split, 3 * n + 1)
                pool.tensor_copy(hi, w).then_inc(m_split, 1)
                pool.wait_ge(m_split, 3 * n + 2)
                pool.tensor_tensor(lo, w, hi, ALU.subtract).then_inc(m_split, 1)
                if n + 2 < len(work):
                    pool.wait_ge(m_split, 3 * n + 3)
                    load(n + 2)

        @block.sync
        def _(sp):
            rows = attd[0:B * T * D].rearrange("(b h s p j) -> b p h s j", h=NH, s=TT, p=P, j=HV)
            with sp.Fori(0, B) as b:
                sp.wait_ge(att_done, at(b, 1, 2))
                for s_ in range(TT):
                    sp.dma_start(rows[bass.ds(b, 1), :, :, s_, :].rearrange("o p h j -> (o p) h j"),
                                 att[:, :, s_, :]).then_inc(att_sent, 16)
            sp.wait_ge(att_sent, 16 * TT * (B + 2))

        @block.tensor
        def _(pe):
            def project(b):
                pe.wait_ge(xn_steps, at(b, XN, XN))
                pe.wait_ge(qk_split, at(b, 2, 0))
                pe.wait_ge(v_split, at(b, 1, 0))
                for j, (n, bank) in enumerate((("q", pq), ("k", pk))):
                    for m in range(KT):
                        o = bank[:, m, :]
                        pe.matmul(o, brow[0:2, j * D + m * P:j * D + (m + 1) * P], ones2[0:2, :], start=(m == 0),
                                  stop=False, skip_group_check=True)
                        w = (lambda k, n=n, m=m: w_hi[n][:, k, m * P:(m + 1) * P],
                             lambda k, n=n, m=m: w_lo[n][:, k, m * P:(m + 1) * P])
                        last = split_matmul(pe, o, w, (lambda k: xn_h[:, k, :], lambda k: xn_l[:, k, :]), False,
                                            last=True)
                    last.then_inc(proj_pe, 1)
                for u in range(TT):
                    o = pv[:, u, :]
                    pe.matmul(o, ones2[0:2, 0:P], brow[0:2, 2 * D:3 * D], start=(u == 0), stop=False,
                              skip_group_check=True)
                    w = (lambda k, u=u: xn_h[:, k, u * P:(u + 1) * P], lambda k, u=u: xn_l[:, k, u * P:(u + 1) * P])
                    last = split_matmul(pe, o, w, (lambda k: w_hi["v"][:, k, :], lambda k: w_lo["v"][:, k, :]), False,
                                        last=True)
                last.then_inc(proj_pe, 1)

            def scores(b, h):
                r0, m = DK * (h % 4), h // 4
                if h == 0:
                    pe.wait_ge(qk_split, at(b, 2, 2))
                pe.wait_ge(exp_done, at(b, 2 * NH, 2 * (h - 1)))
                for s_ in range(TT):
                    for q, k in ((q_h, k_h), (q_l, k_h), (q_h, k_l)):
                        last = pe.matmul(sc[h % 2][:, s_, :], q[r0:r0 + DK, m, s_ * P:(s_ + 1) * P],
                                         k[r0:r0 + DK, m, :], start=(s_ == 0 and k is k_h and q is q_h),
                                         stop=(k is k_l), skip_group_check=True, tile_position=(r0, 0))
                last.then_inc(sc_pe, 1)

            def turn(b, h):
                pe.wait_ge(exp_done, at(b, 2 * NH, 2 * (h + 1)))
                pe.wait_ge(pt_lo, at(b, NH, h + 1))
                first = True
                for s_ in range(TT):
                    for u in range(TT):
                        last = pe.matmul(pt[h % 2][:, u, s_ * P:(s_ + 1) * P], prob[:, h % 2, s_, u * P:(u + 1) * P],
                                         ident[:, :], is_transpose=True, start=first, stop=True,
                                         skip_group_check=True)
                        first = False
                last.then_inc(t_pe, 1)

            def values(b, h):
                pe.wait_ge(pt_lo, at(b, NH, h + 3))
                if h == 0:
                    pe.wait_ge(v_split, at(b, 1, 1))
                    pe.wait_ge(att_done, at(b, 1, 1))
                hd = h % NH
                for s_ in range(TT):
                    o = po[:, hd, s_, :]
                    for u in range(TT):
                        for pp, vp in ((pt_h, v_h), (pt_h, v_l), (pt_l, v_h)):
                            last = pe.matmul(o, pp[:, h % 2, u, s_ * P:(s_ + 1) * P], vp[:, u, hd * HV:(hd + 1) * HV],
                                             start=(h == 0 and s_ == 0 and u == 0 and pp is pt_h and vp is v_h),
                                             stop=(u == TT - 1 and pp is pt_l), skip_group_check=True)
                last.then_inc(pv_pe, 1)

            project(0)
            with pe.Fori(0, B) as b:
                for h in range(NH):
                    if h > 0:
                        scores(b, h)
                    turn(b, h - 1)
                    values(b, h - 3)
                    if h == 0:
                        scores(b, h)
                    if h == 4:
                        project(b + 1)
            turn(B, -1)
            for h in (-3, -2, -1):
                values(B, h)

        @block.scalar
        def _(act):
            def flat(a):
                return a.rearrange("p k n -> p (k n)")

            def exps(b, h):
                act.wait_ge(neg_max, at(b, NH, h + 1))
                act.wait_ge(t_pe, at(b, NH, h))
                if h == 0:
                    act.wait_ge(r_done, at(b, 1, 1))
                for s_ in range(TT):
                    act.activation(prob[:, h % 2, s_, :], sc[h % 2][:, s_, :], ACT.Exp, bias=nmax[:, h % 2, s_:s_ + 1],
                                   accum_out=sums[:, h, s_:s_ + 1]).then_inc(exp_done, 1)

            def high(b, h):
                act.wait_ge(t_pe, at(b, NH, h + 2))
                act.wait_ge(pv_pe, at(b, NH, h + 2))
                act.activation(flat(pt_h[:, h % 2]), flat(pt[h % 2][:, :, :]), ACT.Copy).then_inc(pt_hi, 1)

            act.activation(first_exp[:, :], mean_w[:, 0:1], ACT.Exp)
            with act.Fori(0, B) as b:
                for h in range(NH):
                    if h == 0:
                        act.wait_ge(sc_pe, at(b, NH, 0))
                        act.wait_ge(proj_pe, at(b, 3, 1))
                        act.activation(flat(q_h[:, :, :]), flat(pq[:, :, :]), ACT.Copy,
                                       scale=float(DK) ** -0.5 / S).then_inc(proj_read, 1)
                        act.wait_ge(proj_pe, at(b, 3, 2))
                        act.activation(flat(k_h[:, :, :]), flat(pk[:, :, :]), ACT.Copy,
                                       scale=1.0 / S).then_inc(proj_read, 1)
                    high(b, h - 2)
                    exps(b, h)
                    if h == 2:
                        act.wait_ge(pv_pe, at(b, NH, 3))
                        act.wait_ge(proj_pe, at(b, 3, 3))
                        act.activation(flat(v_h[:, :, :]), flat(pv[:, :, :]), ACT.Copy,
                                       scale=1.0 / S).then_inc(proj_read, 1)
            high(B, -2)
            high(B, -1)

        @block.vector
        def _(dve):
            def split_x(b, row):
                dve.wait_ge(proj_pe, at(b, 3, 0))
                dve.tensor_scalar(xn_h[:, :, :], row, 1.0, None, ALU.mult).then_inc(xn_steps, 1)
                dve.wait_ge(xn_steps, at(b, XN, 1))
                dve.tensor_tensor(xn_l[:, :, :], row, xn_h[:, :, :], ALU.subtract).then_inc(xn_steps, 1)

            def low(b, h):
                dve.wait_ge(pt_hi, at(b, NH, h + 3))
                dve.tensor_tensor(pt_l[:, h % 2], pt[h % 2][:, :, :], pt_h[:, h % 2], ALU.subtract).then_inc(pt_lo, 1)

            def inverse(b):
                dve.wait_ge(exp_done, at(b, 2 * NH, 0))
                dve.wait_ge(att_done, at(b, 1, 0))
                dve.reciprocal(rinv[:, :, :], sums[:, :, :]).then_inc(r_done, 1)

            def finish(b):
                dve.wait_ge(r_done, at(b, 1, 1))
                dve.wait_ge(pv_pe, at(b, NH, 3))
                dve.wait_ge(att_sent, at(b, 16 * TT, 0))
                dve.tensor_tensor(att[:, :, :, :].rearrange("p h s j -> p (h s) j"),
                                  po[:, :, :, :].rearrange("p h s j -> p (h s) j"),
                                  rinv[:, :, :].rearrange("p h s -> p (h s)").unsqueeze(2)
                                  .to_broadcast([P, NH * TT, HV]), ALU.mult).then_inc(att_done, 1)

            def rows(first):
                o = LAG * CW + first
                return hs1[:, :, o:o + NCH * CW].rearrange("p k (t b) -> p k t b", b=B)

            split_x(0, rows(0)[:, :, :, 0])
            with dve.Fori(0, B) as b:
                for h in range(NH):
                    if h == 0:
                        for j, (lo, hi, bank, f) in enumerate(((q_l, q_h, pq, float(DK) ** -0.5 / S),
                                                               (k_l, k_h, pk, 1.0 / S))):
                            dve.wait_ge(proj_read, at(b, 3, j + 1))
                            dve.scalar_tensor_tensor(out=lo[:, :, :], in0=bank[:, :, :], scalar=f, in1=hi[:, :, :],
                                                     op0=ALU.mult, op1=ALU.subtract).then_inc(qk_split, 1)
                        inverse(b)
                    dve.wait_ge(sc_pe, at(b, NH, h + 1))
                    dve.wait_ge(exp_done, at(b, 2 * NH, 2 * (h - 1)))
                    dve.tensor_reduce(nmax[:, h % 2, :], sc[h % 2][:, :, :], AX_X, ALU.max,
                                      negate=True).then_inc(neg_max, 1)
                    low(b, h - 2)
                    if h == 2:
                        finish(b)
                        dve.wait_ge(proj_read, at(b, 3, 3))
                        dve.scalar_tensor_tensor(out=v_l[:, :, :], in0=pv[:, :, :], scalar=1.0 / S, in1=v_h[:, :, :],
                                                 op0=ALU.mult, op1=ALU.subtract).then_inc(v_split, 1)
                    if h == 2:
                        split_x(b + 1, rows(1)[:, :, :, bass.ds(b, 1)].rearrange("p k t o -> p k (t o)"))
            inverse(B)
            low(B, -2)
            low(B, -1)
            finish(B)


M_OFF = [min(m * P, HF - P) for m in range(HM)]
G3 = 3 * D
GRP = 2 * EA
GM = HM // 2
NI3 = NCH + 1
OLAG = 2
SLOT_GROUPS = [[0], [1], [2], [3], [4], [5], [6], [7, 8], [9], [10], [11], [12], [13], [14], [15], [16, 17]]
MISC3 = (0, 3, 6)


def pipeline_two(nc, t, arena, attd, x2d, m12_h, m12_l, out):
    with ExitStack() as ctx:
        def sb(name, shape, dt=F32):
            return ctx.enter_context(nc.sbuf_tensor(name, shape, dt))

        def sem(name):
            return ctx.enter_context(nc.semaphore(name))

        m3_h, m3_l = sb("m3_h", [P, EA, HM, D], F16), sb("m3_l", [P, EA, HM, D], F16)
        gx_w = [sb(f"gx_w{p}", [P, KT, G3], F16) for p in range(2)]
        gu_w = [sb(f"gu_w{p}", [P, KT, G3], F16) for p in range(2)]
        wg = [sb(f"wg{p}", [P, KT, E2], F16) for p in range(2)]
        vt_h, vt_l = sb("vt_h", [P, 6, B], F16), sb("vt_l", [P, 6, B], F16)
        rrow = sb("rrow", [2, E2], F16)
        ones2 = sb("ones2c", [2, P], F16)
        ident = sb("ident3", [P, P])
        ident_h = sb("ident_h", [P, P], F16)
        iota = sb("iota3", [P, E2, TOP2])
        k2 = "(k p) n -> p k n"

        with ExitStack() as st:
            s_x = st.enter_context(nc.sbuf_tensor("s_x", [P, KT, G3], F32))
            s_u = st.enter_context(nc.sbuf_tensor("s_u", [P, KT, G3], F32))
            s_c = arena[:, 0, 0:KT * G3].rearrange("p (k n) -> p k n", k=KT)
            s_row = st.enter_context(nc.sbuf_tensor("s_row", [1, G3 + E2], F32))
            s_rl = st.enter_context(nc.sbuf_tensor("s_rl", [1, E2], F16))
            s_wg = st.enter_context(nc.sbuf_tensor("s_wg", [P, KT, E2], F32))
            s_cond = st.enter_context(nc.sbuf_tensor("s_cond3", [P, KT, B], F32))
            s_one = st.enter_context(nc.sbuf_tensor("s_one", [1, B], F32))
            vps = st.enter_context(nc.psum_tensor("vps", [P, 6, B], F32))
            loaded, ready, vt_pe, vt_read, cast, low, row_sent = (
                st.enter_context(nc.semaphore("g_" + n)) for n in
                ("loaded", "ready", "vt_pe", "vt_read", "cast", "low", "row_sent"))
            smalls = [(s_x[:, :, :], gx_w[0][:, :, :], gx_w[1][:, :, :], S),
                      (s_u[:, :, 0:2 * D], gu_w[0][:, :, 0:2 * D], gu_w[1][:, :, 0:2 * D], S / 2),
                      (s_u[:, :, 2 * D:G3], gu_w[0][:, :, 2 * D:G3], gu_w[1][:, :, 2 * D:G3], S / 4),
                      (s_wg[:, :, :], wg[0][:, :, :], wg[1][:, :, :], S / 2),
                      (s_row[0:1, G3:G3 + E2], rrow[0:1, :], s_rl[0:1, :], S),
                      (ident[:, :], ident_h[:, :], None, 1.0)]
            row = "(a n) -> a n"
            loads = [(s_c[:, :, g * D:(g + 1) * D], t["g_c" + n].rearrange(k2, p=P)) for g, n in enumerate("zrh")]
            loads += [(s_x[:, :, g * D:(g + 1) * D], t["g_w" + n].rearrange(k2, p=P)) for g, n in enumerate("zrh")]
            loads += [(s_u[:, :, g * D:(g + 1) * D], t["g_u" + n].rearrange(k2, p=P)) for g, n in enumerate("zrh")]
            loads += [(s_row[0:1, g * D:(g + 1) * D], t["g_b" + n].rearrange(row, a=1)) for g, n in enumerate("zrh")]
            loads += [(s_row[0:1, G3:G3 + E2], t["m_rb"].rearrange(row, a=1)), (s_wg[:, :, :], t["m_wg"].rearrange(k2, p=P)),
                      (s_cond[:, :, :], t["cond"].rearrange("(k p) b -> p k b", p=P)), (ident[:, :], t["k_ident"]),
                      (iota[:, :, :].rearrange("p e j -> p (e j)"), t["k_iota4"])]
            block = st.enter_context(nc.Block())

            @block.sync
            def _(sp):
                for dst, src in loads:
                    sp.dma_start(dst, src).then_inc(loaded, 16)
                sp.wait_ge(low, 5)
                sp.dma_start(rrow[1:2, :], s_rl[0:1, :]).then_inc(row_sent, 16)
                sp.wait_ge(row_sent, 16)

            @block.gpsimd
            def _(pool):
                pool.memset(s_one[0:1, :], 1.0).then_inc(ready, 1)
                pool.memset(ones2[:, :], 1.0).then_inc(ready, 1)

            @block.tensor
            def _(pe):
                pe.wait_ge(loaded, 16 * len(loads))
                pe.wait_ge(ready, 2)
                for m in range(6):
                    pe.matmul(vps[:, m, :], s_row[0:1, m * P:(m + 1) * P], s_one[0:1, :], start=(m == 0), stop=False,
                              skip_group_check=True)
                    for k in range(KT):
                        last = pe.matmul(vps[:, m, :], s_c[:, k, m * P:(m + 1) * P], s_cond[:, k, :], start=False,
                                         stop=(k == KT - 1), skip_group_check=True)
                last.then_inc(vt_pe, 1)

            @block.scalar
            def _(act):
                act.wait_ge(loaded, 16 * len(loads))
                for src, hi, _lo, f in smalls:
                    act.activation(hi, src, ACT.Copy, scale=f).then_inc(cast, 1)

            @block.vector
            def _(dve):
                for n, (src, hi, lo, f) in enumerate(smalls[:5]):
                    dve.wait_ge(cast, n + 1)
                    dve.scalar_tensor_tensor(out=lo, in0=src, scalar=f, in1=hi, op0=ALU.mult,
                                             op1=ALU.subtract).then_inc(low, 1)
                dve.wait_ge(vt_pe, 1)
                dve.tensor_scalar(vt_h[:, :, :], vps[:, :, :], S, None, ALU.mult).then_inc(vt_read, 1)
                dve.wait_ge(vt_read, 1)
                dve.scalar_tensor_tensor(out=vt_l[:, :, :], in0=vps[:, :, :], scalar=S, in1=vt_h[:, :, :],
                                         op0=ALU.mult, op1=ALU.subtract).then_inc(vt_read, 1)

        x3 = arena[:, :, 0:(NCH + OLAG + 2) * CW]
        pieces = [(m, e) for m in range(HM) for e in range(0, EA, 3)]
        m3_stage = [x3[:, j // 2, (6 + 6 * (j % 2)) * CW:(12 + 6 * (j % 2)) * CW] for j in range(4)]
        def tile(name, dt=F16):
            return sb(name, [P, KT, CW], dt)
        g_hh, g_hl = tile("g_hh"), tile("g_hl")
        hc_h, hc_l = tile("hc_h"), tile("hc_l")
        gx_h, gx_l = tile("gx_h"), tile("gx_l")
        attr = sb("attr", [P, D])
        x2r = tile("x2r", F32)
        outc = tile("outc", F32)
        zr = sb("zr", [P, 32])
        cand = sb("cand", [P, 16])
        h32 = sb("h32", [P, 16])
        rh32 = sb("rh32", [P, 16])
        rh_h, rh_l = sb("rh_h", [P, KT, B], F16), sb("rh_l", [P, KT, B], F16)
        zc, zm = sb("zc", [P, 16]), sb("zm", [P, 16])
        th = sb("th", [P, 2, GM * CW])
        uu = sb("uu", [P, GM * CW])
        a32 = sb("a32", [P, 2, GM * CW])
        a_h, a_l = sb("a_h", [P, 2, GM * CW], F16), sb("a_l", [P, 2, GM * CW], F16)
        acc = sb("acc3", [P, D])
        lg = sb("lg3", [P, E2])
        m8 = sb("m83", [P, 8])
        i8 = sb("i83", [P, 8], U32)
        idf = sb("idf3", [P, TOP2])
        eq = sb("eq", [P, E2, TOP2])
        rt = sb("rt3", [P, 4, E2])
        sm = sb("sm3", [P, 3])
        wts = sb("wts3", [P, EA])

        g_b = [ctx.enter_context(nc.psum_tensor(f"g_b{h}", [P, 8, 6, B], F32)) for h in range(2)]
        p1 = [ctx.enter_context(nc.psum_tensor(f"p1{h}", [P, 512], F32)) for h in range(2)]
        p2 = [ctx.enter_context(nc.psum_tensor(f"p2{h}", [P, 512], F32)) for h in range(2)]
        po = ctx.enter_context(nc.psum_tensor("po3", [P, D], F32))
        z = ctx.enter_context(nc.psum_tensor("z3", [P, 512], F32))

        zr_pe, zr_act, u_pe, u_act = (sem(n) for n in ("zr_pe", "zr_act", "u_pe", "u_act"))
        rh_hi, rh_32, rh_lo, z_parts, z_mix, h_new, h_hi, h_lo = (
            sem(n) for n in ("rh_hi", "rh_32", "rh_lo", "z_parts", "z_mix", "h_new", "h_hi3", "h_lo3"))
        hid_pe, th_act, u_done, a_done, a_hi, a_lo, w3_pe, po_free = (
            sem(n) for n in ("hid_pe", "th_act", "u_done", "a_done", "a_hi3", "a_lo3", "w3_pe", "po_free"))
        z_full, gate_read = sem("z_full3"), sem("gate_read")
        hc_copied, route, x3_done, x3_split, out_done = (
            sem(n) for n in ("hc_copied", "route3", "x3_done", "x3_split", "out_done"))
        exp_done = sem("exp3")
        m3_staged = [sem(f"m3_staged{j}") for j in range(4)]
        m3_hi, m3_lo = sem("m3_hi_done"), sem("m3_lo_done")
        rows_in, out_sent = sem("rows_in"), sem("out_sent")
        RIN = 16 * (B + 1)
        NR = 10
        per = [(n, c, c) for n, c in (
            (zr_pe, 16), (zr_act, 16), (u_pe, 16), (u_act, 16), (rh_hi, 16), (rh_32, 16), (rh_lo, 16), (z_parts, 16),
            (z_mix, 16), (h_new, 16), (h_hi, 16), (h_lo, 16), (hc_copied, 2), (x3_done, 1), (x3_split, 2),
            (rows_in, RIN))]
        per += [(n, c, 0) for n, c in (
            (hid_pe, GRP), (th_act, GRP), (u_done, GRP), (a_done, GRP), (a_hi, GRP), (a_lo, GRP), (w3_pe, GRP),
            (po_free, EA), (gate_read, 1), (route, NR), (out_done, 1), (exp_done, 1), (out_sent, 16))]
        per += [(z_full, 3, 1)]

        def project_half(pe, half):
            first = True
            for m in range(6):
                o = g_b[half][:, :, m, :]
                for v in (vt_h, vt_l):
                    pe.matmul(o, ident_h[:, :], v[:, m, :].unsqueeze(1).to_broadcast([P, 8, B]), start=first,
                              stop=False, skip_group_check=True)
                    first = False
                w = (lambda k, m=m: gx_w[0][:, k, m * P:(m + 1) * P], lambda k, m=m: gx_w[1][:, k, m * P:(m + 1) * P])
                r = slice(half * HALF, (half + 1) * HALF)
                last = split_matmul(pe, o, w, (lambda k: gx_h[:, k, r], lambda k: gx_l[:, k, r]), False)
            return last

        def pieces_of(slot):
            return range(2 * slot, 2 * slot + 2) if slot < 2 else range(slot + 2, slot + 3)

        def piece(n):
            m, e = pieces[n]
            return (m3_stage[n % 4].rearrange("p (e d) -> p e d", d=D), m3_h[:, e:e + 3, m, :], m3_l[:, e:e + 3, m, :])

        def load_rows(sp, c, done):
            for b in range(B):
                sp.dma_start(attr[b * C:(b + 1) * C, :],
                             attd[bass.ds(c * (C * D) + b * T * D, C * D)].rearrange("(t d) -> t d", d=D))\
                    .then_inc(done, 16)
            sp.dma_start(x2r[:, :, :], x2d[:, :, bass.ds((c + (LAG - 1)) * CW, CW)]).then_inc(done, 16)

        def turn_rows(pe):
            for k in range(KT):
                last = pe.matmul(z[:, k * P:(k + 1) * P], attr[:, k * P:(k + 1) * P], ident[:, :], is_transpose=True,
                                 start=(k == 0), stop=True, skip_group_check=True)
            return last

        def add_rows(dve, dst):
            return dve.tensor_tensor(dst.rearrange("p k (t b) -> p k t b", b=B),
                                     z[:, 0:D].rearrange("p (k b t) -> p k t b", k=KT, b=B),
                                     x2r[:, :, :].rearrange("p k (t b) -> p k t b", b=B), ALU.add)

        with ExitStack() as st:
            cleared, hid_zero, pad_sent, x_in, x_tr, x_out, x_first = (
                st.enter_context(nc.semaphore("f_" + n)) for n in
                ("cleared", "hid_zero", "pad_sent", "x_in", "x_tr", "x_out", "x_first"))
            block = st.enter_context(nc.Block())

            @block.gpsimd
            def _(pool):
                for tl in (g_hh, g_hl, hc_l):
                    pool.memset(tl[:, :, :], 0.0)
                pool.memset(hc_h[:, :, :], 0.0).then_inc(hid_zero, 1)
                pool.memset(x3[:, :, 0:OLAG * CW], 0.0)
                for tl in (a_h, a_l, th):
                    pool.memset(tl[:, :, :], 0.0)
                pool.memset(h32[:, :], 0.0)
                pool.memset(acc[:, :], 0.0).then_inc(cleared, 1)
                pool.memset(wts[:, 0:E2], 0.0)
                pool.memset(wts[:, E2:EA], 1.0 / S)

            @block.sync
            def _(sp):
                load_rows(sp, 0, x_in)
                sp.wait_ge(cleared, 1)
                sp.dma_start(attd[B * T * D:(B * T + 2 * C) * D].rearrange("(r d) -> r d", d=D),
                             acc[0:2 * C, :]).then_inc(pad_sent, 16)
                sp.wait_ge(pad_sent, 16)
                for s, n, first in per:
                    sp.sem_inc(s, 2 * n - first)

            @block.tensor
            def _(pe):
                pe.wait_ge(x_in, 16 * (B + 1))
                turn_rows(pe).then_inc(x_tr, 1)
                pe.wait_ge(x_first, 2)
                project_half(pe, 0)
                pe.wait_ge(hid_zero, 1)
                for bank in (*p1, *p2):
                    for j in range(GM):
                        pe.matmul(bank[:, j * CW:(j + 1) * CW], gx_w[0][:, 0, 0:P], hc_h[:, 0, :], start=(j == 0),
                                  stop=True, skip_group_check=True)
                for k in range(KT):
                    pe.matmul(po[:, k * CW:(k + 1) * CW], gx_w[0][:, 0, 0:P], hc_h[:, 0, :], start=(k == 0),
                              stop=True, skip_group_check=True)

            @block.vector
            def _(dve):
                dve.wait_ge(x_in, 16 * (B + 1))
                dve.wait_ge(x_tr, 1)
                c0 = x3[:, :, OLAG * CW:(OLAG + 1) * CW]
                add_rows(dve, c0).then_inc(x_out, 1)
                dve.wait_ge(x_out, 1)
                dve.tensor_copy(gx_h[:, :, :], c0).then_inc(x_first, 1)
                dve.wait_ge(x_first, 1)
                dve.tensor_tensor(gx_l[:, :, :], c0, gx_h[:, :, :], ALU.subtract).then_inc(x_first, 1)

        block = ctx.enter_context(nc.Block())

        @block.sync
        def _(sp):
            load_rows(sp, 1, rows_in)
            for n, (m, e) in enumerate(pieces):
                if n >= 4:
                    sp.wait_ge(m3_lo, n - 3)
                sp.dma_start(piece(n)[0], t["m_w3"][m * P:(m + 1) * P, e:e + 3, :]).then_inc(m3_staged[n % 4], 16)
            with sp.Fori(1, NI3) as i:
                sp.wait_ge(x3_done, at(i, 1, 0))
                load_rows(sp, i + 1, rows_in)
                sp.wait_ge(out_done, at(i, 1, 1))
                sp.dma_start(out[:, :, bass.ds((i - 1) * CW, CW)], outc[:, :, :]).then_inc(out_sent, 16)
            sp.wait_ge(out_done, at(NI3, 1, 1))
            sp.dma_start(out[:, :, (NI3 - 1) * CW:NI3 * CW], outc[:, :, :]).then_inc(out_sent, 16)
            sp.wait_ge(out_sent, 16 + 16 * (NI3 + 1))

        def before(slot):
            return [(g, (g + 2) % GRP) for g in SLOT_GROUPS[(slot - 1) % C]]

        @block.tensor
        def _(pe):
            def zr_gates(i, slot):
                prev = (slot - 1) % C * B
                o = g_b[slot // 8]
                pe.wait_ge(h_hi, at(i, C, slot))
                for m in range(4):
                    for k in range(KT):
                        for w in gu_w:
                            pe.matmul(o[:, slot % 8, m, :], w[:, k, m * P:(m + 1) * P], g_hh[:, k, prev:prev + B],
                                      start=False, stop=False, skip_group_check=True)
                pe.wait_ge(h_lo, at(i, C, slot))
                for m in range(4):
                    for k in range(KT):
                        last = pe.matmul(o[:, slot % 8, m, :], gu_w[0][:, k, m * P:(m + 1) * P],
                                         g_hl[:, k, prev:prev + B], start=False, stop=(k == KT - 1),
                                         skip_group_check=True)
                last.then_inc(zr_pe, 1)

            def candidate(i, slot):
                o = g_b[slot // 8]
                pe.wait_ge(rh_hi, at(i, C, slot + 1))
                for m in (4, 5):
                    for k in range(KT):
                        for w in gu_w:
                            pe.matmul(o[:, slot % 8, m, :], w[:, k, m * P:(m + 1) * P], rh_h[:, k, :],
                                      start=False, stop=False, skip_group_check=True)
                pe.wait_ge(rh_lo, at(i, C, slot + 1))
                for m in (4, 5):
                    for k in range(KT):
                        last = pe.matmul(o[:, slot % 8, m, :], gu_w[0][:, k, m * P:(m + 1) * P], rh_l[:, k, :],
                                         start=False, stop=(k == KT - 1), skip_group_check=True)
                last.then_inc(u_pe, 1)

            def hidden(i, g):
                e = g // 2
                pe.wait_ge(a_done, at(i, GRP, g + 1))
                for mat, bank in enumerate((p1[g % 2], p2[g % 2])):
                    for j in range(GM):
                        c = M_OFF[g % 2 * GM + j]
                        w = (lambda k: m12_h[:, mat, k, e, c:c + P], lambda k: m12_l[:, mat, k, e, c:c + P])
                        last = split_matmul(pe, bank[:, j * CW:(j + 1) * CW], w,
                                            (lambda k: hc_h[:, k, :], lambda k: hc_l[:, k, :]), j == 0, last=True)
                last.then_inc(hid_pe, 1)

            def down(i, k):
                g = (k - 2) % GRP
                e = g // 2
                pe.wait_ge(a_hi, at(i, GRP, k + 1))
                pe.wait_ge(a_lo, at(i, GRP, k + 1))
                if g % 2 == 0:
                    pe.wait_ge(po_free, at(i, EA, k // 2 + 1))
                for j in range(GM):
                    m = g % 2 * GM + j
                    r = slice(j * CW, (j + 1) * CW)
                    for x, w in ((a_h, m3_h), (a_h, m3_l), (a_l, m3_h)):
                        last = pe.matmul(po[:, :], x[:, g % 2, r], w[:, e, m, :],
                                         start=(m == 0 and x is a_h and w is m3_h), stop=(m == HM - 1 and x is a_l),
                                         skip_group_check=True)
                last.then_inc(w3_pe, 1)

            def misc(i, slot):
                if slot == 0:
                    pe.wait_ge(hc_copied, at(i, 2, 0))
                    pe.wait_ge(x3_done, at(i, 1, 0))
                    pe.matmul(z[:, 0:E2], ones2[0:2, :], rrow[0:2, :], start=True, stop=False, skip_group_check=True)
                    last = split_matmul(pe, z[:, 0:E2], (lambda k: hc_h[:, k, :], lambda k: hc_l[:, k, :]),
                                        (lambda k: wg[0][:, k, :], lambda k: wg[1][:, k, :]), False, last=True)
                elif slot == 3:
                    pe.wait_ge(po_free, at(i, EA, 2))
                    if isinstance(i, int) and i == NI3:
                        pe.wait_ge(x3_done, at(i, 1, 0))
                    else:
                        pe.wait_ge(gate_read, at(i, 1, 1))
                    for k in range(KT):
                        last = pe.matmul(z[:, k * P:(k + 1) * P], acc[:, k * P:(k + 1) * P], ident[:, :],
                                         is_transpose=True, start=(k == 0), stop=True, skip_group_check=True)
                else:
                    pe.wait_ge(rows_in, at(i, RIN, RIN))
                    pe.wait_ge(out_done, at(i, 1, 1))
                    last = turn_rows(pe)
                last.then_inc(z_full, 1)

            def iteration(i, experts, scan=True):
                for slot in range(C):
                    if scan:
                        zr_gates(i, slot)
                    if slot == 2 and scan:
                        pe.wait_ge(u_act, at(i, C, 0))
                        project_half(pe, 1)
                    if slot == 12 and scan:
                        pe.wait_ge(x3_split, at(i, 2, 2))
                        pe.wait_ge(u_act, at(i, C, 8))
                        project_half(pe, 0)
                    if slot in MISC3 and (experts or slot == 6):
                        misc(i, slot)
                    if not experts:
                        candidate(i, slot)
                        continue
                    for n, k in enumerate(SLOT_GROUPS[slot]):
                        hidden(i, k)
                        if n == 0 and scan:
                            candidate(i, slot)
                        down(i, k)
            iteration(0, False)
            pe.wait_ge(m3_lo, len(pieces))
            with pe.Fori(1, NI3 - 1) as i:
                iteration(i, True)
            with pe.Fori(NI3 - 1, NI3) as i:
                iteration(i, True, scan=False)
            down(NI3, 0)
            down(NI3, 1)
            misc(NI3, 3)

        @block.scalar
        def _(act):
            def high(i, slot):
                for g, n in before(slot):
                    act.wait_ge(a_done, at(i, GRP, n + 1))
                    act.wait_ge(w3_pe, at(i, GRP, n - 1))
                    act.activation(a_h[:, g % 2, :], a32[:, g % 2, :], ACT.Copy).then_inc(a_hi, 1)

            act.activation(cand[:, 0:1], wts[:, 0:1], ACT.Exp)
            def iteration(i, experts, scan=True):
                for slot in range(C):
                    bank = g_b[slot // 8]
                    if scan:
                        act.wait_ge(zr_pe, at(i, C, slot + 1))
                        act.activation(zr[:, :], bank[:, slot % 8, 0:4].rearrange("p m b -> p (m b)"), ACT.Tanh,
                                       scale=0.5 / S).then_inc(zr_act, 1)
                    if experts:
                        high(i, slot)
                    else:
                        for n in pieces_of(slot):
                            act.wait_ge(m3_staged[n % 4], 16 * (n // 4 + 1))
                            staged, hi, _lo = piece(n)
                            act.activation(hi, staged, ACT.Copy, scale=S).then_inc(m3_hi, 1)
                    if scan:
                        act.wait_ge(u_pe, at(i, C, slot + 1))
                        act.activation(cand[:, :], bank[:, slot % 8, 4:6].rearrange("p m b -> p (m b)"), ACT.Tanh,
                                       scale=1.0 / S).then_inc(u_act, 1)
                    for k in SLOT_GROUPS[slot] if experts else ():
                        act.wait_ge(hid_pe, at(i, GRP, k + 1))
                        act.wait_ge(u_done, at(i, GRP, k + 1))
                        act.activation(th[:, k % 2, :], p1[k % 2][:, 0:GM * CW], ACT.Tanh,
                                       scale=0.5 / S).then_inc(th_act, 1)
                    if slot == 1 and experts:
                        act.wait_ge(route, at(i, NR, 2))
                        act.activation(rt[:, 1, :], rt[:, 0, :], ACT.Exp).then_inc(exp_done, 1)

            iteration(0, False)
            with act.Fori(1, NI3 - 1) as i:
                iteration(i, True)
            with act.Fori(NI3 - 1, NI3) as i:
                iteration(i, True, scan=False)
            high(NI3, 0)

        @block.gpsimd
        def _(pool):
            def low(i, slot):
                for g, n in before(slot):
                    pool.wait_ge(a_hi, at(i, GRP, n + 1))
                    pool.tensor_tensor(a_l[:, g % 2, :], a32[:, g % 2, :], a_h[:, g % 2, :],
                                       ALU.subtract).then_inc(a_lo, 1)

            with pool.Fori(1, NI3) as i:
                for slot in range(C):
                    low(i, slot)
            low(NI3, 0)

        @block.vector
        def _(dve):
            def swiglu(i, slot):
                for g, n in before(slot):
                    dve.wait_ge(th_act, at(i, GRP, n - 1))
                    dve.wait_ge(a_done, at(i, GRP, n))
                    dve.scalar_tensor_tensor(out=uu[:, :], in0=th[:, g % 2, :], scalar=1.0,
                                             in1=p1[g % 2][:, 0:GM * CW], op0=ALU.add, op1=ALU.mult).then_inc(u_done, 1)
                    dve.wait_ge(u_done, at(i, GRP, n + 1))
                    dve.wait_ge(a_lo, at(i, GRP, n - 1))
                    dve.scalar_tensor_tensor(out=a32[:, g % 2, :], in0=uu[:, :], scalar=0.5 / S / S,
                                             in1=p2[g % 2][:, 0:GM * CW], op0=ALU.mult, op1=ALU.mult).then_inc(a_done, 1)

            def add_expert(i, slot):
                for k, _n in before(slot):
                    if k % 2 == 0:
                        continue
                    e = (k - 2) % GRP // 2
                    dve.wait_ge(w3_pe, at(i, GRP, k + 1 - (GRP if slot == 0 else 0)))
                    dve.wait_ge(po_free, at(i, EA, (k // 2 + 1) % EA))
                    if e == 0:
                        dve.wait_ge(route, at(i, NR, NR))
                        dve.tensor_scalar(acc[:, :], po[:, :], wts[:, 0:1], None, ALU.mult).then_inc(po_free, 1)
                    else:
                        dve.scalar_tensor_tensor(out=acc[:, :], in0=po[:, :], scalar=wts[:, e:e + 1], in1=acc[:, :],
                                                 op0=ALU.mult, op1=ALU.add).then_inc(po_free, 1)

            def misc(i, slot):
                if slot == 0:
                    dve.wait_ge(z_full, at(i, 3, 1))
                    dve.tensor_scalar(lg[:, :], z[:, 0:E2], 1.0 / S, None, ALU.mult).then_inc(gate_read, 1)
                elif slot == 1:
                    dve.max(m8[:, :], lg[:, :]).then_inc(route, 1)
                    dve.wait_ge(route, at(i, NR, 1))
                    dve.tensor_tensor(rt[:, 0, :], lg[:, :], m8[:, 0:1].to_broadcast([P, E2]),
                                      ALU.subtract).then_inc(route, 1)
                    dve.max_index(i8[:, :], m8[:, :], lg[:, :]).then_inc(route, 1)
                    dve.wait_ge(route, at(i, NR, 3))
                    dve.tensor_copy(idf[:, :], i8[:, 0:TOP2]).then_inc(route, 1)
                elif slot == 2:
                    dve.wait_ge(route, at(i, NR, 4))
                    dve.tensor_tensor(eq[:, :, :], iota[:, :, :], idf[:, :].unsqueeze(1).to_broadcast([P, E2, TOP2]),
                                      ALU.is_equal).then_inc(route, 1)
                    dve.wait_ge(route, at(i, NR, 5))
                    dve.tensor_reduce(rt[:, 2, :], eq[:, :, :], AX_X, ALU.add).then_inc(route, 1)
                    dve.wait_ge(route, at(i, NR, 6))
                    dve.wait_ge(exp_done, at(i, 1, 1))
                    dve.tensor_tensor(rt[:, 3, :], rt[:, 1, :], rt[:, 2, :], ALU.mult).then_inc(route, 1)
                    dve.wait_ge(route, at(i, NR, 7))
                    dve.tensor_reduce(sm[:, 0:1], rt[:, 3, :], AX_X, ALU.add).then_inc(route, 1)
                    dve.wait_ge(route, at(i, NR, 8))
                    dve.reciprocal(sm[:, 1:2], sm[:, 0:1]).then_inc(route, 1)
                    dve.wait_ge(route, at(i, NR, 9))
                    dve.tensor_scalar(wts[:, 0:E2], rt[:, 3, :], sm[:, 1:2], 1.0 / S, ALU.mult,
                                      ALU.mult).then_inc(route, 1)
                elif slot == 3:
                    dve.wait_ge(z_full, at(i, 3, 1 if isinstance(i, int) and i == NI3 else 2))
                    dve.wait_ge(out_sent, at(i, 16, 0))
                    x = x3[:, :, i * CW:(i + 1) * CW] if isinstance(i, int) else x3[:, :, bass.ds(i * CW, CW)]
                    dve.tensor_tensor(outc[:, :, :], z[:, 0:D].rearrange("p (k n) -> p k n", n=CW), x,
                                      ALU.add).then_inc(out_done, 1)
                elif slot == 6:
                    dve.wait_ge(z_full, at(i, 3, 3))
                    x = x3[:, :, bass.ds((i + (OLAG + 1)) * CW, CW)]
                    add_rows(dve, x).then_inc(x3_done, 1)
                    dve.wait_ge(x3_done, at(i, 1, 1))
                    dve.tensor_scalar(gx_h[:, :, :], x, 1.0, None, ALU.mult).then_inc(x3_split, 1)
                    dve.wait_ge(x3_split, at(i, 2, 1))
                    dve.tensor_tensor(gx_l[:, :, :], x, gx_h[:, :, :], ALU.subtract).then_inc(x3_split, 1)

            kb = "p (k b) -> p k b"
            def reset_product(i, slot):
                dve.wait_ge(zr_act, at(i, C, slot + 1))
                dve.wait_ge(h_new, at(i, C, slot))
                r3, h3 = zr[:, 16:32].rearrange(kb, b=B), h32[:, :].rearrange(kb, b=B)
                dve.scalar_tensor_tensor(out=rh_h[:, :, :], in0=r3, scalar=1.0, in1=h3, op0=ALU.add,
                                         op1=ALU.mult).then_inc(rh_hi, 1)
                dve.scalar_tensor_tensor(out=rh32[:, :].rearrange(kb, b=B), in0=r3, scalar=1.0, in1=h3,
                                         op0=ALU.add, op1=ALU.mult).then_inc(rh_32, 1)
                dve.wait_ge(rh_hi, at(i, C, slot + 1))
                dve.wait_ge(rh_32, at(i, C, slot + 1))
                dve.tensor_tensor(rh_l[:, :, :], rh32[:, :].rearrange(kb, b=B), rh_h[:, :, :],
                                  ALU.subtract).then_inc(rh_lo, 1)

            def new_state(i, slot):
                dve.wait_ge(u_act, at(i, C, slot + 1))
                dve.scalar_tensor_tensor(out=zm[:, :], in0=zr[:, 0:16], scalar=1.0, in1=cand[:, :], op0=ALU.add,
                                         op1=ALU.mult).then_inc(z_mix, 1)
                dve.wait_ge(z_mix, at(i, C, slot + 1))
                dve.wait_ge(z_parts, at(i, C, slot + 1))
                rr = slice(slot * B, (slot + 1) * B)
                dve.scalar_tensor_tensor(out=g_hh[:, :, rr], in0=zc[:, :].rearrange(kb, b=B), scalar=-0.5,
                                         in1=zm[:, :].rearrange(kb, b=B), op0=ALU.mult, op1=ALU.add).then_inc(h_hi, 1)
                dve.scalar_tensor_tensor(out=h32[:, :], in0=zc[:, :], scalar=-0.5, in1=zm[:, :], op0=ALU.mult,
                                         op1=ALU.add).then_inc(h_new, 1)
                dve.wait_ge(h_hi, at(i, C, slot + 1))
                dve.wait_ge(h_new, at(i, C, slot + 1))
                dve.tensor_tensor(g_hl[:, :, rr], h32[:, :].rearrange(kb, b=B), g_hh[:, :, rr],
                                  ALU.subtract).then_inc(h_lo, 1)
                if slot == C - 1:
                    dve.wait_ge(h_lo, at(i, C, C))
                    dve.wait_ge(hid_pe, at(i, GRP, GRP))
                    dve.tensor_copy(hc_h[:, :, :], g_hh[:, :, :]).then_inc(hc_copied, 1)
                    dve.tensor_copy(hc_l[:, :, :], g_hl[:, :, :]).then_inc(hc_copied, 1)

            def iteration(i, experts, scan=True):
                for slot in range(C):
                    if experts:
                        swiglu(i, slot)
                        add_expert(i, slot)
                    if scan:
                        reset_product(i, slot)
                    if slot == 0 and experts:
                        misc(i, slot)
                        dve.wait_ge(gate_read, at(i, 1, 1))
                    if scan:
                        dve.scalar_tensor_tensor(out=zc[:, :], in0=zr[:, 0:16], scalar=1.0, in1=h32[:, :],
                                                 op0=ALU.subtract, op1=ALU.mult).then_inc(z_parts, 1)
                    if slot == 6 or slot in (1, 2, 3) and experts:
                        misc(i, slot)
                    for n in () if experts else pieces_of(slot):
                        dve.wait_ge(m3_hi, n + 1)
                        staged, hi, lo = piece(n)
                        dve.scalar_tensor_tensor(out=lo, in0=staged, scalar=S, in1=hi, op0=ALU.mult,
                                                 op1=ALU.subtract).then_inc(m3_lo, 1)
                    if scan:
                        new_state(i, slot)

            iteration(0, False)
            with dve.Fori(1, NI3 - 1) as i:
                iteration(i, True)
            with dve.Fori(NI3 - 1, NI3) as i:
                iteration(i, True, scan=False)
            swiglu(NI3, 0)
            add_expert(NI3, 0)
            add_expert(NI3, 2)
            misc(NI3, 3)


def build_kernel(nc, t, out):
    x2d = nc.dram_tensor("x2_dram", (P, KT, (NI + 1) * CW), F32).ap()
    attd = nc.dram_tensor("attention_dram", ((B * T + 2 * C) * D,), F32).ap()
    with nc.sbuf_tensor("hs1", [P, KT, NI * CW + B], F32) as hs1:
        with nc.sbuf_tensor("xs", [P, KT, (NCH + 2 * LAG + 1) * CW], F32) as xs:
            pipeline_one(nc, t, xs, hs1, x2d)
        with (nc.sbuf_tensor("m12_h", [P, 2, KT, EA, HF], F16) as m12_h,
              nc.sbuf_tensor("m12_l", [P, 2, KT, EA, HF], F16) as m12_l):
            attention_two(nc, t, hs1, attd, m12_h, m12_l)
            pipeline_two(nc, t, hs1, attd, x2d, m12_h, m12_l, out)


def _layout(d):
    f = np.float32
    head = np.arange(P) // 16
    th = np.pi / 2 * np.arange(1, B + 1) / B
    tr = lambda a: np.ascontiguousarray(np.transpose(a))
    hidden = lambda r, s: np.ascontiguousarray(np.concatenate([d[r], d[s][None]]).transpose(2, 0, 1))
    down = np.concatenate([d["L1_ffn_W3"], d["L1_ffn_Ws3"][None]]).transpose(2, 0, 1)
    cut = (HM - 1) * P
    return {
        "x": np.ascontiguousarray(np.transpose(d["x"], (2, 1, 0)).reshape(D, T * B)),
        "cond": tr(d["cond_1024"]),
        "a_wx": d["L0_cond_Wx"], "a_wh": d["L0_cond_Wh"], "a_b": d["L0_cond_b"],
        "e_wx": d["L1_cond_Wx"], "e_wh": d["L1_cond_Wh"], "e_b": d["L1_cond_b"],
        "wq": tr(d["L0_attn_Wq"]), "wk": tr(d["L0_attn_Wk"]), "wv": tr(d["L0_attn_Wv"]), "wo": tr(d["L0_attn_Wo"]),
        "c_wx": d["L0_cond2_Wx"], "c_wh": d["L0_cond2_Wh"], "c_b": d["L0_cond2_b"],
        "f_wm": d["L0_ffn_Wm"], "f_bm": d["L0_ffn_bm"], "f_emb": d["L0_ffn_expert_emb"],
        "f_w1": d["L0_ffn_W1"], "f_b1": tr(d["L0_ffn_b1"]), "f_w2": d["L0_ffn_W2"],
        "f_b2": np.ascontiguousarray(np.concatenate(
            [np.pad(d["L0_ffn_b2"], ((0, 0), (h * HD, D - (h + 1) * HD))) for h in range(NH)])), "f_wo": d["L0_ffn_Wo"], "f_bo": d["L0_ffn_bo"],
        "g_cz": d["L1_cond2_C_z"], "g_cr": d["L1_cond2_C_r"], "g_ch": d["L1_cond2_C"],
        "g_wz": d["L1_cond2_W_z"], "g_wr": d["L1_cond2_W_r"], "g_wh": d["L1_cond2_W"],
        "g_uz": d["L1_cond2_U_z"], "g_ur": d["L1_cond2_U_r"], "g_uh": d["L1_cond2_U"],
        "g_bz": d["L1_cond2_b_z"], "g_br": d["L1_cond2_b_r"], "g_bh": d["L1_cond2_b"],
        "m_wg": tr(d["L1_ffn_Wg"]), "m_rb": d["L1_ffn_routing_bias"],
        "m_w1": hidden("L1_ffn_W1", "L1_ffn_Ws1"), "m_w2": hidden("L1_ffn_W2", "L1_ffn_Ws2"),
        "m_w3": np.concatenate([down[:cut], np.zeros((HM * P - HF, EA, D), f), down[cut:]]),
        "k_iota4": np.tile(np.repeat(np.arange(E2), TOP2)[None], (P, 1)).astype(f),
        "l_wq": d["L1_attn_Wq"], "l_wk": d["L1_attn_Wk"], "l_wv": d["L1_attn_Wv"], "l_bq": d["L1_attn_bq"],
        "l_bk": d["L1_attn_bk"], "l_bv": d["L1_attn_bv"],
        "l_gamma": tr(d["L1_attn_gamma"].reshape(KT, P)), "l_beta": tr(d["L1_attn_beta"].reshape(KT, P)),
        "k_ident": np.eye(P, dtype=f), "k_gsum": (head[:, None] == head[None]).astype(f),
        "k_wcos": np.tile(np.cos(th[:, None] - th[None]).reshape(1, -1), (P, 1)).astype(f),
        "k_iota": np.tile(np.arange(E1)[None], (P, 1)).astype(f),
    }


def kernel(**inputs):
    import concourse.bacc as _bacc
    from concourse.bass_utils import run_bass_kernel_spmd as _run

    nc = _bacc.Bacc("TRN2", target_bir_lowering=False, num_devices=1)
    arrays = {"in_" + k: np.ascontiguousarray(v)
              for k, v in _layout({k: np.asarray(v) for k, v in inputs.items()}).items()}
    t = {k[3:]: nc.dram_tensor(k, v.shape, mybir.dt.from_np(v.dtype), kind="ExternalInput").ap()
         for k, v in arrays.items()}
    out = nc.dram_tensor("out_dram", (P, KT, NI3 * CW), F32, kind="ExternalOutput").ap()
    build_kernel(nc, t, out)
    r = _run(nc, [arrays], core_ids=[0]).results[0]["out_dram"]
    r = r[:, :, CW:].transpose(1, 0, 2).reshape(D, T, B)
    return np.ascontiguousarray(r.transpose(2, 1, 0))
```
